# Optimizing a Trainium2 kernel written in Bass

```python
import numpy as np
import jax
import jax.numpy as jnp

def _softmax(x, axis=-1):
    return jax.nn.softmax(x, axis=axis)

def _gelu(x):
    return jax.nn.gelu(x, approximate=True)

def _silu(x):
    return jax.nn.silu(x)

def _sigmoid(x):
    return jax.nn.sigmoid(x)

def _layernorm(x, axis=-1, eps=1e-05):
    m = jnp.mean(x, axis=axis, keepdims=True)
    v = jnp.var(x, axis=axis, keepdims=True)
    return (x - m) / jnp.sqrt(v + eps)

def _scatter_add(tgt, idx, src, axis=0):
    return tgt.at[idx].add(src)

def _segment_sum(src, seg, n):
    return jax.ops.segment_sum(src, seg, n)
kernel_name = 'mk_gnn_resnorm_d4_gnn_r32_5cd20b'

def setup_inputs(seed: int=0):
    np.random.seed(seed)
    _w = jnp.asarray

    def _rec_inputs():
        import jax
        import jax.numpy as jnp
        _gk = jax.random.key(seed)
        x = -2.473e-05 + 0.125 * jax.random.normal(jax.random.fold_in(_gk, 1), (3125, 64), jnp.float32)
        _s = jax.random.randint(jax.random.fold_in(_gk, 2), (50000,), 0, 3125, jnp.int32)
        _d = jax.random.randint(jax.random.fold_in(_gk, 3), (50000,), 0, 3125, jnp.int32)
        _loop = jnp.arange(3125, dtype=jnp.int32)
        src = jnp.concatenate([_s, _d, _loop])
        dst = jnp.concatenate([_d, _s, _loop])
        _o = jnp.argsort(dst, stable=True)
        src = src[_o]
        dst = dst[_o]
        edge_attr_3 = 0.00117183 + 1.0004 * jax.random.normal(jax.random.fold_in(_gk, 12), (103125, 3), jnp.float32)
        edge_attr_32 = 0.000196303 + 1.00016 * jax.random.normal(jax.random.fold_in(_gk, 13), (103125, 32), jnp.float32)
        return (x, src, dst, edge_attr_3, edge_attr_32)
    x, src, dst, edge_attr_3, edge_attr_32 = _rec_inputs()

    def _L0_gnn_setup():
        import jax, jax.numpy as jnp
        import numpy as np
        NUM_NODES = 3125
        EMBED_DIM = 64
        HIDDEN_DIM = 64
        HEADS = 4
        NEG_SLOPE = 0.2

        def _gat_conv(x, src, dst, num_nodes, W, a_s, a_d, heads, out_ch):
            h = (x @ W).reshape(-1, heads, out_ch)
            alpha_s = (h * a_s[None]).sum(-1)
            alpha_d = (h * a_d[None]).sum(-1)
            e = alpha_s[src] + alpha_d[dst]
            e = jnp.where(e > 0, e, NEG_SLOPE * e)
            m = jax.ops.segment_max(e, dst, num_segments=num_nodes)
            w = jnp.exp(e - m[dst])
            denom = jax.ops.segment_sum(w, dst, num_segments=num_nodes)
            alpha = w / (denom[dst] + 1e-16)
            out = jax.ops.segment_sum(alpha[:, :, None] * h[src], dst, num_segments=num_nodes)
            return out

        def _forward(edge_index, emb, W1, a_src1, a_dst1, b1, W2, a_src2, a_dst2, b2):
            N = emb.shape[0]
            loops = jnp.arange(N, dtype=edge_index.dtype)
            src = jnp.concatenate([edge_index[0], loops])
            dst = jnp.concatenate([edge_index[1], loops])
            x = _gat_conv(emb, src, dst, N, W1, a_src1, a_dst1, HEADS, HIDDEN_DIM // HEADS)
            x = x.reshape(N, -1) + b1
            x = jax.nn.elu(x)
            x = _gat_conv(x, src, dst, N, W2, a_src2, a_dst2, 1, HIDDEN_DIM)
            x = x[:, 0, :] + b2
            norm = jnp.maximum(jnp.linalg.norm(x, axis=1, keepdims=True), 1e-12)
            return x / norm
        key = jax.random.key(seed)
        ks = jax.random.split(key, 10)
        E = 31250
        edge_index = jax.random.randint(ks[0], (2, E), 0, NUM_NODES, dtype=jnp.int64)
        out1 = HIDDEN_DIM // HEADS
        s = 1.0 / np.sqrt(EMBED_DIM)
        emb = jax.random.normal(ks[1], (NUM_NODES, EMBED_DIM), jnp.float32) * s
        W1 = jax.random.normal(ks[2], (EMBED_DIM, HEADS * out1), jnp.float32) * s
        a_src1 = jax.random.normal(ks[3], (HEADS, out1), jnp.float32) * 0.1
        a_dst1 = jax.random.normal(ks[4], (HEADS, out1), jnp.float32) * 0.1
        b1 = jnp.zeros((HEADS * out1,), jnp.float32)
        W2 = jax.random.normal(ks[5], (HIDDEN_DIM, HIDDEN_DIM), jnp.float32) * s
        a_src2 = jax.random.normal(ks[6], (1, HIDDEN_DIM), jnp.float32) * 0.1
        a_dst2 = jax.random.normal(ks[7], (1, HIDDEN_DIM), jnp.float32) * 0.1
        b2 = jnp.zeros((HIDDEN_DIM,), jnp.float32)
        return {'edge_index': edge_index, 'emb': emb, 'W1': W1, 'a_src1': a_src1, 'a_dst1': a_dst1, 'b1': b1, 'W2': W2, 'a_src2': a_src2, 'a_dst2': a_dst2, 'b2': b2}
    _L0_gnn_all = _L0_gnn_setup()
    _L0_gnn_in = {k: v for k, v in _L0_gnn_all.items() if k in ('W1', 'a_src1', 'a_dst1', 'b1', 'W2', 'a_src2', 'a_dst2', 'b2')}
    del _L0_gnn_all

    def _L1_gnn_setup():
        import jax, jax.numpy as jnp
        import numpy as np
        N = 50000
        E = 25000
        D = 64
        H = 64
        DE = 32

        def _transformer_conv(x, src, dst, edge_attr, wq, bq, wk, bk, wv, bv, we, ws, bs, n_nodes):
            q = x @ wq + bq
            k = x @ wk + bk
            v = x @ wv + bv
            e = edge_attr @ we
            ke = k[src] + e
            score = jnp.sum(q[dst] * ke, axis=-1) / jnp.sqrt(jnp.asarray(ke.shape[-1], x.dtype))
            smax = jax.ops.segment_max(score, dst, num_segments=n_nodes)
            a = jnp.exp(score - smax[dst])
            denom = jax.ops.segment_sum(a, dst, num_segments=n_nodes)
            alpha = a / denom[dst]
            msg = alpha[:, None] * (v[src] + e)
            out = jax.ops.segment_sum(msg, dst, num_segments=n_nodes)
            out = out + x @ ws + bs
            return out
        key = jax.random.key(seed)
        ks = jax.random.split(key, 24)

        def g(i, shape, scale):
            return jax.random.normal(ks[i], shape, dtype=jnp.float32) * scale
        inp = {'x': g(0, (N, D), 1.0), 'edge_index': jax.random.randint(ks[1], (2, E), 0, N, dtype=jnp.int64), 'edge_attr': g(2, (E, DE), 1.0), 'q1_w': g(3, (D, H), D ** (-0.5)), 'q1_b': jnp.zeros((H,), jnp.float32), 'k1_w': g(4, (D, H), D ** (-0.5)), 'k1_b': jnp.zeros((H,), jnp.float32), 'v1_w': g(5, (D, H), D ** (-0.5)), 'v1_b': jnp.zeros((H,), jnp.float32), 'e1_w': g(6, (DE, H), DE ** (-0.5)), 's1_w': g(7, (D, H), D ** (-0.5)), 's1_b': jnp.zeros((H,), jnp.float32), 'q2_w': g(8, (H, H), H ** (-0.5)), 'q2_b': jnp.zeros((H,), jnp.float32), 'k2_w': g(9, (H, H), H ** (-0.5)), 'k2_b': jnp.zeros((H,), jnp.float32), 'v2_w': g(10, (H, H), H ** (-0.5)), 'v2_b': jnp.zeros((H,), jnp.float32), 'e2_w': g(11, (DE, H), DE ** (-0.5)), 's2_w': g(12, (H, H), H ** (-0.5)), 's2_b': jnp.zeros((H,), jnp.float32), 'skip_w': g(13, (2 * H, D), (2 * H) ** (-0.5)), 'skip_b': jnp.zeros((D,), jnp.float32)}
        return inp
    _L1_gnn_all = _L1_gnn_setup()
    _L1_gnn_in = {k: v for k, v in _L1_gnn_all.items() if k in ('q1_w', 'q1_b', 'k1_w', 'k1_b', 'v1_w', 'v1_b', 'e1_w', 's1_w', 's1_b', 'q2_w', 'q2_b', 'k2_w', 'k2_b', 'v2_w', 'v2_b', 'e2_w', 's2_w', 's2_b', 'skip_w', 'skip_b')}
    del _L1_gnn_all

    def _L2_gnn_setup():
        import jax, jax.numpy as jnp
        import numpy as np
        M = 50000
        E = 25000
        C_IN = 64
        C_OUT = 64
        DIM = 3
        RADIUS = 1.0
        EPS = 1e-05

        def layer_norm(x, g, b):
            mu = jnp.mean(x, axis=-1, keepdims=True)
            var = jnp.mean((x - mu) ** 2, axis=-1, keepdims=True)
            return (x - mu) * jax.lax.rsqrt(var + EPS) * g + b
        key = jax.random.key(seed)
        ks = jax.random.split(key, 12)
        inv = 1.0 / np.sqrt(C_OUT)
        return {'source': jax.random.randint(ks[0], (E,), 0, M), 'target': jax.random.randint(ks[1], (E,), 0, M), 'features': jax.random.normal(ks[2], (M, C_IN), dtype=jnp.float32), 'hood_coords': jax.random.normal(ks[3], (E, DIM), dtype=jnp.float32), 'Wd1': jax.random.normal(ks[4], (DIM, C_OUT), dtype=jnp.float32) / np.sqrt(DIM), 'bd1': jnp.zeros((C_OUT,), jnp.float32), 'g1': jnp.ones((C_OUT,), jnp.float32), 'b1': jnp.zeros((C_OUT,), jnp.float32), 'Wd2': jax.random.normal(ks[5], (C_OUT, C_OUT), dtype=jnp.float32) * inv, 'bd2': jnp.zeros((C_OUT,), jnp.float32), 'g2': jnp.ones((C_OUT,), jnp.float32), 'b2': jnp.zeros((C_OUT,), jnp.float32), 'W1': jax.random.normal(ks[6], (C_IN, C_OUT), dtype=jnp.float32) / np.sqrt(C_IN), 'W2': jax.random.normal(ks[7], (C_IN, C_OUT), dtype=jnp.float32) / np.sqrt(C_IN), 'W3': jax.random.normal(ks[8], (C_IN, C_OUT), dtype=jnp.float32) / np.sqrt(C_IN)}
    _L2_gnn_all = _L2_gnn_setup()
    _L2_gnn_in = {k: v for k, v in _L2_gnn_all.items() if k in ('Wd1', 'bd1', 'g1', 'b1', 'Wd2', 'bd2', 'g2', 'b2', 'W1', 'W2', 'W3')}
    del _L2_gnn_all

    def _L3_gnn_setup():
        import jax, jax.numpy as jnp
        import numpy as np
        NUM_NODES = 150000
        EMB_DIM = 64
        NUM_EDGES = 62500
        key = jax.random.key(seed)
        k1, k2 = jax.random.split(key)
        x = jax.random.normal(k1, (NUM_NODES, EMB_DIM), dtype=jnp.float32)
        edge_index = jax.random.randint(k2, (2, NUM_EDGES), 0, NUM_NODES, dtype=jnp.int64)
        return {'x': x, 'edge_index': edge_index}
    _L3_gnn_all = _L3_gnn_setup()
    _L3_gnn_in = {k: v for k, v in _L3_gnn_all.items() if k in ()}
    del _L3_gnn_all
    return {'x': x, 'src': src, 'dst': dst, 'edge_attr_3': edge_attr_3, 'edge_attr_32': edge_attr_32, 'L0_gnn_W1': _L0_gnn_in['W1'], 'L0_gnn_a_src1': _L0_gnn_in['a_src1'], 'L0_gnn_a_dst1': _L0_gnn_in['a_dst1'], 'L0_gnn_b1': _L0_gnn_in['b1'], 'L0_gnn_W2': _L0_gnn_in['W2'], 'L0_gnn_a_src2': _L0_gnn_in['a_src2'], 'L0_gnn_a_dst2': _L0_gnn_in['a_dst2'], 'L0_gnn_b2': _L0_gnn_in['b2'], 'L1_gnn_q1_w': _L1_gnn_in['q1_w'], 'L1_gnn_q1_b': _L1_gnn_in['q1_b'], 'L1_gnn_k1_w': _L1_gnn_in['k1_w'], 'L1_gnn_k1_b': _L1_gnn_in['k1_b'], 'L1_gnn_v1_w': _L1_gnn_in['v1_w'], 'L1_gnn_v1_b': _L1_gnn_in['v1_b'], 'L1_gnn_e1_w': _L1_gnn_in['e1_w'], 'L1_gnn_s1_w': _L1_gnn_in['s1_w'], 'L1_gnn_s1_b': _L1_gnn_in['s1_b'], 'L1_gnn_q2_w': _L1_gnn_in['q2_w'], 'L1_gnn_q2_b': _L1_gnn_in['q2_b'], 'L1_gnn_k2_w': _L1_gnn_in['k2_w'], 'L1_gnn_k2_b': _L1_gnn_in['k2_b'], 'L1_gnn_v2_w': _L1_gnn_in['v2_w'], 'L1_gnn_v2_b': _L1_gnn_in['v2_b'], 'L1_gnn_e2_w': _L1_gnn_in['e2_w'], 'L1_gnn_s2_w': _L1_gnn_in['s2_w'], 'L1_gnn_s2_b': _L1_gnn_in['s2_b'], 'L1_gnn_skip_w': _L1_gnn_in['skip_w'], 'L1_gnn_skip_b': _L1_gnn_in['skip_b'], 'L2_gnn_Wd1': _L2_gnn_in['Wd1'], 'L2_gnn_bd1': _L2_gnn_in['bd1'], 'L2_gnn_g1': _L2_gnn_in['g1'], 'L2_gnn_b1': _L2_gnn_in['b1'], 'L2_gnn_Wd2': _L2_gnn_in['Wd2'], 'L2_gnn_bd2': _L2_gnn_in['bd2'], 'L2_gnn_g2': _L2_gnn_in['g2'], 'L2_gnn_b2': _L2_gnn_in['b2'], 'L2_gnn_W1': _L2_gnn_in['W1'], 'L2_gnn_W2': _L2_gnn_in['W2'], 'L2_gnn_W3': _L2_gnn_in['W3']}

def reference(x, src, dst, edge_attr_3, edge_attr_32, L0_gnn_W1, L0_gnn_a_src1, L0_gnn_a_dst1, L0_gnn_b1, L0_gnn_W2, L0_gnn_a_src2, L0_gnn_a_dst2, L0_gnn_b2, L1_gnn_q1_w, L1_gnn_q1_b, L1_gnn_k1_w, L1_gnn_k1_b, L1_gnn_v1_w, L1_gnn_v1_b, L1_gnn_e1_w, L1_gnn_s1_w, L1_gnn_s1_b, L1_gnn_q2_w, L1_gnn_q2_b, L1_gnn_k2_w, L1_gnn_k2_b, L1_gnn_v2_w, L1_gnn_v2_b, L1_gnn_e2_w, L1_gnn_s2_w, L1_gnn_s2_b, L1_gnn_skip_w, L1_gnn_skip_b, L2_gnn_Wd1, L2_gnn_bd1, L2_gnn_g1, L2_gnn_b1, L2_gnn_Wd2, L2_gnn_bd2, L2_gnn_g2, L2_gnn_b2, L2_gnn_W1, L2_gnn_W2, L2_gnn_W3):
    import jax
    import jax.numpy as jnp

    def _L0_gnn_ref(edge_index, emb, W1, a_src1, a_dst1, b1, W2, a_src2, a_dst2, b2):
        import jax, jax.numpy as jnp
        import numpy as np
        NUM_NODES = 3125
        EMBED_DIM = 64
        HIDDEN_DIM = 64
        HEADS = 4
        NEG_SLOPE = 0.2

        def _gat_conv(x, src, dst, num_nodes, W, a_s, a_d, heads, out_ch):
            h = (x @ W).reshape(-1, heads, out_ch)
            alpha_s = (h * a_s[None]).sum(-1)
            alpha_d = (h * a_d[None]).sum(-1)
            e = alpha_s[src] + alpha_d[dst]
            e = jnp.where(e > 0, e, NEG_SLOPE * e)
            m = jax.ops.segment_max(e, dst, num_segments=num_nodes)
            w = jnp.exp(e - m[dst])
            denom = jax.ops.segment_sum(w, dst, num_segments=num_nodes)
            alpha = w / (denom[dst] + 1e-16)
            out = jax.ops.segment_sum(alpha[:, :, None] * h[src], dst, num_segments=num_nodes)
            return out

        def _forward(edge_index, emb, W1, a_src1, a_dst1, b1, W2, a_src2, a_dst2, b2):
            N = emb.shape[0]
            loops = jnp.arange(N, dtype=edge_index.dtype)
            src = jnp.concatenate([edge_index[0], loops])
            dst = jnp.concatenate([edge_index[1], loops])
            x = _gat_conv(emb, src, dst, N, W1, a_src1, a_dst1, HEADS, HIDDEN_DIM // HEADS)
            x = x.reshape(N, -1) + b1
            x = jax.nn.elu(x)
            x = _gat_conv(x, src, dst, N, W2, a_src2, a_dst2, 1, HIDDEN_DIM)
            x = x[:, 0, :] + b2
            norm = jnp.maximum(jnp.linalg.norm(x, axis=1, keepdims=True), 1e-12)
            return x / norm
        return _forward(edge_index, emb, W1, a_src1, a_dst1, b1, W2, a_src2, a_dst2, b2)

    def _L1_gnn_ref(x, edge_index, edge_attr, q1_w, q1_b, k1_w, k1_b, v1_w, v1_b, e1_w, s1_w, s1_b, q2_w, q2_b, k2_w, k2_b, v2_w, v2_b, e2_w, s2_w, s2_b, skip_w, skip_b):
        import jax, jax.numpy as jnp
        import numpy as np
        N = 50000
        E = 25000
        D = 64
        H = 64
        DE = 32

        def _transformer_conv(x, src, dst, edge_attr, wq, bq, wk, bk, wv, bv, we, ws, bs, n_nodes):
            q = x @ wq + bq
            k = x @ wk + bk
            v = x @ wv + bv
            e = edge_attr @ we
            ke = k[src] + e
            score = jnp.sum(q[dst] * ke, axis=-1) / jnp.sqrt(jnp.asarray(ke.shape[-1], x.dtype))
            smax = jax.ops.segment_max(score, dst, num_segments=n_nodes)
            a = jnp.exp(score - smax[dst])
            denom = jax.ops.segment_sum(a, dst, num_segments=n_nodes)
            alpha = a / denom[dst]
            msg = alpha[:, None] * (v[src] + e)
            out = jax.ops.segment_sum(msg, dst, num_segments=n_nodes)
            out = out + x @ ws + bs
            return out
        src, dst = (edge_index[0], edge_index[1])
        n = x.shape[0]
        h1 = jax.nn.relu(_transformer_conv(x, src, dst, edge_attr, q1_w, q1_b, k1_w, k1_b, v1_w, v1_b, e1_w, s1_w, s1_b, n))
        h2 = jax.nn.relu(_transformer_conv(h1, src, dst, edge_attr, q2_w, q2_b, k2_w, k2_b, v2_w, v2_b, e2_w, s2_w, s2_b, n))
        skip_xs = jnp.concatenate([h1, h2], axis=-1)
        return jax.nn.relu(skip_xs @ skip_w + skip_b)

    def _L2_gnn_ref(source, target, features, hood_coords, Wd1, bd1, g1, b1, Wd2, bd2, g2, b2, W1, W2, W3):
        import jax, jax.numpy as jnp
        import numpy as np
        M = 50000
        E = 25000
        C_IN = 64
        C_OUT = 64
        DIM = 3
        RADIUS = 1.0
        EPS = 1e-05

        def layer_norm(x, g, b):
            mu = jnp.mean(x, axis=-1, keepdims=True)
            var = jnp.mean((x - mu) ** 2, axis=-1, keepdims=True)
            return (x - mu) * jax.lax.rsqrt(var + EPS) * g + b
        m = features.shape[0]
        x = hood_coords / RADIUS
        d = jax.nn.gelu(layer_norm(x @ Wd1 + bd1, g1, b1), approximate=False)
        d = jax.nn.gelu(layer_norm(d @ Wd2 + bd2, g2, b2), approximate=False)
        w1 = features @ W1
        w2 = features @ W2
        w3 = features @ W3
        logits = w1[target] - w2[source] + d
        seg_max = jax.ops.segment_max(logits, target, num_segments=m)
        seg_max = jnp.where(jnp.isfinite(seg_max), seg_max, 0.0)
        e = jnp.exp(logits - seg_max[target])
        denom = jax.ops.segment_sum(e, target, num_segments=m)
        a = e / denom[target]
        out = jax.ops.segment_sum(a * (w3[source] + d), target, num_segments=m)
        return out

    def _L3_gnn_ref(x, edge_index):
        import jax, jax.numpy as jnp
        import numpy as np
        NUM_NODES = 150000
        EMB_DIM = 64
        NUM_EDGES = 62500
        N = x.shape[0]
        row, col = (edge_index[0], edge_index[1])
        deg = jax.ops.segment_sum(jnp.ones(row.shape[0], dtype=x.dtype), col, num_segments=N)
        deg_inv_sqrt = jnp.where(deg > 0, jax.lax.rsqrt(jnp.where(deg > 0, deg, 1.0)), 0.0)
        norm = (deg_inv_sqrt[row] * deg_inv_sqrt[col])[:, None]

        def lgconv(h):
            return jax.ops.segment_sum(h[row] * norm, col, num_segments=N)
        emb_0 = x
        emb_1 = lgconv(emb_0)
        emb_2 = lgconv(emb_1)
        return (emb_0 + emb_1 + emb_2) / 3.0
    edge_index = jnp.stack([src, dst])
    x = _layernorm(x + _L0_gnn_ref(edge_index, x, L0_gnn_W1, L0_gnn_a_src1, L0_gnn_a_dst1, L0_gnn_b1, L0_gnn_W2, L0_gnn_a_src2, L0_gnn_a_dst2, L0_gnn_b2), axis=-1)
    x = _layernorm(x + _L1_gnn_ref(x, edge_index, edge_attr_32, L1_gnn_q1_w, L1_gnn_q1_b, L1_gnn_k1_w, L1_gnn_k1_b, L1_gnn_v1_w, L1_gnn_v1_b, L1_gnn_e1_w, L1_gnn_s1_w, L1_gnn_s1_b, L1_gnn_q2_w, L1_gnn_q2_b, L1_gnn_k2_w, L1_gnn_k2_b, L1_gnn_v2_w, L1_gnn_v2_b, L1_gnn_e2_w, L1_gnn_s2_w, L1_gnn_s2_b, L1_gnn_skip_w, L1_gnn_skip_b), axis=-1)
    x = _layernorm(x + _L2_gnn_ref(src, dst, x, edge_attr_3, L2_gnn_Wd1, L2_gnn_bd1, L2_gnn_g1, L2_gnn_b1, L2_gnn_Wd2, L2_gnn_bd2, L2_gnn_g2, L2_gnn_b2, L2_gnn_W1, L2_gnn_W2, L2_gnn_W3), axis=-1)
    x = _layernorm(x + _L3_gnn_ref(x, edge_index), axis=-1)
    return x

_drawn_inputs = setup_inputs


def setup_inputs(seed=0):
    import zlib

    import numpy as np

    out = dict(_drawn_inputs(seed))
    spreads = {'L0_gnn_b1': (0.0, 0.1),
     'L0_gnn_b2': (0.0, 0.1),
     'L1_gnn_q1_b': (0.0, 0.8),
     'L1_gnn_k1_b': (0.0, 2.0),
     'L1_gnn_v1_b': (0.0, 0.299),
     'L1_gnn_s1_b': (0.0, 0.1),
     'L1_gnn_q2_b': (0.0, 0.8),
     'L1_gnn_k2_b': (0.0, 2.0),
     'L1_gnn_v2_b': (0.0, 0.328),
     'L1_gnn_s2_b': (0.0, 0.407),
     'L1_gnn_skip_b': (0.0, 0.1),
     'L2_gnn_bd1': (0.0, 0.1),
     'L2_gnn_g1': (1.0, 0.2),
     'L2_gnn_b1': (0.0, 0.1),
     'L2_gnn_bd2': (0.0, 0.1),
     'L2_gnn_g2': (1.0, 0.2),
     'L2_gnn_b2': (0.0, 0.1)}
    factors = {'L0_gnn_W1': 2.853,
     'L0_gnn_a_src1': 8.0,
     'L0_gnn_a_dst1': 21.384,
     'L0_gnn_a_src2': 8.0,
     'L0_gnn_a_dst2': 61.067,
     'L2_gnn_W1': 200.0}
    for name, (base, spread) in spreads.items():
        noise = np.random.default_rng([zlib.crc32(name.encode()), seed]).standard_normal(out[name].shape)
        drawn = base * np.exp(spread * noise) if base else spread * noise
        out[name] = jnp.asarray(drawn.astype(out[name].dtype))
    for name, factor in factors.items():
        out[name] = (out[name] * factor).astype(out[name].dtype)
    return out
```

```python
import numpy as np
import concourse.bass as bass
from concourse import mybir
from contextlib import ExitStack

N, E, D = 3125, 103125, 64
NP, NT = 125, 25
T = 128
J = 4
W = J * T
G = 102
S = G * W
EP = 2 * S
TILES = EP // T
BIG = 1.0e30
OOB = 1.0e6
EPS = 1e-5
DE = 32

KINDS = ["gat1", "gat2", "tc1", "tc2", "pt", "gc1", "gc2"]

CI, CB, CM, CN = 0, 128, 256, 320
CE, CO = CN + NT, CN + NT + 128
CW = CO + 128


def shape_constants():
    c = np.zeros((128, CW), np.float32)
    c[:, CI:CI + 128] = np.eye(128)
    c[:64, CB:CB + 64] = 1
    c[64:, CB + 64:CB + 128] = 1
    for k in range(2):
        c[k::2, CE + 128 * k:CE + 128 * k + 128] = np.eye(128)[k::2]
    f = np.arange(64)
    c[:64, CM:CM + 64] = f[:, None] // 16 == f[None, :] // 16
    c[:NP, CN:CN + NT] = np.arange(N).reshape(NP, NT)
    return c


def build(nc, a):
    f32, bf16, i32 = mybir.dt.float32, mybir.dt.bfloat16, mybir.dt.int32
    ALU, ACT, AX = mybir.AluOpType, mybir.ActivationFunctionType, mybir.AxisListType.X
    ds = bass.ds
    on_axis0 = lambda ap: bass.IndirectOffsetOnAxis(ap=ap, axis=0)
    ctx = ExitStack()

    def sb(name, shape, dt=f32):
        return ctx.enter_context(nc.sbuf_tensor(name, shape, dt))

    def dram(name, shape, dt=f32):
        return nc.dram_tensor(name, shape, dt, kind="Internal").ap()

    sems = {}

    def sem(name):
        if name not in sems:
            sems[name] = ctx.enter_context(nc.semaphore(name))
        return sems[name]

    def need(eng, name, value):
        if not isinstance(value, int) or value > 0:
            eng.wait_ge(sem(name), value)

    with ctx:
        table = dram("table", [N, 128])
        table3 = dram("table3", [N, 64])
        spread = dram("spread", [EP, 64])
        flags = dram("flags", [G, 2, 2 * W], bf16)
        ends = dram("ends", [EP, 128])
        ends3 = dram("ends3", [EP, 64])
        dist = dram("dist", [G, 128, W])
        starts_d = dram("starts_d", [N + 1])

        cst = sb("cst", [128, CW])
        ident, bones = cst[:, CI:CI + 128], cst[:, CB:CB + 128]
        hmask, nid = cst[0:64, CM:CM + 64], cst[0:NP, CN:CN + NT]
        even, odd = cst[:, CE:CE + 128], cst[:, CO:CO + 128]
        X = sb("X", [NP, NT, D])
        H = sb("H", [NP, NT, D])
        SK = sb("SK", [NP, NT, D])
        tmp = [sb(f"tmp{i}", [NP, NT, D]) for i in range(2)]
        TT = sb("TT", [128, NT, 256])
        R = sb("R", [NP, NT, 128])
        R3 = R[:, :, 0:64]
        xT = sb("xT", [65, NT, NP])
        h1T = sb("h1T", [65, NT, NP])
        starts = sb("starts", [NP, NT])
        endsn = sb("endsn", [NP, NT])
        has = sb("has", [NP, NT])
        dinv = sb("dinv", [NP, NT])
        st1 = [sb(f"st{i}", [NP, NT]) for i in range(4)]
        idx_end = sb("idx_end", [NP, NT], i32)
        idx_a = sb("idx_a", [NP, NT], i32)
        idx_b = sb("idx_b", [NP, NT], i32)
        idx_t = sb("idx_t", [NP, NT], i32)
        midd = sb("midd", [64, 2], i32)
        cross = sb("cross", [64, 1])
        crossb = sb("crossb", [64, 1])
        wc = {"gat1": sb("wc_gat1", [65, 192]), "gat2": sb("wc_gat2", [65, 192]),
              "tc1": sb("wc_tc1", [65, 256]), "tc2": sb("wc_tc2", [65, 256]), "pt": sb("wc_pt", [65, 192])}
        wT = sb("wT", [64, 2, 64])
        avec = sb("avec", [64, 4])
        amat = sb("amat", [64, 2, 192])
        skw = sb("skw", [65, 2, 64])
        we = [sb(f"we{i}", [64, 128]) for i in range(2)]
        bias = sb("bias", [NP, 2, 64])
        wd1 = sb("wd1", [7, 128])
        wd2 = sb("wd2", [128, 128])
        pv4 = sb("pv4", [128, 5])
        mcol = sb("mcol", [128, 2])
        epsc = sb("epsc", [128, 1])
        Gt = [sb(f"Gt{i}", [128, J, 2, 128]) for i in range(2)]
        ix = [sb(f"ix{i}", [128, 2 * J], i32) for i in range(2)]
        xd = [sb(f"xd{i}", [128, J, 2, 64]) for i in range(2)]
        fl = [sb(f"fl{i}", [128, 2 * W], bf16) for i in range(2)]
        ea = [sb(f"ea{i}", [128, W]) for i in range(2)]
        ex = [sb(f"ex{i}", [128, W]) for i in range(2)]
        sr = sb("sr", [128, W])
        sl = sb("sl", [128, W])
        M = [sb(f"M{i}", [128, W + 1]) for i in range(2)]
        arg = [sb(f"arg{i}", [128, 2 * W]) for i in range(2)]
        ap = [sb(f"ap{i}", [128, 2 * W]) for i in range(2)]
        pv = sb("pv", [128, W])
        num = [sb(f"num{i}", [128, W]) for i in range(2)]
        den = [sb(f"den{i}", [128, W]) for i in range(2)]
        O = [sb(f"O{i}", [128, 2, J, 128]) for i in range(2)]
        O3 = [o[:, :, :, 0:64] for o in O]
        mg = sb("mg", [128, 3])
        mgb = sb("mgb", [64, 3])
        mw = sb("mw", [64, 6])
        parity = sb("parity", [64, 2])

        ps = [ctx.enter_context(nc.psum_tensor(f"ps{i}", [128, 512], f32)) for i in range(8)]
        pX, pS, pV, pR, pN, pD = ps[0], ps[1], [ps[2], ps[3]], ps[4], ps[5], ps[6]

        flat = lambda t: t.rearrange("p t c -> p (t c)")
        bc = lambda t: t.unsqueeze(2).to_broadcast([NP, NT, 64])

        class Chain:

            def __init__(self, name):
                self.eng, self.sem, self.n = None, sem(name), 0

            def __call__(self, instruction):
                self.n += 1
                instruction.then_inc(self.sem, 1)
                self.eng.wait_ge(self.sem, self.n)

        node_chain = Chain("vector_chain")

        def dve_chain(dve):
            node_chain.eng = dve
            return node_chain


        def base(kind):
            if kind.startswith("gc"):
                return G * (int(kind[-1]) - 1)
            return G * KINDS.index(kind)

        def order(kind):
            return KINDS.index(kind)

        def rows_merged(kind):
            return sum(1 if k.startswith("gc") else 2 for k in KINDS[:order(kind) + 1])

        def walk(step):
            step(0, 0)
            step(0, 1)
            return step

        def pass_sp(sp, kind):
            gc = kind.startswith("gc")
            B = base(kind)
            if not gc:
                sp.wait_ge(sem(f"{kind}_spread"), 16 * 2 * NT)

            def step(it, s):
                g = 2 * it + s
                n = B + g + 1
                need(sp, f"{kind}_gathered{s}", 2 * J * 16 * it)
                sp.dma_start(ix[s][:, :], a["src_g"][ds(g, 1), :, :].rearrange("a p j -> p (a j)")) \
                    .then_inc(sem(f"{kind}_indices{s}"), 16)
                if gc:
                    if not isinstance(it, int) or it > 0:
                        sp.wait_ge(sem("gc_summed"), n - 2)
                    for c in range(2):
                        sp.dma_start(fl[s][64 * c:64 * c + 64, 0:W],
                                     flags[ds(g, 1), c, 0:W].to_broadcast([64, W])) \
                            .then_inc(sem(f"{kind}_loaded{s}"), 16)
                    return
                if not isinstance(it, int) or it > 0:
                    sp.wait_ge(sem("denominated"), n - 2)
                    sp.wait_ge(sem("values_turned"), n - 2)
                for c in range(2):
                    sp.dma_start(fl[s][64 * c:64 * c + 64, :], flags[ds(g, 1), c, :].to_broadcast([64, 2 * W])) \
                        .then_inc(sem(f"{kind}_loaded{s}"), 16)
                sv = spread.rearrange("(c g j p) f -> c g p j f", c=2, g=G, j=J)
                for c in range(2):
                    sp.dma_start(xd[s][:, :, c, :], sv[c, ds(g, 1)].rearrange("a p j f -> p (a j) f")) \
                        .then_inc(sem(f"{kind}_loaded{s}"), 16)
                if kind in ("tc1", "tc2"):
                    sp.dma_start(ea[s][0:64, :], a["ea32"][ds(g, 1), :, :].rearrange("a p j -> p (a j)")) \
                        .then_inc(sem(f"{kind}_loaded{s}"), 16)
                if kind == "pt":
                    sp.dma_start(ea[s][:, :], dist[ds(g, 1), :, :].rearrange("a p j -> p (a j)")) \
                        .then_inc(sem(f"{kind}_loaded{s}"), 16)

            walk(step)
            with sp.Fori(1, G // 2) as it:
                step(it, 0)
                step(it, 1)

        def nload(kind):
            return 2 if kind.startswith("gc") else 4 if kind.startswith("gat") else 5

        def pass_pool(pool, kind):
            gc = kind.startswith("gc")
            B = base(kind)
            pool.wait_ge(sem("tables_written"), 16 * (order(kind) + 1))

            def step(it, s):
                n = B + 2 * it + s + 1
                pool.wait_ge(sem(f"{kind}_indices{s}"), 16 * (it + 1))
                if not isinstance(it, int) or it > 0:
                    pool.wait_ge(sem("gc_turned" if gc else "values_turned"), n - 2)
                pool.nop(nofuse=True)
                for c in range(2):
                    for j in range(J):
                        k = c * J + j
                        src = table3 if gc else table
                        to = Gt[s][:, j, 0, 64 * c:64 * c + 64] if gc else Gt[s][:, j, c, :]
                        pool.indirect_dma_start(out=to, out_offset=None, in_=src[:, :],
                                                in_offset=on_axis0(ix[s][:, k:k + 1])) \
                            .then_inc(sem(f"{kind}_gathered{s}"), 16)

            walk(step)
            with pool.Fori(1, G // 2) as it:
                step(it, 0)
                step(it, 1)

        def pass_pe(pe, kind):
            gc = kind.startswith("gc")
            B = base(kind)
            edge = None if kind.startswith("gat") or gc else we[int(kind == "tc2")] if kind != "pt" else ident
            ek = 128 if kind == "pt" else 64

            def turn(out, s, half, signal):
                if edge is not None:
                    pe.matmul(out[:, :], edge[0:ek, :], ea[s][0:ek, :], start=True, stop=False)
                for j in range(J):
                    rows = Gt[s][:, j, :, :].rearrange("p c f -> p (c f)")[:, half:256:2]
                    cols = out[:, T * j:T * j + T]
                    if edge is None:
                        last = pe.matmul(cols, rows, ident, start=True, stop=True)
                    else:
                        last = pe.matmul(cols, rows, ident, start=False, stop=(j == J - 1))
                last.then_inc(sem(signal), 1)

            def front(it, s):
                n = B + 2 * it + s + 1
                first = isinstance(it, int)
                if gc:
                    pe.wait_ge(sem(f"{kind}_gathered{s}"), 2 * J * 16 * (it + 1))
                    if not first:
                        pe.wait_ge(sem("gc_summed"), n - 2)
                    for j in range(J):
                        last = pe.transpose(pV[s][:, T * j:T * j + T], Gt[s][:, j, 0, :], ident)
                    last.then_inc(sem("gc_turned"), 1)
                    return
                pe.wait_ge(sem(f"{kind}_loaded{s}"), 16 * nload(kind) * (it + 1))
                need(pe, "spread_out", n - 1)
                for j in range(J):
                    last = pe.transpose(pX[:, T * j:T * j + T],
                                        xd[s][:, j, :, :].rearrange("p c f -> p (c f)"), ident)
                last.then_inc(sem("targets_turned"), 1)
                pe.wait_ge(sem(f"{kind}_gathered{s}"), 2 * J * 16 * (it + 1))
                need(pe, "combined", n - 1)
                turn(pS, s, 0, "logits_turned")
                if n - 2 > 0 if isinstance(n, int) else True:
                    pe.wait_ge(sem("weighed"), n - 2)
                turn(pV[s], s, 1, "values_turned")
                if kind in ("tc1", "tc2"):
                    pe.wait_ge(sem("combined"), n)
                    need(pe, "arguments", n - 1)
                    pe.matmul(pR[:, :], bones, sr[:, :], start=True, stop=True) \
                        .then_inc(sem("scored"), 1)

            def back(it, s):
                n = B + 2 * it + s + 1
                if gc:
                    pe.wait_ge(sem("gc_summed"), n)
                    need(pe, "gc_evacuated", n - 1)
                    for j in range(J):
                        last = pe.transpose(pN[:, T * j:T * j + T], num[s][:, T * j:T * j + T], ident)
                    last.then_inc(sem("gc_back"), 1)
                    return
                pe.wait_ge(sem("numerated"), n)
                pe.wait_ge(sem("denominated"), n)
                need(pe, "evacuated", n - 1)
                for j in range(J):
                    pe.transpose(pN[:, T * j:T * j + T], num[s][:, T * j:T * j + T], ident)
                for j in range(J):
                    out, part = pD[:, T * j:T * j + T], den[s][:, T * j:T * j + T]
                    if kind.startswith("gat"):
                        pe.matmul(out, part, even, start=True, stop=False)
                        last = pe.matmul(out, M[s][:, T * j + 1:T * j + T + 1], odd, start=False, stop=True)
                    else:
                        last = pe.transpose(out, part, ident)
                last.then_inc(sem("turned_back"), 1)

            front(0, 0)
            front(0, 1)
            back(0, 0)
            with pe.Fori(1, G // 2) as it:
                front(it, 0)
                back(it - 1, 1)
                front(it, 1)
                back(it, 0)
            back(G // 2 - 1, 1)

        def pass_dve(dve, kind):
            gc = kind.startswith("gc")
            B = base(kind)
            tc = kind in ("tc1", "tc2")
            B_tc = G * (int(kind[-1]) - 1) if tc else 0
            B_gat = G * (int(kind[-1]) - 1) if kind.startswith("gat") else 0

            def front(it, s):
                g = 2 * it + s
                n = B + g + 1
                first = isinstance(it, int)
                dve.wait_ge(sem(f"{kind}_loaded{s}"), 16 * nload(kind) * (it + 1))
                inside, new = fl[s][:, 0:W], fl[s][:, W:2 * W]
                if gc:
                    dve.wait_ge(sem("gc_turned"), n)
                    if n - 2 > 0 if isinstance(n, int) else True:
                        dve.wait_ge(sem("gc_back"), n - 2)
                    need(dve, "gc_summed", n - 1)
                    dve.tensor_tensor_scan(num[s][:, :], inside, pV[s][:, :], num[1 - s][:, W - 1:W],
                                           ALU.mult, ALU.add).then_inc(sem("gc_summed"), 1)
                    return
                dve.wait_ge(sem("targets_turned"), n)
                dve.tensor_tensor_scan(ex[s][:, :], inside, pX[:, :], ex[1 - s][:, W - 1:W],
                                       ALU.mult, ALU.add).then_inc(sem("spread_out"), 1)
                dve.wait_ge(sem("spread_out"), n)
                dve.wait_ge(sem("logits_turned"), n)
                if tc and (n - 1 > 0 if isinstance(n, int) else True):
                    if not (isinstance(it, int) and g == 0):
                        dve.wait_ge(sem("scored"), B_tc + g)
                dve.tensor_tensor(sr[:, :], pS[:, :], ex[s][:, :], ALU.mult if tc else ALU.add) \
                    .then_inc(sem("combined"), 1)
                if tc:
                    dve.wait_ge(sem("scored"), B_tc + g + 1)
                    dve.tensor_scalar(sl[:, :], pR[:, :], 0.125, None, ALU.mult).then_inc(sem("logits"), 1)
                    logit = sl
                elif kind.startswith("gat"):
                    dve.wait_ge(sem("combined"), n)
                    dve.scalar_tensor_tensor(sl[:, :], sr[:, :], 0.2, sr[:, :], ALU.mult, ALU.max) \
                        .then_inc(sem("logits"), 1)
                    logit = sl
                else:
                    logit = sr
                if kind.startswith("gat") and (n - 2 > 0 if isinstance(n, int) else True):
                    dve.wait_ge(sem("turned_back"), n - 2)
                dve.tensor_copy(M[s][:, 0:1], M[1 - s][:, W:W + 1]).then_inc(sem("max_carried"), 1)
                if logit is sl:
                    dve.wait_ge(sem("logits"), B + g + 1)
                else:
                    dve.wait_ge(sem("combined"), n)
                dve.tensor_tensor_scan(M[s][:, 1:W + 1], new, logit[:, :], M[1 - s][:, W:W + 1],
                                       ALU.add, ALU.max).then_inc(sem("maxima"), 1)
                if n - 2 > 0 if isinstance(n, int) else True:
                    dve.wait_ge(sem("exponentiated"), n - 2)
                dve.wait_ge(sem("max_carried"), n)
                dve.wait_ge(sem("maxima"), n)
                dve.tensor_tensor(arg[s][:, W:2 * W], logit[:, :], M[s][:, 1:W + 1], ALU.subtract) \
                    .then_inc(sem("arguments"), 1)
                dve.tensor_tensor(arg[s][:, 0:W], M[s][:, 0:W], new, ALU.add).then_inc(sem("shifted"), 1)
                dve.wait_ge(sem("shifted"), n)
                dve.tensor_tensor(arg[s][:, 0:W], arg[s][:, 0:W], M[s][:, 1:W + 1], ALU.subtract) \
                    .then_inc(sem("decays"), 1)

            def back(it, s):
                if gc:
                    return
                n = B + 2 * it + s + 1
                dve.wait_ge(sem("exponentiated"), n)
                dve.wait_ge(sem("values_turned"), n)
                need(dve, "numerated", n - 1)
                need(dve, "denominated", n - 1)
                dve.tensor_tensor(pv[:, :], ap[s][:, W:2 * W], pV[s][:, :], ALU.mult) \
                    .then_inc(sem("weighed"), 1)
                if n - 2 > 0 if isinstance(n, int) else True:
                    dve.wait_ge(sem("turned_back"), n - 2)
                dve.tensor_tensor_scan(den[s][:, :], ap[s][:, 0:W], ap[s][:, W:2 * W], den[1 - s][:, W - 1:W],
                                       ALU.mult, ALU.add).then_inc(sem("denominated"), 1)
                dve.wait_ge(sem("weighed"), n)
                dve.tensor_tensor_scan(num[s][:, :], ap[s][:, 0:W], pv[:, :], num[1 - s][:, W - 1:W],
                                       ALU.mult, ALU.add).then_inc(sem("numerated"), 1)

            front(0, 0)
            front(0, 1)
            back(0, 0)
            with dve.Fori(1, G // 2) as it:
                front(it, 0)
                back(it - 1, 1)
                front(it, 1)
                back(it, 0)
            back(G // 2 - 1, 1)

            chain = dve_chain(dve)
            if gc:
                dve.wait_ge(sem("gc_summed"), B + G)
                chain(dve.tensor_copy(mg[:, 1:2], num[1][:, W - 1:W]))
            else:
                dve.wait_ge(sem("numerated"), B + G)
                dve.wait_ge(sem("denominated"), B + G)
                chain(dve.tensor_copy(mg[:, 0:1], M[1][:, W:W + 1]))
                chain(dve.tensor_copy(mg[:, 1:2], num[1][:, W - 1:W]))
                chain(dve.tensor_copy(mg[:, 2:3], den[1][:, W - 1:W]))
            dve.sem_inc(sem("last"), 1)
            dve.wait_ge(sem("moved"), 16 * (order(kind) + 1))
            if gc:
                chain(dve.scalar_tensor_tensor(mw[:, 4:5], mgb[:, 1:2], cross[:, 0:1], mg[0:64, 1:2],
                                               ALU.mult, ALU.add))
            else:
                chain(dve.tensor_tensor(mw[:, 0:1], mgb[:, 0:1], crossb[:, :], ALU.add))
                chain(dve.tensor_tensor(mw[:, 1:2], mw[:, 0:1], mg[0:64, 0:1], ALU.max))
                chain(dve.tensor_tensor(mw[:, 2:3], mg[0:64, 0:1], mw[:, 1:2], ALU.subtract))
                chain(dve.tensor_tensor(mw[:, 3:4], mw[:, 0:1], mw[:, 1:2], ALU.subtract))
                dve.sem_inc(sem("merge_arg"), 1)
                dve.wait_ge(sem("merge_exp"), order(kind) + 1)
                chain(dve.tensor_tensor(mgb[:, 1:2], mgb[:, 1:2], mw[:, 3:4], ALU.mult))
                chain(dve.tensor_tensor(mgb[:, 2:3], mgb[:, 2:3], mw[:, 3:4], ALU.mult))
                chain(dve.scalar_tensor_tensor(mw[:, 4:5], mg[0:64, 1:2], mw[:, 2:3], mgb[:, 1:2],
                                               ALU.mult, ALU.add))
                chain(dve.scalar_tensor_tensor(mw[:, 5:6], mg[0:64, 2:3], mw[:, 2:3], mgb[:, 2:3],
                                               ALU.mult, ALU.add))
                if kind.startswith("gat"):
                    chain(dve.tensor_tensor(mw[:, 5:6], mw[:, 5:6], parity[:, 0:1], ALU.mult))
                    chain(dve.scalar_tensor_tensor(mw[:, 5:6], mw[:, 1:2], parity[:, 1:2], mw[:, 5:6],
                                                   ALU.mult, ALU.add))
            dve.sem_inc(sem("merged"), 1)

        def pass_act(act, kind):
            gc = kind.startswith("gc")
            B = base(kind)

            def front(it, s):
                n = B + 2 * it + s + 1
                act.wait_ge(sem("arguments"), n)
                act.wait_ge(sem("decays"), n)
                if n - 2 > 0 if isinstance(n, int) else True:
                    act.wait_ge(sem("numerated"), n - 2)
                act.activation(ap[s][:, :], arg[s][:, :], ACT.Exp).then_inc(sem("exponentiated"), 1)

            def back(it, s):
                n = B + 2 * it + s + 1
                act.wait_ge(sem("gc_back" if gc else "turned_back"), n)
                if not isinstance(it, int) or it > 0:
                    act.wait_ge(sem(f"{kind}_stored{s}"), 32 * it)
                o = sem("gc_evacuated" if gc else "evacuated")
                w = 64 if gc else 128
                if not gc:
                    act.activation(O[s][:, :, :, 0:64],
                                   pN[:, :].rearrange("p (j c f) -> p c j f", j=J, c=2), ACT.Copy)
                    act.activation(O[s][:, :, :, 64:128],
                                   pD[:, :].rearrange("p (j c f) -> p c j f", j=J, c=2), ACT.Copy) \
                        .then_inc(o, 1)
                else:
                    act.activation(O3[s], pN[:, :].rearrange("p (j c f) -> p c j f", j=J, c=2), ACT.Copy) \
                        .then_inc(o, 1)
                act.wait_ge(o, n)
                g = 2 * it + s
                to = (ends3 if gc else ends).rearrange("(c g j p) f -> c g p j f", c=2, g=G, j=J)
                for c in range(2):
                    act.dma_start(to[c, ds(g, 1)].rearrange("a p j f -> p (a j) f"), O[s][:, c, :, 0:w]) \
                        .then_inc(sem(f"{kind}_stored{s}"), 16)

            if gc:
                back(0, 0)
                back(0, 1)
                with act.Fori(1, G // 2) as it:
                    back(it, 0)
                    back(it, 1)
            else:
                front(0, 0)
                front(0, 1)
                back(0, 0)
                with act.Fori(1, G // 2) as it:
                    front(it, 0)
                    back(it - 1, 1)
                    front(it, 1)
                    back(it, 0)
                back(G // 2 - 1, 1)
                act.wait_ge(sem("merge_arg"), order(kind) + 1)
                act.activation(mw[:, 2:4], mw[:, 2:4], ACT.Exp).then_inc(sem("merge_exp"), 1)

        def merge_sp(sp, kind):
            gc = kind.startswith("gc")
            sp.wait_ge(sem("last"), order(kind) + 1)
            sp.dma_start(mgb[:, :], mg[64:128, :]).then_inc(sem("moved"), 16)
            sp.wait_ge(sem("merged"), order(kind) + 1)
            for s in range(2):
                sp.wait_ge(sem(f"{kind}_stored{s}"), 32 * (G // 2))
            if gc:
                sp.dma_start(ends3[S - 1, :].rearrange("(f a) -> f a", a=1), mw[:, 4:5]) \
                    .then_inc(sem("row_merged"), 16)
            else:
                for h in range(2):
                    sp.dma_start(ends[S - 1, 64 * h:64 * h + 64].rearrange("(f a) -> f a", a=1),
                                 mw[:, 4 + h:5 + h]).then_inc(sem("row_merged"), 16)

        def take_pool(pool, kind):
            gc = kind.startswith("gc")
            pool.wait_ge(sem("row_merged"), 16 * rows_merged(kind))
            for t in range(NT):
                pool.indirect_dma_start(out=R3[:, t, :] if gc else R[:, t, :], out_offset=None,
                                        in_=(ends3 if gc else ends)[:, :],
                                        in_offset=on_axis0(idx_end[:, t:t + 1])) \
                    .then_inc(sem("taken"), 16)

        def scatter_pool(pool, kind):
            pool.wait_ge(sem("tabled"), NT * (order(kind) + 1))
            for t in range(NT):
                for ix_ in (idx_a, idx_b):
                    pool.indirect_dma_start(out=spread[:, :], out_offset=on_axis0(ix_[:, t:t + 1]),
                                            in_=TT[0:NP, t, 128:192], in_offset=None,
                                            bounds_check=EP - 1, oob_is_err=False) \
                        .then_inc(sem(f"{kind}_spread"), 16)

        def tables_sp(sp, kind):
            sp.wait_ge(sem("tabled"), NT * (order(kind) + 1))
            sp.dma_start(table.rearrange("(p t) c -> p t c", t=NT), TT[0:NP, :, 0:128]) \
                .then_inc(sem("tables_written"), 16)

        SOFT = KINDS[:5]
        NORMS = ["gat2", "tc2", "pt", "gc2"]
        CH = [(i, min(4, NT - i)) for i in range(0, NT, 4)]

        def turns_before(kind, tag):
            done = [(k, g) for k in SOFT for g in (("x", "h2") if k == "tc2" else ("x",))]
            return len(CH) * done.index((kind, tag))

        def turn_nodes_pe(pe, kind, x, tag):
            b = turns_before(kind, tag)
            for k, (t0, m) in enumerate(CH):
                if k >= 2:
                    pe.wait_ge(sem("nodes_kept"), b + k - 1)
                for i in range(m):
                    last = pe.transpose(ps[7 * (k % 2)][0:64, NP * i:NP * i + NP], x[:, t0 + i, :], ident[0:NP, 0:NP])
                last.then_inc(sem("nodes_turned"), 1)

        def turn_nodes_act(act, kind, to, tag):
            b = turns_before(kind, tag)
            for k, (t0, m) in enumerate(CH):
                act.wait_ge(sem("nodes_turned"), b + k + 1)
                act.activation(to[0:64, t0:t0 + m, :],
                               ps[7 * (k % 2)][0:64, 0:NP * m].rearrange("p (t n) -> p t n", n=NP), ACT.Copy) \
                    .then_inc(sem("nodes_kept"), 1)

        def tables_pe(pe, kind, x, to):
            pe.wait_ge(sem(f"{kind}_features"), 1)
            turn_nodes_pe(pe, kind, x, "x")
            pe.wait_ge(sem("nodes_kept"), turns_before(kind, "x") + len(CH))
            w = wc[kind]
            for t in range(NT):
                if t >= 2:
                    pe.wait_ge(sem("tabled"), NT * order(kind) + t - 1)
                pe.matmul(ps[5 + t % 2][0:NP, 0:w.shape[1]], to[:, t, :], w[:, :], start=True, stop=True) \
                    .then_inc(sem("multiplied"), 1)

        def tables_dve(dve, kind):
            w = wc[kind].shape[1]
            for t in range(NT):
                dve.wait_ge(sem("multiplied"), NT * order(kind) + t + 1)
                out = ps[5 + t % 2][0:NP, :]
                dve.tensor_copy(TT[0:NP, t, 0:128].rearrange("p (f h) -> p h f", h=2),
                                out[:, 0:128].rearrange("p (h f) -> p h f", h=2))
                dve.tensor_copy(TT[0:NP, t, 128:w], out[:, 128:w]).then_inc(sem("tabled"), 1)

        def layer_norm(c, dve, kind, x):
            c(dve.tensor_reduce(st1[0][:, :], x[:, :, :], AX, ALU.add))
            c(dve.tensor_scalar(st1[0][:, :], st1[0][:, :], -1.0 / D, None, ALU.mult))
            c(dve.tensor_tensor(x[:, :, :], x[:, :, :], bc(st1[0][:, :]), ALU.add))
            c(dve.tensor_tensor(tmp[0][:, :, :], x[:, :, :], x[:, :, :], ALU.mult))
            c(dve.tensor_reduce(st1[0][:, :], tmp[0][:, :, :], AX, ALU.add))
            c(dve.tensor_scalar(st1[0][:, :], st1[0][:, :], 1.0 / D, EPS, ALU.mult, ALU.add))
            dve.sem_inc(sem("variances"), 1)
            dve.wait_ge(sem("deviations"), NORMS.index(kind) + 1)
            c(dve.reciprocal(st1[1][:, :], st1[1][:, :]))
            c(dve.tensor_tensor(x[:, :, :], x[:, :, :], bc(st1[1][:, :]), ALU.mult))

        def sqrt_act(act, kind, tag):
            if tag == "std":
                act.wait_ge(sem("variances"), NORMS.index(kind) + 1)
            else:
                act.wait_ge(sem("squared_norms"), 1)
            act.activation(st1[1][:, :], st1[0][:, :], ACT.Sqrt) \
                .then_inc(sem("deviations" if tag == "std" else "norms"), 1)

        def divide(c, dve, kind, out):
            dve.wait_ge(sem("taken"), 16 * NT * (order(kind) + 1))
            c(dve.reciprocal(out[:, :, :], R[:, :, 64:128]))
            c(dve.tensor_tensor(out[:, :, :], out[:, :, :], R[:, :, 0:64], ALU.mult))
            c(dve.tensor_tensor(out[:, :, :], out[:, :, :], bc(has[:, :]), ALU.mult))

        def add_self_loops(c, dve, kind):
            pairs = lambda t: t.rearrange("p t (i k) -> p t i k", k=2)
            packed = pairs(R[:, :, 64:128])
            own = pairs(TT[0:NP, :, 0:128])
            logit, value = own[:, :, :, 0], own[:, :, :, 1]
            s0, top = tmp[0], tmp[1]
            dve.wait_ge(sem("taken"), 16 * NT * (order(kind) + 1))
            c(dve.tensor_tensor(s0[:, :, :], logit, TT[0:NP, :, 128:192], ALU.add))
            c(dve.scalar_tensor_tensor(flat(s0[:, :, :]), flat(s0[:, :, :]), 0.2, flat(s0[:, :, :]),
                                       ALU.mult, ALU.max))
            for k in range(2):
                c(dve.tensor_tensor(pairs(SK[:, :, :])[:, :, :, k], packed[:, :, :, 1],
                                    has[:, :].unsqueeze(2).to_broadcast([NP, NT, 32]), ALU.mult))
            c(dve.tensor_scalar(st1[0][:, :], has[:, :], -1.0, BIG, ALU.add, ALU.mult))
            c(dve.tensor_tensor(SK[:, :, :], SK[:, :, :], bc(st1[0][:, :]), ALU.add))
            c(dve.tensor_tensor(top[:, :, :], SK[:, :, :], s0[:, :, :], ALU.max))
            c(dve.tensor_tensor(s0[:, :, :], s0[:, :, :], top[:, :, :], ALU.subtract))
            c(dve.tensor_tensor(SK[:, :, :], SK[:, :, :], top[:, :, :], ALU.subtract))
            dve.sem_inc(sem("loop_args"), 1)
            dve.wait_ge(sem("loop_exps"), 2 * (order(kind) + 1))
            for k in range(2):
                c(dve.tensor_tensor(pairs(H[:, :, :])[:, :, :, k], packed[:, :, :, 0],
                                    pairs(SK[:, :, :])[:, :, :, k], ALU.mult))
            c(dve.tensor_tensor(H[:, :, :], H[:, :, :], s0[:, :, :], ALU.add))
            c(dve.tensor_scalar(H[:, :, :], H[:, :, :], 1e-16, None, ALU.add))
            c(dve.reciprocal(H[:, :, :], H[:, :, :]))
            c(dve.tensor_tensor(SK[:, :, :], SK[:, :, :], R[:, :, 0:64], ALU.mult))
            c(dve.tensor_tensor(s0[:, :, :], s0[:, :, :], value, ALU.mult))
            c(dve.tensor_tensor(SK[:, :, :], SK[:, :, :], s0[:, :, :], ALU.add))
            c(dve.tensor_tensor(H[:, :, :], H[:, :, :], SK[:, :, :], ALU.mult))

        def post_dve(dve, kind):
            c = dve_chain(dve)
            nxt = KINDS[KINDS.index(kind) + 1] if kind != "gc2" else "out"
            if kind == "gat1":
                add_self_loops(c, dve, kind)
                c(dve.tensor_tensor(H[:, :, :], H[:, :, :],
                                    bias[:, 0:1, :].to_broadcast([NP, NT, 64]), ALU.add))
                c(dve.tensor_scalar(tmp[0][:, :, :], H[:, :, :], 0.0, None, ALU.min))
                dve.sem_inc(sem("elu_arg"), 1)
                dve.wait_ge(sem("elu_exp"), 1)
                c(dve.tensor_scalar(tmp[1][:, :, :], tmp[1][:, :, :], -1.0, None, ALU.add))
                c(dve.scalar_tensor_tensor(flat(H[:, :, :]), flat(H[:, :, :]), 0.0, flat(tmp[1][:, :, :]),
                                           ALU.max, ALU.add))
            elif kind == "gat2":
                add_self_loops(c, dve, kind)
                c(dve.tensor_tensor(H[:, :, :], H[:, :, :],
                                    bias[:, 1:2, :].to_broadcast([NP, NT, 64]), ALU.add))
                c(dve.tensor_tensor(tmp[0][:, :, :], H[:, :, :], H[:, :, :], ALU.mult))
                c(dve.tensor_reduce(st1[0][:, :], tmp[0][:, :, :], AX, ALU.add))
                dve.sem_inc(sem("squared_norms"), 1)
                dve.wait_ge(sem("norms"), 1)
                c(dve.tensor_scalar(st1[1][:, :], st1[1][:, :], 1e-12, None, ALU.max))
                c(dve.reciprocal(st1[1][:, :], st1[1][:, :]))
                c(dve.tensor_tensor(H[:, :, :], H[:, :, :], bc(st1[1][:, :]), ALU.mult))
                c(dve.tensor_tensor(X[:, :, :], X[:, :, :], H[:, :, :], ALU.add))
                layer_norm(c, dve, kind, X)
            elif kind in ("tc1", "tc2"):
                divide(c, dve, kind, H)
                c(dve.tensor_tensor(H[:, :, :], H[:, :, :], TT[0:NP, :, 192:256], ALU.add))
                c(dve.tensor_scalar(H[:, :, :], H[:, :, :], 0.0, None, ALU.max))
                if kind == "tc2":
                    dve.sem_inc(sem("h2_ready"), 1)
                    for t in range(NT):
                        dve.wait_ge(sem("skipped"), t + 1)
                        dve.scalar_tensor_tensor(X[:, t, :], ps[5 + t % 2][0:NP, 0:64], 0.0, X[:, t, :],
                                                 ALU.max, ALU.add).then_inc(sem("skip_added"), 1)
                    dve.wait_ge(sem("skip_added"), NT)
                    layer_norm(c, dve, kind, X)
            elif kind == "pt":
                divide(c, dve, kind, H)
                c(dve.tensor_tensor(X[:, :, :], X[:, :, :], H[:, :, :], ALU.add))
                layer_norm(c, dve, kind, X)
                c(dve.tensor_tensor(SK[:, :, :], X[:, :, :], bc(dinv[:, :]), ALU.mult))
            else:
                dve.wait_ge(sem("taken"), 16 * NT * (order(kind) + 1))
                c(dve.tensor_tensor(H[:, :, :] if kind == "gc1" else tmp[1][:, :, :], R3,
                                    bc(dinv[:, :]), ALU.mult))
                if kind == "gc1":
                    c(dve.tensor_tensor(SK[:, :, :], H[:, :, :], bc(dinv[:, :]), ALU.mult))
                else:
                    c(dve.tensor_tensor(H[:, :, :], H[:, :, :], X[:, :, :], ALU.add))
                    c(dve.tensor_tensor(H[:, :, :], H[:, :, :], tmp[1][:, :, :], ALU.add))
                    c(dve.scalar_tensor_tensor(flat(X[:, :, :]), flat(H[:, :, :]), 1.0 / 3.0,
                                               flat(X[:, :, :]), ALU.mult, ALU.add))
                    layer_norm(c, dve, kind, X)
            dve.sem_inc(sem(f"{nxt}_features"), 1)

        def post_act(act, kind):
            if kind.startswith("gat"):
                act.wait_ge(sem("loop_args"), order(kind) + 1)
                for t in (tmp[0], SK):
                    act.activation(t[:, :, :], t[:, :, :], ACT.Exp).then_inc(sem("loop_exps"), 1)
            if kind == "gat1":
                act.wait_ge(sem("elu_arg"), 1)
                act.activation(tmp[1][:, :, :], tmp[0][:, :, :], ACT.Exp).then_inc(sem("elu_exp"), 1)
            if kind == "gat2":
                sqrt_act(act, kind, "norm")
            if kind == "tc2":
                turn_nodes_act(act, kind, xT, "h2")
            if kind in ("gat2", "tc2", "pt", "gc2"):
                sqrt_act(act, kind, "std")

        def post_pe(pe, kind):
            if kind != "tc2":
                return
            pe.wait_ge(sem("h2_ready"), 1)
            turn_nodes_pe(pe, kind, H, "h2")
            pe.wait_ge(sem("nodes_kept"), turns_before(kind, "h2") + len(CH))
            for t in range(NT):
                if t >= 2:
                    pe.wait_ge(sem("skip_added"), t - 1)
                out = ps[5 + t % 2][0:NP, 0:64]
                pe.matmul(out, h1T[0:64, t, :], skw[0:64, 0, :], start=True, stop=False)
                pe.matmul(out, xT[:, t, :], skw[:, 1, :], start=False, stop=True).then_inc(sem("skipped"), 1)

        node_in = {"gat1": (X, xT), "gat2": (H, xT), "tc1": (X, xT), "tc2": (H, h1T), "pt": (X, xT)}

        Q = 3
        mu, mv = [ps[0], ps[1], ps[2]], [ps[3], ps[4], ps[5]]
        msq = [num[0], num[1], den[0]]
        mvar = [ex[0], ex[1], den[1]]
        mh = [sr, sl, pv]
        mx = [ea[0], ea[1], arg[0]]

        def mlp_sp(sp):
            def step(it):
                if not isinstance(it, int):
                    sp.wait_ge(sem("mlp_first"), Q * it)
                for q in range(Q):
                    sp.dma_start(mx[q][0:6, 0:W], a["ea3"][ds(Q * it + q, 1), :, :].rearrange("a p j -> p (a j)")) \
                        .then_inc(sem(f"mlp_in{q}"), 16)
            sp.wait_ge(sem("mlp_ones"), 3)
            step(0)
            with sp.Fori(1, G // Q) as it:
                step(it)

        def mlp_pe(pe):
            pe.wait_ge(sem("mlp_ready"), 1)

            def step(it):
                n = Q * it
                for q in range(Q):
                    pe.wait_ge(sem(f"mlp_in{q}"), 16 * (it + 1))
                    if not isinstance(it, int):
                        pe.wait_ge(sem("mlp_scaled"), 2 * n - Q + q + 1)
                    pe.matmul(mu[q][:, :], wd1[:, :], mx[q][0:7, 0:W], start=True, stop=True) \
                        .then_inc(sem("mlp_first"), 1)
                for q in range(Q):
                    pe.wait_ge(sem("mlp_squared"), 2 * n + q + 1)
                    pe.matmul(mv[q][:, :], bones, msq[q][:, :], start=True, stop=True) \
                        .then_inc(sem("mlp_vars"), 1)
                for q in range(Q):
                    pe.wait_ge(sem("mlp_gelus"), 2 * n + q + 1)
                    pe.matmul(mu[q][:, :], wd2[:, :], mh[q][:, :], start=True, stop=True) \
                        .then_inc(sem("mlp_second"), 1)
                for q in range(Q):
                    pe.wait_ge(sem("mlp_squared"), 2 * n + Q + q + 1)
                    pe.matmul(mv[q][:, :], bones, msq[q][:, :], start=True, stop=True) \
                        .then_inc(sem("mlp_vars"), 1)

            step(0)
            with pe.Fori(1, G // Q) as it:
                step(it)

        def mlp_act(act):
            act.wait_ge(sem("mlp_ready"), 1)

            def half(it, k):
                n = 2 * Q * it + k * Q
                for q in range(Q):
                    act.wait_ge(sem("mlp_second" if k else "mlp_first"), Q * it + q + 1)
                    if k:
                        act.activation(msq[q][:, :], mu[q][:, :], ACT.Square, bias=pv4[:, 2:3]) \
                            .then_inc(sem("mlp_squared"), 1)
                    else:
                        act.activation(msq[q][:, :], mu[q][:, :], ACT.Square).then_inc(sem("mlp_squared"), 1)
                for q in range(Q):
                    act.wait_ge(sem("mlp_vars"), n + q + 1)
                    act.activation(mvar[q][:, :], mv[q][:, :], ACT.Sqrt, scale=1.0 / D, bias=epsc[:, :]) \
                        .then_inc(sem("mlp_std"), 1)
                for q in range(Q):
                    act.wait_ge(sem("mlp_scaled"), n + q + 1)
                    if not k and not isinstance(it, int):
                        act.wait_ge(sem(f"mlp_stored{q}"), 16 * it)
                    act.activation(mh[q][:, :], mvar[q][:, :], ACT.Gelu, scale=pv4[:, 3 * k:3 * k + 1],
                                   bias=pv4[:, 1 + 3 * k:2 + 3 * k]).then_inc(sem("mlp_gelus"), 1)
                    if k:
                        act.wait_ge(sem("mlp_gelus"), n + q + 1)
                        act.dma_start(dist[ds(Q * it + q, 1), :, :].rearrange("a p j -> p (a j)"), mh[q][:, :]) \
                            .then_inc(sem(f"mlp_stored{q}"), 16)

            half(0, 0)
            half(0, 1)
            with act.Fori(1, G // Q) as it:
                half(it, 0)
                half(it, 1)

        def mlp_dve(dve):
            def half(it, k):
                n = 2 * Q * it + k * Q
                for q in range(Q):
                    dve.wait_ge(sem("mlp_std"), n + q + 1)
                    dve.reciprocal(mvar[q][:, :], mvar[q][:, :]).then_inc(sem("mlp_rstd"), 1)
                    dve.wait_ge(sem("mlp_rstd"), n + q + 1)
                    if k:
                        dve.scalar_tensor_tensor(mvar[q][:, :], mu[q][:, :], pv4[:, 2:3], mvar[q][:, :],
                                                 ALU.add, ALU.mult).then_inc(sem("mlp_scaled"), 1)
                    else:
                        dve.tensor_tensor(mvar[q][:, :], mu[q][:, :], mvar[q][:, :], ALU.mult) \
                            .then_inc(sem("mlp_scaled"), 1)
            half(0, 0)
            half(0, 1)
            with dve.Fori(1, G // Q) as it:
                half(it, 0)
                half(it, 1)
            for q in range(Q):
                dve.wait_ge(sem(f"mlp_stored{q}"), 16 * (G // Q))

        DI = TT[:, :, :].rearrange("p t c -> p (t c)").bitcast(i32)
        cur, prv = DI[0:G, 0:2 * W], DI[0:G, 2 * W:4 * W]
        heads_i = DI[0:NP, 4 * W:4 * W + TILES]
        heads = SK[:, :, :].rearrange("p t c -> p (t c)")[:, 0:TILES]
        ZC = 3072
        zeros = arg
        less = R[:, :, :].rearrange("p t c -> p (t c)")
        rows_i = R[:, :, :].bitcast(i32)
        fbuf = O[0][0:G, :, :, :].rearrange("p c j f -> p (c j f)").bitcast(bf16)

        def setup_sp(sp):
            n = [0]

            def load(dst, src, name="setup_loaded"):
                n[0] += 16
                sp.dma_start(dst, src).then_inc(sem(name), 16)

            sp.wait_ge(sem("cleared"), 1)
            load(cst[:, :], a["consts"][:, :])
            d = a["dst_s"]
            for c in range(2):
                load(cur[:, W * c:W * c + W], d[c, 1:S + 1].rearrange("(g w) -> g w", w=W))
                load(prv[:, W * c:W * c + W], d[c, 0:S].rearrange("(g w) -> g w", w=W))
            load(heads_i, a["heads"].unsqueeze(0).to_broadcast([NP, TILES]))
            load(midd[:, :], a["mid"].unsqueeze(0).to_broadcast([64, 2]))
            load(X[:, :, :], a["x"].rearrange("(p t) c -> p t c", t=NT))
            load(wT[:, 0, :], a["w1t"][:, :])
            load(wT[:, 1, :], a["w2t"][:, :])
            col = lambda v: v.rearrange("(f a) -> f a", a=1)
            row = lambda v: v.rearrange("(a f) -> a f", a=1)
            for k, v in enumerate(["L0_gnn_a_src1", "L0_gnn_a_dst1", "L0_gnn_a_src2", "L0_gnn_a_dst2"]):
                load(avec[:, k:k + 1], col(a[v].rearrange("h c -> (h c)")))
            for k in (1, 2):
                w = wc[f"tc{k}"]
                for i, q in enumerate("kvqs"):
                    load(w[0:64, 64 * i:64 * i + 64], a[f"L1_gnn_{q}{k}_w"][:, :])
                    load(w[64:65, 64 * i:64 * i + 64], row(a[f"L1_gnn_{q}{k}_b"]))
                for c in range(2):
                    load(we[k - 1][DE * c:DE * c + DE, 64 * c:64 * c + 64], a[f"L1_gnn_e{k}_w"][:, :])
                load(bias[:, k - 1, :], a[f"L0_gnn_b{k}"].unsqueeze(0).to_broadcast([NP, 64]))
            load(skw[0:64, 0, :], a["L1_gnn_skip_w"][0:64, :])
            load(skw[0:64, 1, :], a["L1_gnn_skip_w"][64:128, :])
            load(skw[64:65, 1, :], row(a["L1_gnn_skip_b"]))
            for i, q in enumerate(["W2", "W3", "W1"]):
                load(wc["pt"][0:64, 64 * i:64 * i + 64], a[f"L2_gnn_{q}"][:, :])
            for c in range(2):
                load(wd1[3 * c:3 * c + 3, 64 * c:64 * c + 64], a["L2_gnn_Wd1"][:, :])
                load(wd1[6:7, 64 * c:64 * c + 64], row(a["L2_gnn_bd1"]))
                load(wd2[64 * c:64 * c + 64, 64 * c:64 * c + 64], a["L2_gnn_Wd2"][:, :])
                for i, q in enumerate(["g1", "b1", None, "g2", "b2"]):
                    if q:
                        load(pv4[64 * c:64 * c + 64, i:i + 1], col(a[f"L2_gnn_{q}"]))
                load(bd2row[:, 64 * c:64 * c + 64], row(a["L2_gnn_bd2"]))
            assert n[0] == 16 * LOADS, n[0] // 16
            sv = spread.rearrange("e f -> (e f)").rearrange("(p k z) -> p k z", p=128, z=2 * W)
            for k in range(EP * 64 // 128 // (2 * W)):
                sp.dma_start(sv[:, k, :], arg[1][:, :]).then_inc(sem("spread_zero"), 16)
            sp.wait_ge(sem("flags_made"), 1)
            for c in range(2):
                sp.dma_start(flags[:, c, :], fbuf[:, 2 * W * c:2 * W * c + 2 * W]).then_inc(sem("flags_out"), 16)
            sp.wait_ge(sem("starts_made"), 1)
            sp.dma_start(starts_d[0:N].rearrange("(p t) -> p t", t=NT), starts[:, :]).then_inc(sem("starts_out"), 16)
            sp.dma_start(starts_d[N:N + 1].unsqueeze(0), ecol[:, :]).then_inc(sem("starts_out"), 16)
            sp.wait_ge(sem("starts_out"), 32)
            sp.dma_start(endsn[:, :], starts_d[1:N + 1].rearrange("(p t) -> p t", t=NT)).then_inc(sem("ends_in"), 16)
            sp.wait_ge(sem("flags_out"), 32)
            sp.wait_ge(sem("spread_zero"), 16 * (EP * 64 // 128 // (2 * W)))

        LOADS = 5 + 1 + 1 + 2 + 1 + 4 + 2 * (8 + 2 + 1) + 3 + 3 + 2 * (1 + 1 + 1 + 4 + 1)
        bd2row = sb("bd2row", [1, 128])
        ecol = sb("ecol", [1, 1])

        def setup_pool(pool):
            pool.wait_ge(sem("tile_index"), 1)
            for t in range(NT):
                pool.indirect_dma_start(out=rows_i[:, t, :], out_offset=None, in_=a["dst_rows"][:, :],
                                        in_offset=on_axis0(idx_t[:, t:t + 1])).then_inc(sem("rows_in"), 16)

        def setup_pe(pe):
            pe.wait_ge(sem("amat_made"), 1)
            for k in range(2):
                pe.matmul(ps[6][0:64, 192 * k:192 * k + 192], wT[:, k, :], amat[:, k, :], start=True, stop=True) \
                    .then_inc(sem("gat_weights"), 1)
            pe.matmul(ps[7][:, 0:1], bd2row[:, :], cst[0:1, CI:CI + 1], start=True, stop=True) \
                .then_inc(sem("bd2_turned"), 1)

        def setup_dve(dve):
            c = dve_chain(dve)
            for t in (xT, h1T):
                dve.memset(t[64:65, :, :], 1.0)
            for t in mx:
                dve.memset(t[0:32, 0:W], 1.0)
            for t in (we[0], we[1], wd1, wd2):
                dve.memset(t[:, :], 0.0)
            for w in (wc["gat1"], wc["gat2"], wc["pt"]):
                dve.memset(w[64:65, :], 0.0)
            dve.memset(ecol[:, :], float(E))
            for s in (ex[1], num[1], den[1], M[1]):
                dve.memset(s[:, :], 0.0)
            dve.memset(mg[:, :], 0.0)
            dve.memset(epsc[:, :], EPS)
            c(dve.memset(arg[1][:, :], 0.0))
            dve.sem_inc(sem("cleared"), 1)
            dve.sem_inc(sem("mlp_ones"), 3)
            dve.wait_ge(sem("setup_loaded"), 16 * LOADS)
            for k in range(2):
                c(dve.tensor_copy(amat[:, k, 64:128], ident[0:64, 0:64]))
                for i in range(2):
                    block = amat[:, k, 128 * i:128 * i + 64]
                    mask = bones[0:64, 0:64] if k else hmask
                    c(dve.tensor_scalar(block, mask, avec[:, 2 * k + i:2 * k + i + 1], None, ALU.mult))
            c(dve.tensor_reduce(parity[:, 0:1], even[0:64, :], AX, ALU.add))
            c(dve.tensor_reduce(parity[:, 1:2], odd[0:64, :], AX, ALU.add))
            for t, p in ((wd1, 7), (wd2, 128), (bd2row, 1)):
                v = t[:, :].rearrange("p (c f) -> p c f", c=2)
                c(dve.tensor_reduce(mcol[0:p, :], v, AX, ALU.add))
                c(dve.tensor_scalar(mcol[0:p, :], mcol[0:p, :], -1.0 / D, None, ALU.mult))
                c(dve.tensor_tensor(v, v, mcol[0:p, :].unsqueeze(2).to_broadcast([p, 2, 64]), ALU.add))
            c(dve.tensor_scalar(wc["pt"][0:64, 0:64], wc["pt"][0:64, 0:64], -1.0, None, ALU.mult))
            dve.sem_inc(sem("amat_made"), 1)
            for k in range(2):
                dve.wait_ge(sem("gat_weights"), 2)
                c(dve.tensor_copy(wc[f"gat{k + 1}"][0:64, :], ps[6][0:64, 192 * k:192 * k + 192]))
            dve.wait_ge(sem("bd2_turned"), 1)
            c(dve.tensor_copy(pv4[:, 2:3], ps[7][:, 0:1]))
            dve.sem_inc(sem("mlp_ready"), 2)
            for k in range(2):
                f = fbuf[:, 2 * W * k:2 * W * k + 2 * W]
                c(dve.tensor_tensor(f[:, 0:W], cur[:, W * k:W * k + W], prv[:, W * k:W * k + W], ALU.is_equal))
                c(dve.tensor_scalar(f[:, W:2 * W], f[:, 0:W], -1.0, BIG, ALU.add, ALU.mult))
            dve.sem_inc(sem("flags_made"), 1)
            c(dve.tensor_tensor(cross[:, :], midd[:, 0:1], midd[:, 1:2], ALU.is_equal))
            c(dve.tensor_scalar(crossb[:, :], cross[:, :], -1.0, BIG, ALU.add, ALU.mult))
            c(dve.tensor_copy(heads, heads_i))
            for t in range(NT):
                c(dve.tensor_scalar(less[:, 0:TILES], heads, nid[:, t:t + 1], None, ALU.is_lt))
                c(dve.tensor_reduce(st1[0][:, t:t + 1], less[:, 0:TILES], AX, ALU.add))
            c(dve.tensor_scalar(st1[0][:, :], st1[0][:, :], -1.0, 0.0, ALU.add, ALU.max))
            c(dve.tensor_copy(idx_t[:, :], st1[0][:, :]))
            dve.sem_inc(sem("tile_index"), 1)
            dve.wait_ge(sem("rows_in"), 16 * NT)
            c(dve.tensor_copy(R[:, :, :], rows_i))
            c(dve.tensor_tensor(R[:, :, :], R[:, :, :], nid.unsqueeze(2).to_broadcast([NP, NT, 128]), ALU.is_lt))
            c(dve.tensor_reduce(starts[:, :], R[:, :, :], AX, ALU.add))
            c(dve.scalar_tensor_tensor(starts[:, :], st1[0][:, :], float(T), starts[:, :], ALU.mult, ALU.add))
            dve.sem_inc(sem("starts_made"), 1)
            dve.wait_ge(sem("ends_in"), 16)
            deg, t1, t2 = st1[1], st1[2], st1[3]
            c(dve.tensor_tensor(deg[:, :], endsn[:, :], starts[:, :], ALU.subtract))
            c(dve.tensor_scalar(has[:, :], deg[:, :], 0.0, None, ALU.is_gt))
            c(dve.tensor_scalar(st1[0][:, :], deg[:, :], 1.0, None, ALU.max))
            dve.sem_inc(sem("degrees"), 1)
            dve.wait_ge(sem("degree_root"), 1)
            c(dve.reciprocal(dinv[:, :], dinv[:, :]))
            c(dve.tensor_tensor(dinv[:, :], dinv[:, :], has[:, :], ALU.mult))
            c(dve.tensor_scalar(t1[:, :], endsn[:, :], -1.0, 0.0, ALU.add, ALU.max))
            c(dve.tensor_scalar(t1[:, :], t1[:, :], float(S - 1), None, ALU.min))
            c(dve.tensor_scalar(t2[:, :], starts[:, :], -1.0, float(3 * S - 1), ALU.mult, ALU.add))
            in_b = deg
            c(dve.tensor_scalar(in_b[:, :], starts[:, :], float(S), None, ALU.is_ge))
            c(dve.tensor_tensor(t2[:, :], t2[:, :], t1[:, :], ALU.subtract))
            c(dve.tensor_tensor(t2[:, :], t2[:, :], in_b[:, :], ALU.mult))
            c(dve.tensor_tensor(t1[:, :], t1[:, :], t2[:, :], ALU.add))
            c(dve.tensor_copy(idx_end[:, :], t1[:, :]))
            def place(out, value, keep):
                c(dve.tensor_tensor(keep, keep, has[:, :], ALU.mult))
                c(dve.tensor_scalar(value, value, -OOB, None, ALU.add))
                c(dve.tensor_tensor(value, value, keep, ALU.mult))
                c(dve.tensor_scalar(value, value, OOB, None, ALU.add))
                c(dve.tensor_copy(out[:, :], value))
            c(dve.tensor_copy(t1[:, :], starts[:, :]))
            c(dve.tensor_scalar(t2[:, :], starts[:, :], float(S), None, ALU.is_lt))
            place(idx_a, t1[:, :], t2[:, :])
            c(dve.tensor_scalar(t1[:, :], endsn[:, :], -1.0, float(3 * S), ALU.mult, ALU.add))
            c(dve.tensor_scalar(t2[:, :], endsn[:, :], float(S), None, ALU.is_gt))
            place(idx_b, t1[:, :], t2[:, :])
            dve.sem_inc(sem("gat1_features"), 2)

        def setup_act(act):
            act.wait_ge(sem("degrees"), 1)
            act.activation(dinv[:, :], st1[0][:, :], ACT.Sqrt).then_inc(sem("degree_root"), 1)

        block = ctx.enter_context(nc.Block())

        @block.sync
        def _(sp):
            setup_sp(sp)
            mlp_sp(sp)
            for kind in KINDS:
                if kind in SOFT:
                    tables_sp(sp, kind)
                else:
                    sp.wait_ge(sem(f"{kind}_features"), 1)
                    sp.dma_start(table3.rearrange("(p t) c -> p t c", t=NT), SK[:, :, :]) \
                        .then_inc(sem("tables_written"), 16)
                if kind == "pt":
                    for q in range(Q):
                        sp.wait_ge(sem(f"mlp_stored{q}"), 16 * (G // Q))
                pass_sp(sp, kind)
                merge_sp(sp, kind)
            sp.wait_ge(sem("out_features"), 1)
            sp.dma_start(a["out"].rearrange("(p t) c -> p t c", t=NT), X[:, :, :]).then_inc(sem("written"), 16)
            sp.wait_ge(sem("written"), 16)

        @block.gpsimd
        def _(pool):
            setup_pool(pool)
            pool.wait_ge(sem("gat1_features"), 2)
            pool.wait_ge(sem("spread_zero"), 16 * (EP * 64 // 128 // (2 * W)))
            for kind in KINDS:
                if kind in SOFT:
                    scatter_pool(pool, kind)
                pass_pool(pool, kind)
                take_pool(pool, kind)

        @block.tensor
        def _(pe):
            setup_pe(pe)
            mlp_pe(pe)
            pe.wait_ge(sem("mlp_scaled"), 2 * G)
            for kind in KINDS:
                if kind in SOFT:
                    tables_pe(pe, kind, *node_in[kind])
                pass_pe(pe, kind)
                post_pe(pe, kind)

        @block.vector
        def _(dve):
            setup_dve(dve)
            mlp_dve(dve)
            for kind in KINDS:
                if kind in SOFT:
                    tables_dve(dve, kind)
                pass_dve(dve, kind)
                post_dve(dve, kind)

        @block.scalar
        def _(act):
            setup_act(act)
            mlp_act(act)
            for kind in KINDS:
                if kind in SOFT:
                    turn_nodes_act(act, kind, node_in[kind][1], "x")
                pass_act(act, kind)
                post_act(act, kind)


WEIGHTS = (["L0_gnn_" + w for w in ("a_src1", "a_dst1", "b1", "a_src2", "a_dst2", "b2")]
           + [f"L1_gnn_{w}{k}_{p}" for k in (1, 2) for w in "qkvs" for p in "wb"]
           + ["L1_gnn_e1_w", "L1_gnn_e2_w", "L1_gnn_skip_w", "L1_gnn_skip_b"]
           + ["L2_gnn_" + w for w in ("Wd1", "bd1", "g1", "b1", "Wd2", "bd2", "g2", "b2", "W1", "W2", "W3")])


def lay_out(inputs):
    f = {k: np.asarray(v) for k, v in inputs.items()}

    def streams(v, pad):
        v = np.concatenate([v, np.full((EP - E,) + v.shape[1:], pad, v.dtype)])
        return np.stack([v[:S], v[S:][::-1]])

    src = streams(f["src"], 0).reshape(2, G, J, T)
    dst = np.concatenate([f["dst"], np.full(EP - E, N, f["dst"].dtype)])
    both = streams(f["dst"], N)
    arrays = {
        "x": f["x"],
        "consts": shape_constants(),
        "src_g": np.ascontiguousarray(src.transpose(1, 3, 0, 2).reshape(G, T, 2 * J)),
        "dst_s": np.ascontiguousarray(np.concatenate([np.full((2, 1), -1, both.dtype), both], 1)),
        "dst_rows": dst.reshape(TILES, T),
        "heads": np.ascontiguousarray(dst[::T]),
        "mid": np.ascontiguousarray(dst[S - 1:S + 1]),
        "w1t": np.ascontiguousarray(f["L0_gnn_W1"].T),
        "w2t": np.ascontiguousarray(f["L0_gnn_W2"].T),
    }
    for name, key, k in (("ea32", "edge_attr_32", DE), ("ea3", "edge_attr_3", 3)):
        v = streams(f[key], 0).reshape(2, G, W, k)
        arrays[name] = np.ascontiguousarray(v.transpose(1, 0, 3, 2).reshape(G, 2 * k, W))
    for w in WEIGHTS:
        arrays[w] = f[w]
    return arrays


def kernel(**inputs):
    import concourse.bacc as bacc
    from concourse.bass_utils import run_bass_kernel_spmd

    nc = bacc.Bacc("TRN2", target_bir_lowering=False, num_devices=1)
    arrays = lay_out(inputs)
    a, feeds = {}, {}
    for name, v in arrays.items():
        feeds[f"in_{name}"] = v
        a[name] = nc.dram_tensor(f"in_{name}", v.shape, mybir.dt.from_np(v.dtype), kind="ExternalInput").ap()
    a["out"] = nc.dram_tensor("out_0", (N, D), mybir.dt.float32, kind="ExternalOutput").ap()
    build(nc, a)
    r = run_bass_kernel_spmd(nc, [feeds], core_ids=[0])
    return r.results[0]["out_0"]
```

```python
import numpy as np
import concourse.bass as bass
from concourse import mybir
from contextlib import ExitStack

N, E, D = 3125, 103125, 64
NP, NT = 125, 25
T = 128
J = 4
W = J * T
G = 102
U = 3
assert G % U == 0
S = G * W
EP = 2 * S
TILES = EP // T
BIG = 1.0e30
OOB = 1.0e6
EPS = 1e-5
DE = 32

KINDS = ["gat1", "gat2", "tc1", "tc2", "pt", "gc1", "gc2"]

CI, CB, CM, CN = 0, 128, 256, 320
CE, CO = CN + NT, CN + NT + 128
CW = CO + 128


def shape_constants():
    c = np.zeros((128, CW), np.float32)
    c[:, CI:CI + 128] = np.eye(128)
    c[:64, CB:CB + 64] = 1
    c[64:, CB + 64:CB + 128] = 1
    for k in range(2):
        c[k::2, CE + 128 * k:CE + 128 * k + 128] = np.eye(128)[k::2]
    f = np.arange(64)
    c[:64, CM:CM + 64] = f[:, None] // 16 == f[None, :] // 16
    c[:NP, CN:CN + NT] = np.arange(N).reshape(NP, NT)
    return c


def build(nc, a):
    f32, bf16, i32 = mybir.dt.float32, mybir.dt.bfloat16, mybir.dt.int32
    ALU, ACT, AX = mybir.AluOpType, mybir.ActivationFunctionType, mybir.AxisListType.X
    ds = bass.ds
    on_axis0 = lambda ap: bass.IndirectOffsetOnAxis(ap=ap, axis=0)
    ctx = ExitStack()

    def sb(name, shape, dt=f32):
        return ctx.enter_context(nc.sbuf_tensor(name, shape, dt))

    def dram(name, shape, dt=f32):
        return nc.dram_tensor(name, shape, dt, kind="Internal").ap()

    sems = {}

    def sem(name):
        if name not in sems:
            sems[name] = ctx.enter_context(nc.semaphore(name))
        return sems[name]

    def need(eng, name, value):
        if not isinstance(value, int) or value > 0:
            eng.wait_ge(sem(name), value)

    with ctx:
        table = dram("table", [N, 128])
        table3 = dram("table3", [N, 64])
        spread = dram("spread", [EP, 64])
        flags = dram("flags", [G, 2, 2 * W], bf16)
        ends = dram("ends", [EP, 128])
        ends3 = dram("ends3", [EP, 64])
        dist = dram("dist", [G, 128, W])
        starts_d = dram("starts_d", [N + 1])

        cst = sb("cst", [128, CW])
        ident, bones = cst[:, CI:CI + 128], cst[:, CB:CB + 128]
        bones8 = sb("bones8", [128, 128])
        hmask, nid = cst[0:64, CM:CM + 64], cst[0:NP, CN:CN + NT]
        even, odd = cst[:, CE:CE + 128], cst[:, CO:CO + 128]
        X = sb("X", [NP, NT, D])
        H = sb("H", [NP, NT, D])
        SK = sb("SK", [NP, NT, D])
        tmp = [sb(f"tmp{i}", [NP, NT, D]) for i in range(2)]
        TT = sb("TT", [128, NT, 256])
        R = sb("R", [NP, NT, 128])
        R3 = R[:, :, 0:64]
        xT = sb("xT", [65, NT, NP])
        h1T = sb("h1T", [65, NT, NP])
        starts = sb("starts", [NP, NT])
        endsn = sb("endsn", [NP, NT])
        has = sb("has", [NP, NT])
        dinv = sb("dinv", [NP, NT])
        st1 = [sb(f"st{i}", [NP, NT]) for i in range(4)]
        idx_end = sb("idx_end", [NP, NT], i32)
        idx_a = sb("idx_a", [NP, NT], i32)
        idx_b = sb("idx_b", [NP, NT], i32)
        idx_t = sb("idx_t", [NP, NT], i32)
        midd = sb("midd", [64, 2], i32)
        cross = sb("cross", [64, 1])
        crossb = sb("crossb", [64, 1])
        wc = {"gat1": sb("wc_gat1", [65, 192]), "gat2": sb("wc_gat2", [65, 192]),
              "tc1": sb("wc_tc1", [65, 256]), "tc2": sb("wc_tc2", [65, 256]), "pt": sb("wc_pt", [65, 192])}
        wT = sb("wT", [64, 2, 64])
        avec = sb("avec", [64, 4])
        amat = sb("amat", [64, 2, 192])
        skw = sb("skw", [65, 2, 64])
        we = [sb(f"we{i}", [64, 128]) for i in range(2)]
        bias = sb("bias", [NP, 2, 64])
        wd1 = sb("wd1", [7, 128])
        wd2 = sb("wd2", [128, 128])
        pv4 = sb("pv4", [128, 5])
        mcol = sb("mcol", [128, 2])
        epsc = sb("epsc", [128, 1])
        Gt = [sb(f"Gt{i}", [128, J, 2, 128]) for i in range(U)]
        ix = [sb(f"ix{i}", [128, 2 * J], i32) for i in range(U)]
        xd = [sb(f"xd{i}", [128, J, 2, 64]) for i in range(U)]
        fl = [sb(f"fl{i}", [128, 2 * W], bf16) for i in range(U)]
        ea = [sb(f"ea{i}", [128, W]) for i in range(U)]
        ex = [sb(f"ex{i}", [128, W]) for i in range(U)]
        sr = sb("sr", [128, W])
        sl = sb("sl", [128, W])
        M = [sb(f"M{i}", [128, W + 1]) for i in range(U)]
        arg = sb("arg", [128, 2 * W])
        ap = sb("ap", [128, 2 * W])
        pv = sb("pv", [128, W])
        num = [sb(f"num{i}", [128, W]) for i in range(U)]
        den = [sb(f"den{i}", [128, W]) for i in range(U)]
        O = [sb(f"O{i}", [128, 2, J, 128]) for i in range(U)]
        O3 = [o[:, :, :, 0:64] for o in O]
        mg = sb("mg", [128, 3])
        mgb = sb("mgb", [64, 3])
        mw = sb("mw", [64, 6])
        parity = sb("parity", [64, 2])

        ps = [ctx.enter_context(nc.psum_tensor(f"ps{i}", [128, 512], f32)) for i in range(8)]
        pX, pS, pV, pR, pN, pD = ps[0], ps[1], ps[2:5], ps[5], ps[6], ps[7]

        flat = lambda t: t.rearrange("p t c -> p (t c)")
        bc = lambda t: t.unsqueeze(2).to_broadcast([NP, NT, 64])

        class Chain:

            def __init__(self, name):
                self.eng, self.sem, self.n = None, sem(name), 0

            def __call__(self, instruction):
                self.n += 1
                instruction.then_inc(self.sem, 1)
                self.eng.wait_ge(self.sem, self.n)

        node_chain = Chain("vector_chain")

        def dve_chain(dve):
            node_chain.eng = dve
            return node_chain


        def order(kind):
            return KINDS.index(kind)

        def base(kind):
            return G * (int(kind[-1]) - 1) if kind.startswith("gc") else G * order(kind)

        def count(kind, it, s):
            return base(kind) + U * it + s + 1

        def next_group(it, s):
            return (it, s + 1) if s < U - 1 else (it + 1, 0)

        def group_before(it, s):
            return (it, s - 1) if s > 0 else (it - 1, U - 1)

        def rows_merged(kind):
            return sum(1 if k.startswith("gc") else 2 for k in KINDS[:order(kind) + 1])

        def nload(kind):
            return 2 if kind.startswith("gc") else 4 if kind.startswith("gat") else 5

        def loads_before(kind):
            return 16 * (G // U) * sum(nload(k) for k in KINDS[:order(kind)])

        def uses(kind, it):
            return (G // U) * order(kind) + it

        def walk(eng, step):
            for s in range(U):
                step(0, s, s == 0, False)
            with eng.Fori(1, G // U - 1) as it:
                for s in range(U):
                    step(it, s, False, False)
            for s in range(U):
                step(G // U - 1, s, False, s == U - 1)

        def pass_sp(sp, kind):
            gc = kind.startswith("gc")
            if not gc:
                sp.wait_ge(sem(f"{kind}_spread"), 16 * 2 * NT)

            def step(it, s, first, last):
                g = U * it + s
                n = count(kind, it, s)
                need(sp, f"{kind}_gathered{s}", 2 * J * 16 * it)
                sp.dma_start(ix[s][:, :], a["src_g"][ds(g, 1), :, :].rearrange("a p j -> p (a j)")) \
                    .then_inc(sem(f"indices{s}"), 16)
                loaded = sem(f"loaded{s}")
                if gc:
                    need(sp, "gc_summed", n - U)
                    for c in range(2):
                        sp.dma_start(fl[s][64 * c:64 * c + 64, 0:W],
                                     flags[ds(g, 1), c, 0:W].to_broadcast([64, W])).then_inc(loaded, 16)
                    return
                need(sp, "shifted", n - U)
                need(sp, "values_turned", n - U)
                for c in range(2):
                    sp.dma_start(fl[s][64 * c:64 * c + 64, :], flags[ds(g, 1), c, :].to_broadcast([64, 2 * W])) \
                        .then_inc(loaded, 16)
                sv = spread.rearrange("(c g j p) f -> c g p j f", c=2, g=G, j=J)
                for c in range(2):
                    sp.dma_start(xd[s][:, :, c, :], sv[c, ds(g, 1)].rearrange("a p j f -> p (a j) f")) \
                        .then_inc(loaded, 16)
                if kind in ("tc1", "tc2"):
                    sp.dma_start(ea[s][0:64, :], a["ea32"][ds(g, 1), :, :].rearrange("a p j -> p (a j)")) \
                        .then_inc(loaded, 16)
                if kind == "pt":
                    sp.dma_start(ea[s][:, :], dist[ds(g, 1), :, :].rearrange("a p j -> p (a j)")) \
                        .then_inc(loaded, 16)

            walk(sp, step)

        def pass_pool(pool, kind):
            gc = kind.startswith("gc")
            pool.wait_ge(sem("tables_written"), 16 * (order(kind) + 1))

            def step(it, s, first, last):
                pool.wait_ge(sem(f"indices{s}"), 16 * (uses(kind, it) + 1))
                need(pool, "gc_turned" if gc else "values_turned", count(kind, it, s) - U)
                if not isinstance(it, int):
                    pool.nop(nofuse=True)
                for c in range(2):
                    for j in range(J):
                        k = c * J + j
                        src = table3 if gc else table
                        to = Gt[s][:, j, 0, 64 * c:64 * c + 64] if gc else Gt[s][:, j, c, :]
                        pool.indirect_dma_start(out=to, out_offset=None, in_=src[:, :],
                                                in_offset=on_axis0(ix[s][:, k:k + 1])) \
                            .then_inc(sem(f"{kind}_gathered{s}"), 16)

            walk(pool, step)

        def pass_pe(pe, kind):
            gat = kind.startswith("gat")
            edge = None if gat else ident if kind == "pt" else we[int(kind == "tc2")]
            ek = 128 if kind == "pt" else 64

            def turn(out, s, half, signal):
                if edge is not None:
                    pe.matmul(out[:, :], edge[0:ek, :], ea[s][0:ek, :], start=True, stop=False)
                for j in range(J):
                    rows = Gt[s][:, j, :, :].rearrange("p c f -> p (c f)")[:, half:256:2]
                    cols = out[:, T * j:T * j + T]
                    if edge is None:
                        last = pe.transpose(cols, rows, ident)
                    else:
                        last = pe.matmul(cols, rows, ident, start=False, stop=(j == J - 1))
                last.then_inc(sem(signal), 1)

            def turn_targets(it, s):
                n = count(kind, it, s)
                pe.wait_ge(sem(f"loaded{s}"), loads_before(kind) + 16 * nload(kind) * (it + 1))
                need(pe, "spread_out", n - 1)
                for j in range(J):
                    last = pe.transpose(pX[:, T * j:T * j + T],
                                        xd[s][:, j, :, :].rearrange("p c f -> p (c f)"), ident)
                last.then_inc(sem("targets_turned"), 1)

            def turn_sources(it, s):
                n = count(kind, it, s)
                pe.wait_ge(sem(f"{kind}_gathered{s}"), 2 * J * 16 * (it + 1))
                need(pe, "combined", n - 1)
                turn(pS, s, 0, "logits_turned")
                need(pe, "weighed", n - U)
                turn(pV[s], s, 1, "values_turned")

            def score(it, s):
                n = count(kind, it, s)
                pe.wait_ge(sem("combined"), n)
                need(pe, "arguments", n - 1)
                pe.matmul(pR[:, :], bones8[:, :], sr[:, :], start=True, stop=True).then_inc(sem("scored"), 1)

            def turn_back(it, s):
                n = count(kind, it, s)
                pe.wait_ge(sem("denominated"), n)
                need(pe, "evacuated", n - 1)
                for j in range(J):
                    out, part = pD[:, T * j:T * j + T], den[s][:, T * j:T * j + T]
                    if gat:
                        pe.matmul(out, part, even, start=True, stop=False)
                        pe.matmul(out, M[s][:, T * j + 1:T * j + T + 1], odd, start=False, stop=True)
                    else:
                        pe.transpose(out, part, ident)
                pe.wait_ge(sem("numerated"), n)
                for j in range(J):
                    last = pe.transpose(pN[:, T * j:T * j + T], num[s][:, T * j:T * j + T], ident)
                last.then_inc(sem("turned_back"), 1)

            def step(it, s, first, last):
                if not last:
                    turn_targets(*next_group(it, s))
                if kind in ("tc1", "tc2"):
                    score(it, s)
                if not last:
                    turn_sources(*next_group(it, s))
                if not first:
                    turn_back(*group_before(it, s))

            turn_targets(0, 0)
            turn_sources(0, 0)
            walk(pe, step)
            turn_back(G // U - 1, U - 1)

        def sum_pe(pe, kind):
            def turn_back(it, s):
                n = count(kind, it, s)
                pe.wait_ge(sem("gc_summed"), n)
                need(pe, "gc_evacuated", n - 1)
                for j in range(J):
                    last = pe.transpose(pN[:, T * j:T * j + T], num[s][:, T * j:T * j + T], ident)
                last.then_inc(sem("gc_back"), 1)

            def step(it, s, first, last):
                n = count(kind, it, s)
                pe.wait_ge(sem(f"{kind}_gathered{s}"), 2 * J * 16 * (it + 1))
                need(pe, "gc_summed", n - U)
                for j in range(J):
                    turned = pe.transpose(pV[s][:, T * j:T * j + T], Gt[s][:, j, 0, :], ident)
                turned.then_inc(sem("gc_turned"), 1)
                if not first:
                    turn_back(*group_before(it, s))

            walk(pe, step)
            turn_back(G // U - 1, U - 1)

        def merge_states(dve, kind, gc):
            chain = dve_chain(dve)
            if gc:
                dve.wait_ge(sem("gc_summed"), base(kind) + G)
                chain(dve.tensor_copy(mg[:, 1:2], num[U - 1][:, W - 1:W]))
            else:
                dve.wait_ge(sem("numerated"), base(kind) + G)
                dve.wait_ge(sem("denominated"), base(kind) + G)
                chain(dve.tensor_copy(mg[:, 0:1], M[U - 1][:, W:W + 1]))
                chain(dve.tensor_copy(mg[:, 1:2], num[U - 1][:, W - 1:W]))
                chain(dve.tensor_copy(mg[:, 2:3], den[U - 1][:, W - 1:W]))
            dve.sem_inc(sem("last"), 1)
            dve.wait_ge(sem("moved"), 16 * (order(kind) + 1))
            if gc:
                chain(dve.scalar_tensor_tensor(mw[:, 4:5], mgb[:, 1:2], cross[:, 0:1], mg[0:64, 1:2],
                                               ALU.mult, ALU.add))
            else:
                chain(dve.tensor_tensor(mw[:, 0:1], mgb[:, 0:1], crossb[:, :], ALU.add))
                chain(dve.tensor_tensor(mw[:, 1:2], mw[:, 0:1], mg[0:64, 0:1], ALU.max))
                chain(dve.tensor_tensor(mw[:, 2:3], mg[0:64, 0:1], mw[:, 1:2], ALU.subtract))
                chain(dve.tensor_tensor(mw[:, 3:4], mw[:, 0:1], mw[:, 1:2], ALU.subtract))
                dve.sem_inc(sem("merge_arg"), 1)
                dve.wait_ge(sem("merge_exp"), order(kind) + 1)
                chain(dve.tensor_tensor(mgb[:, 1:2], mgb[:, 1:2], mw[:, 3:4], ALU.mult))
                chain(dve.tensor_tensor(mgb[:, 2:3], mgb[:, 2:3], mw[:, 3:4], ALU.mult))
                chain(dve.scalar_tensor_tensor(mw[:, 4:5], mg[0:64, 1:2], mw[:, 2:3], mgb[:, 1:2],
                                               ALU.mult, ALU.add))
                chain(dve.scalar_tensor_tensor(mw[:, 5:6], mg[0:64, 2:3], mw[:, 2:3], mgb[:, 2:3],
                                               ALU.mult, ALU.add))
                if kind.startswith("gat"):
                    chain(dve.tensor_tensor(mw[:, 5:6], mw[:, 5:6], parity[:, 0:1], ALU.mult))
                    chain(dve.scalar_tensor_tensor(mw[:, 5:6], mw[:, 1:2], parity[:, 1:2], mw[:, 5:6],
                                                   ALU.mult, ALU.add))
            dve.sem_inc(sem("merged"), 1)

        def sum_dve(dve, kind):
            def step(it, s, first, last):
                n = count(kind, it, s)
                dve.wait_ge(sem(f"loaded{s}"), loads_before(kind) + 16 * nload(kind) * (it + 1))
                dve.wait_ge(sem("gc_turned"), n)
                need(dve, "gc_back", n - U)
                need(dve, "gc_summed", n - 1)
                dve.tensor_tensor_scan(num[s][:, :], fl[s][:, 0:W], pV[s][:, :], num[s - 1][:, W - 1:W],
                                       ALU.mult, ALU.add).then_inc(sem("gc_summed"), 1)

            walk(dve, step)
            merge_states(dve, kind, True)

        def pass_dve(dve, kind):
            tc, gat = kind in ("tc1", "tc2"), kind.startswith("gat")
            tc_base = base(kind) - base("tc1")
            logit = pR if tc else sl if gat else sr

            def spread_targets(it, s):
                n = count(kind, it, s)
                dve.wait_ge(sem("targets_turned"), n)
                dve.wait_ge(sem(f"loaded{s}"), loads_before(kind) + 16 * nload(kind) * (it + 1))
                dve.tensor_tensor_scan(ex[s][:, :], fl[s][:, 0:W], pX[:, :], ex[s - 1][:, W - 1:W],
                                       ALU.mult, ALU.add).then_inc(sem("spread_out"), 1)

            def step(it, s, first, last):
                n = count(kind, it, s)
                new = fl[s][:, W:2 * W]
                dve.wait_ge(sem("spread_out"), n)
                dve.wait_ge(sem("logits_turned"), n)
                dve.tensor_tensor(sr[:, :], pS[:, :], ex[s][:, :], ALU.mult if tc else ALU.add) \
                    .then_inc(sem("combined"), 1)
                if not last:
                    spread_targets(*next_group(it, s))
                if gat:
                    dve.wait_ge(sem("combined"), n)
                    dve.scalar_tensor_tensor(sl[:, :], sr[:, :], 0.2, sr[:, :], ALU.mult, ALU.max) \
                        .then_inc(sem("logits"), 1)
                if not first:
                    weigh(*group_before(it, s))
                if gat:
                    need(dve, "turned_back", n - U)
                dve.tensor_copy(M[s][:, 0:1], M[s - 1][:, W:W + 1]).then_inc(sem("max_carried"), 1)
                if tc:
                    dve.wait_ge(sem("scored"), n - base("tc1"))
                elif gat:
                    dve.wait_ge(sem("logits"), n)
                else:
                    dve.wait_ge(sem("combined"), n)
                dve.tensor_tensor_scan(M[s][:, 1:W + 1], new, logit[:, :], M[s - 1][:, W:W + 1],
                                       ALU.add, ALU.max).then_inc(sem("maxima"), 1)
                if not first:
                    sum_denominators(*group_before(it, s))
                dve.wait_ge(sem("max_carried"), n)
                dve.wait_ge(sem("maxima"), n)
                need(dve, "exponentiated", n - 1)
                dve.tensor_tensor(arg[:, W:2 * W], logit[:, :], M[s][:, 1:W + 1], ALU.subtract) \
                    .then_inc(sem("arguments"), 1)
                dve.tensor_tensor(arg[:, 0:W], M[s][:, 0:W], new, ALU.add).then_inc(sem("shifted"), 1)
                if not first:
                    sum_numerators(*group_before(it, s))
                dve.wait_ge(sem("shifted"), n)
                dve.tensor_tensor(arg[:, 0:W], arg[:, 0:W], M[s][:, 1:W + 1], ALU.subtract) \
                    .then_inc(sem("decays"), 1)

            def weigh(it, s):
                n = count(kind, it, s)
                dve.wait_ge(sem("exponentiated"), n)
                dve.wait_ge(sem("values_turned"), n)
                need(dve, "numerated", n - 1)
                dve.tensor_tensor(pv[:, :], ap[:, W:2 * W], pV[s][:, :], ALU.mult) \
                    .then_inc(sem("weighed"), 1)

            def sum_denominators(it, s):
                n = count(kind, it, s)
                need(dve, "turned_back", n - U)
                need(dve, "denominated", n - 1)
                dve.tensor_tensor_scan(den[s][:, :], ap[:, 0:W], ap[:, W:2 * W], den[s - 1][:, W - 1:W],
                                       ALU.mult, ALU.add).then_inc(sem("denominated"), 1)

            def sum_numerators(it, s):
                dve.wait_ge(sem("weighed"), count(kind, it, s))
                dve.tensor_tensor_scan(num[s][:, :], ap[:, 0:W], pv[:, :], num[s - 1][:, W - 1:W],
                                       ALU.mult, ALU.add).then_inc(sem("numerated"), 1)

            spread_targets(0, 0)
            walk(dve, step)
            for part in (weigh, sum_denominators, sum_numerators):
                part(G // U - 1, U - 1)
            merge_states(dve, kind, False)

        def pass_act(act, kind):
            gc = kind.startswith("gc")
            w = 64 if gc else 128
            to = (ends3 if gc else ends).rearrange("(c g j p) f -> c g p j f", c=2, g=G, j=J)

            def exponentiate(it, s):
                n = count(kind, it, s)
                act.wait_ge(sem("arguments"), n)
                act.wait_ge(sem("decays"), n)
                need(act, "denominated", n - 1)
                need(act, "numerated", n - 1)
                act.activation(ap[:, :], arg[:, :], ACT.Exp).then_inc(sem("exponentiated"), 1)

            def evacuate(it, s):
                n = count(kind, it, s)
                act.wait_ge(sem("gc_back" if gc else "turned_back"), n)
                need(act, f"stored{s}", 32 * uses(kind, it))
                o = sem("gc_evacuated" if gc else "evacuated")
                for k, bank in enumerate([pN] if gc else [pN, pD]):
                    kept = act.activation(O[s][:, :, :, 64 * k:64 * k + 64],
                                          bank[:, :].rearrange("p (j c f) -> p c j f", j=J, c=2), ACT.Copy)
                kept.then_inc(o, 1)
                act.wait_ge(o, n)
                for c in range(2):
                    act.dma_start(to[c, ds(U * it + s, 1)].rearrange("a p j f -> p (a j) f"), O[s][:, c, :, 0:w]) \
                        .then_inc(sem(f"stored{s}"), 16)

            def step(it, s, first, last):
                if gc:
                    evacuate(it, s)
                    return
                exponentiate(it, s)
                if not first:
                    evacuate(*group_before(it, s))

            walk(act, step)
            if not gc:
                evacuate(G // U - 1, U - 1)
                act.wait_ge(sem("merge_arg"), order(kind) + 1)
                act.activation(mw[:, 2:4], mw[:, 2:4], ACT.Exp).then_inc(sem("merge_exp"), 1)

        def merge_sp(sp, kind):
            gc = kind.startswith("gc")
            sp.wait_ge(sem("last"), order(kind) + 1)
            sp.dma_start(mgb[:, :], mg[64:128, :]).then_inc(sem("moved"), 16)
            sp.wait_ge(sem("merged"), order(kind) + 1)
            for s in range(U):
                sp.wait_ge(sem(f"stored{s}"), 32 * (G // U) * (order(kind) + 1))
            if gc:
                sp.dma_start(ends3[S - 1, :].rearrange("(f a) -> f a", a=1), mw[:, 4:5]) \
                    .then_inc(sem("row_merged"), 16)
            else:
                for h in range(2):
                    sp.dma_start(ends[S - 1, 64 * h:64 * h + 64].rearrange("(f a) -> f a", a=1),
                                 mw[:, 4 + h:5 + h]).then_inc(sem("row_merged"), 16)

        def take_pool(pool, kind):
            gc = kind.startswith("gc")
            pool.wait_ge(sem("row_merged"), 16 * rows_merged(kind))
            for t in range(NT):
                pool.indirect_dma_start(out=R3[:, t, :] if gc else R[:, t, :], out_offset=None,
                                        in_=(ends3 if gc else ends)[:, :],
                                        in_offset=on_axis0(idx_end[:, t:t + 1])) \
                    .then_inc(sem("taken"), 16)

        def scatter_pool(pool, kind):
            pool.wait_ge(sem("tabled"), NT * (order(kind) + 1))
            for t in range(NT):
                for ix_ in (idx_a, idx_b):
                    pool.indirect_dma_start(out=spread[:, :], out_offset=on_axis0(ix_[:, t:t + 1]),
                                            in_=TT[0:NP, t, 128:192], in_offset=None,
                                            bounds_check=EP - 1, oob_is_err=False) \
                        .then_inc(sem(f"{kind}_spread"), 16)

        def tables_sp(sp, kind):
            sp.wait_ge(sem("tabled"), NT * (order(kind) + 1))
            sp.dma_start(table.rearrange("(p t) c -> p t c", t=NT), TT[0:NP, :, 0:128]) \
                .then_inc(sem("tables_written"), 16)

        SOFT = KINDS[:5]
        NORMS = ["gat2", "tc2", "pt", "gc2"]
        CH = [(i, min(4, NT - i)) for i in range(0, NT, 4)]

        def turns_before(kind, tag):
            done = [(k, g) for k in SOFT for g in (("x", "h2") if k == "tc2" else ("x",))]
            return len(CH) * done.index((kind, tag))

        def turn_nodes_pe(pe, kind, x, tag):
            b = turns_before(kind, tag)
            for k, (t0, m) in enumerate(CH):
                if k >= 2:
                    pe.wait_ge(sem("nodes_kept"), b + k - 1)
                for i in range(m):
                    last = pe.transpose(ps[7 * (k % 2)][0:64, NP * i:NP * i + NP], x[:, t0 + i, :], ident[0:NP, 0:NP])
                last.then_inc(sem("nodes_turned"), 1)

        def turn_nodes_act(act, kind, to, tag):
            b = turns_before(kind, tag)
            for k, (t0, m) in enumerate(CH):
                act.wait_ge(sem("nodes_turned"), b + k + 1)
                act.activation(to[0:64, t0:t0 + m, :],
                               ps[7 * (k % 2)][0:64, 0:NP * m].rearrange("p (t n) -> p t n", n=NP), ACT.Copy) \
                    .then_inc(sem("nodes_kept"), 1)

        def tables_pe(pe, kind, x, to):
            pe.wait_ge(sem(f"{kind}_features"), 1)
            turn_nodes_pe(pe, kind, x, "x")
            pe.wait_ge(sem("nodes_kept"), turns_before(kind, "x") + len(CH))
            w = wc[kind]
            for t in range(NT):
                if t >= 2:
                    pe.wait_ge(sem("tabled"), NT * order(kind) + t - 1)
                pe.matmul(ps[5 + t % 2][0:NP, 0:w.shape[1]], to[:, t, :], w[:, :], start=True, stop=True) \
                    .then_inc(sem("multiplied"), 1)

        def tables_dve(dve, kind):
            w = wc[kind].shape[1]
            for t in range(NT):
                dve.wait_ge(sem("multiplied"), NT * order(kind) + t + 1)
                out = ps[5 + t % 2][0:NP, :]
                dve.tensor_copy(TT[0:NP, t, 0:128].rearrange("p (f h) -> p h f", h=2),
                                out[:, 0:128].rearrange("p (h f) -> p h f", h=2))
                dve.tensor_copy(TT[0:NP, t, 128:w], out[:, 128:w]).then_inc(sem("tabled"), 1)

        def layer_norm(c, dve, kind, x):
            c(dve.tensor_reduce(st1[0][:, :], x[:, :, :], AX, ALU.add))
            c(dve.tensor_scalar(st1[0][:, :], st1[0][:, :], -1.0 / D, None, ALU.mult))
            c(dve.tensor_tensor(x[:, :, :], x[:, :, :], bc(st1[0][:, :]), ALU.add))
            c(dve.tensor_tensor(tmp[0][:, :, :], x[:, :, :], x[:, :, :], ALU.mult))
            c(dve.tensor_reduce(st1[0][:, :], tmp[0][:, :, :], AX, ALU.add))
            c(dve.tensor_scalar(st1[0][:, :], st1[0][:, :], 1.0 / D, EPS, ALU.mult, ALU.add))
            dve.sem_inc(sem("variances"), 1)
            dve.wait_ge(sem("deviations"), NORMS.index(kind) + 1)
            c(dve.reciprocal(st1[1][:, :], st1[1][:, :]))
            c(dve.tensor_tensor(x[:, :, :], x[:, :, :], bc(st1[1][:, :]), ALU.mult))

        def sqrt_act(act, kind, tag):
            if tag == "std":
                act.wait_ge(sem("variances"), NORMS.index(kind) + 1)
            else:
                act.wait_ge(sem("squared_norms"), 1)
            act.activation(st1[1][:, :], st1[0][:, :], ACT.Sqrt) \
                .then_inc(sem("deviations" if tag == "std" else "norms"), 1)

        def divide(c, dve, kind, out):
            dve.wait_ge(sem("taken"), 16 * NT * (order(kind) + 1))
            c(dve.reciprocal(out[:, :, :], R[:, :, 64:128]))
            c(dve.tensor_tensor(out[:, :, :], out[:, :, :], R[:, :, 0:64], ALU.mult))
            c(dve.tensor_tensor(out[:, :, :], out[:, :, :], bc(has[:, :]), ALU.mult))

        def add_self_loops(c, dve, kind):
            pairs = lambda t: t.rearrange("p t (i k) -> p t i k", k=2)
            packed = pairs(R[:, :, 64:128])
            own = pairs(TT[0:NP, :, 0:128])
            logit, value = own[:, :, :, 0], own[:, :, :, 1]
            s0, top = tmp[0], tmp[1]
            dve.wait_ge(sem("taken"), 16 * NT * (order(kind) + 1))
            c(dve.tensor_tensor(s0[:, :, :], logit, TT[0:NP, :, 128:192], ALU.add))
            c(dve.scalar_tensor_tensor(flat(s0[:, :, :]), flat(s0[:, :, :]), 0.2, flat(s0[:, :, :]),
                                       ALU.mult, ALU.max))
            for k in range(2):
                c(dve.tensor_tensor(pairs(SK[:, :, :])[:, :, :, k], packed[:, :, :, 1],
                                    has[:, :].unsqueeze(2).to_broadcast([NP, NT, 32]), ALU.mult))
            c(dve.tensor_scalar(st1[0][:, :], has[:, :], -1.0, BIG, ALU.add, ALU.mult))
            c(dve.tensor_tensor(SK[:, :, :], SK[:, :, :], bc(st1[0][:, :]), ALU.add))
            c(dve.tensor_tensor(top[:, :, :], SK[:, :, :], s0[:, :, :], ALU.max))
            c(dve.tensor_tensor(s0[:, :, :], s0[:, :, :], top[:, :, :], ALU.subtract))
            c(dve.tensor_tensor(SK[:, :, :], SK[:, :, :], top[:, :, :], ALU.subtract))
            dve.sem_inc(sem("loop_args"), 1)
            dve.wait_ge(sem("loop_exps"), 2 * (order(kind) + 1))
            for k in range(2):
                c(dve.tensor_tensor(pairs(H[:, :, :])[:, :, :, k], packed[:, :, :, 0],
                                    pairs(SK[:, :, :])[:, :, :, k], ALU.mult))
            c(dve.tensor_tensor(H[:, :, :], H[:, :, :], s0[:, :, :], ALU.add))
            c(dve.tensor_scalar(H[:, :, :], H[:, :, :], 1e-16, None, ALU.add))
            c(dve.reciprocal(H[:, :, :], H[:, :, :]))
            c(dve.tensor_tensor(SK[:, :, :], SK[:, :, :], R[:, :, 0:64], ALU.mult))
            c(dve.tensor_tensor(s0[:, :, :], s0[:, :, :], value, ALU.mult))
            c(dve.tensor_tensor(SK[:, :, :], SK[:, :, :], s0[:, :, :], ALU.add))
            c(dve.tensor_tensor(H[:, :, :], H[:, :, :], SK[:, :, :], ALU.mult))

        def post_dve(dve, kind):
            c = dve_chain(dve)
            nxt = KINDS[KINDS.index(kind) + 1] if kind != "gc2" else "out"
            if kind == "gat1":
                add_self_loops(c, dve, kind)
                c(dve.tensor_tensor(H[:, :, :], H[:, :, :],
                                    bias[:, 0:1, :].to_broadcast([NP, NT, 64]), ALU.add))
                c(dve.tensor_scalar(tmp[0][:, :, :], H[:, :, :], 0.0, None, ALU.min))
                dve.sem_inc(sem("elu_arg"), 1)
                dve.wait_ge(sem("elu_exp"), 1)
                c(dve.tensor_scalar(tmp[1][:, :, :], tmp[1][:, :, :], -1.0, None, ALU.add))
                c(dve.scalar_tensor_tensor(flat(H[:, :, :]), flat(H[:, :, :]), 0.0, flat(tmp[1][:, :, :]),
                                           ALU.max, ALU.add))
            elif kind == "gat2":
                add_self_loops(c, dve, kind)
                c(dve.tensor_tensor(H[:, :, :], H[:, :, :],
                                    bias[:, 1:2, :].to_broadcast([NP, NT, 64]), ALU.add))
                c(dve.tensor_tensor(tmp[0][:, :, :], H[:, :, :], H[:, :, :], ALU.mult))
                c(dve.tensor_reduce(st1[0][:, :], tmp[0][:, :, :], AX, ALU.add))
                dve.sem_inc(sem("squared_norms"), 1)
                dve.wait_ge(sem("norms"), 1)
                c(dve.tensor_scalar(st1[1][:, :], st1[1][:, :], 1e-12, None, ALU.max))
                c(dve.reciprocal(st1[1][:, :], st1[1][:, :]))
                c(dve.tensor_tensor(H[:, :, :], H[:, :, :], bc(st1[1][:, :]), ALU.mult))
                c(dve.tensor_tensor(X[:, :, :], X[:, :, :], H[:, :, :], ALU.add))
                layer_norm(c, dve, kind, X)
            elif kind in ("tc1", "tc2"):
                divide(c, dve, kind, H)
                c(dve.tensor_tensor(H[:, :, :], H[:, :, :], TT[0:NP, :, 192:256], ALU.add))
                c(dve.tensor_scalar(H[:, :, :], H[:, :, :], 0.0, None, ALU.max))
                if kind == "tc2":
                    dve.sem_inc(sem("h2_ready"), 1)
                    for t in range(NT):
                        dve.wait_ge(sem("skipped"), t + 1)
                        dve.scalar_tensor_tensor(X[:, t, :], ps[5 + t % 2][0:NP, 0:64], 0.0, X[:, t, :],
                                                 ALU.max, ALU.add).then_inc(sem("skip_added"), 1)
                    dve.wait_ge(sem("skip_added"), NT)
                    layer_norm(c, dve, kind, X)
            elif kind == "pt":
                divide(c, dve, kind, H)
                c(dve.tensor_tensor(X[:, :, :], X[:, :, :], H[:, :, :], ALU.add))
                layer_norm(c, dve, kind, X)
                c(dve.tensor_tensor(SK[:, :, :], X[:, :, :], bc(dinv[:, :]), ALU.mult))
            else:
                dve.wait_ge(sem("taken"), 16 * NT * (order(kind) + 1))
                c(dve.tensor_tensor(H[:, :, :] if kind == "gc1" else tmp[1][:, :, :], R3,
                                    bc(dinv[:, :]), ALU.mult))
                if kind == "gc1":
                    c(dve.tensor_tensor(SK[:, :, :], H[:, :, :], bc(dinv[:, :]), ALU.mult))
                else:
                    c(dve.tensor_tensor(H[:, :, :], H[:, :, :], X[:, :, :], ALU.add))
                    c(dve.tensor_tensor(H[:, :, :], H[:, :, :], tmp[1][:, :, :], ALU.add))
                    c(dve.scalar_tensor_tensor(flat(X[:, :, :]), flat(H[:, :, :]), 1.0 / 3.0,
                                               flat(X[:, :, :]), ALU.mult, ALU.add))
                    layer_norm(c, dve, kind, X)
            dve.sem_inc(sem(f"{nxt}_features"), 1)

        def post_act(act, kind):
            if kind.startswith("gat"):
                act.wait_ge(sem("loop_args"), order(kind) + 1)
                for t in (tmp[0], SK):
                    act.activation(t[:, :, :], t[:, :, :], ACT.Exp).then_inc(sem("loop_exps"), 1)
            if kind == "gat1":
                act.wait_ge(sem("elu_arg"), 1)
                act.activation(tmp[1][:, :, :], tmp[0][:, :, :], ACT.Exp).then_inc(sem("elu_exp"), 1)
            if kind == "gat2":
                sqrt_act(act, kind, "norm")
            if kind == "tc2":
                turn_nodes_act(act, kind, xT, "h2")
            if kind in ("gat2", "tc2", "pt", "gc2"):
                sqrt_act(act, kind, "std")

        def post_pe(pe, kind):
            if kind != "tc2":
                return
            pe.wait_ge(sem("h2_ready"), 1)
            turn_nodes_pe(pe, kind, H, "h2")
            pe.wait_ge(sem("nodes_kept"), turns_before(kind, "h2") + len(CH))
            for t in range(NT):
                if t >= 2:
                    pe.wait_ge(sem("skip_added"), t - 1)
                out = ps[5 + t % 2][0:NP, 0:64]
                pe.matmul(out, h1T[0:64, t, :], skw[0:64, 0, :], start=True, stop=False)
                pe.matmul(out, xT[:, t, :], skw[:, 1, :], start=False, stop=True).then_inc(sem("skipped"), 1)

        node_in = {"gat1": (X, xT), "gat2": (H, xT), "tc1": (X, xT), "tc2": (H, h1T), "pt": (X, xT)}

        Q = 3
        mu, mv = [ps[0], ps[1], ps[2]], [ps[3], ps[4], ps[5]]
        msq = [num[0], num[1], den[0]]
        mvar = [ex[0], ex[1], den[1]]
        mh = [sr, sl, pv]
        mx = [ea[0], ea[1], ea[2]]

        def mlp_sp(sp):
            def step(it):
                if not isinstance(it, int):
                    sp.wait_ge(sem("mlp_first"), Q * it)
                for q in range(Q):
                    sp.dma_start(mx[q][0:6, 0:W], a["ea3"][ds(Q * it + q, 1), :, :].rearrange("a p j -> p (a j)")) \
                        .then_inc(sem(f"mlp_in{q}"), 16)
            sp.wait_ge(sem("mlp_ones"), 3)
            step(0)
            with sp.Fori(1, G // Q) as it:
                step(it)

        def mlp_pe(pe):
            pe.wait_ge(sem("mlp_ready"), 1)

            def step(it):
                n = Q * it
                for q in range(Q):
                    pe.wait_ge(sem(f"mlp_in{q}"), 16 * (it + 1))
                    if not isinstance(it, int):
                        pe.wait_ge(sem("mlp_scaled"), 2 * n - Q + q + 1)
                    pe.matmul(mu[q][:, :], wd1[:, :], mx[q][0:7, 0:W], start=True, stop=True) \
                        .then_inc(sem("mlp_first"), 1)
                for q in range(Q):
                    pe.wait_ge(sem("mlp_squared"), 2 * n + q + 1)
                    pe.matmul(mv[q][:, :], bones, msq[q][:, :], start=True, stop=True) \
                        .then_inc(sem("mlp_vars"), 1)
                for q in range(Q):
                    pe.wait_ge(sem("mlp_gelus"), 2 * n + q + 1)
                    pe.matmul(mu[q][:, :], wd2[:, :], mh[q][:, :], start=True, stop=True) \
                        .then_inc(sem("mlp_second"), 1)
                for q in range(Q):
                    pe.wait_ge(sem("mlp_squared"), 2 * n + Q + q + 1)
                    pe.matmul(mv[q][:, :], bones, msq[q][:, :], start=True, stop=True) \
                        .then_inc(sem("mlp_vars"), 1)

            step(0)
            with pe.Fori(1, G // Q) as it:
                step(it)

        def mlp_act(act):
            act.wait_ge(sem("mlp_ready"), 1)

            def half(it, k):
                n = 2 * Q * it + k * Q
                for q in range(Q):
                    act.wait_ge(sem("mlp_second" if k else "mlp_first"), Q * it + q + 1)
                    if k:
                        act.activation(msq[q][:, :], mu[q][:, :], ACT.Square, bias=pv4[:, 2:3]) \
                            .then_inc(sem("mlp_squared"), 1)
                    else:
                        act.activation(msq[q][:, :], mu[q][:, :], ACT.Square).then_inc(sem("mlp_squared"), 1)
                for q in range(Q):
                    act.wait_ge(sem("mlp_vars"), n + q + 1)
                    act.activation(mvar[q][:, :], mv[q][:, :], ACT.Sqrt, scale=1.0 / D, bias=epsc[:, :]) \
                        .then_inc(sem("mlp_std"), 1)
                for q in range(Q):
                    act.wait_ge(sem("mlp_scaled"), n + q + 1)
                    if not k and not isinstance(it, int):
                        act.wait_ge(sem(f"mlp_stored{q}"), 16 * it)
                    act.activation(mh[q][:, :], mvar[q][:, :], ACT.Gelu, scale=pv4[:, 3 * k:3 * k + 1],
                                   bias=pv4[:, 1 + 3 * k:2 + 3 * k]).then_inc(sem("mlp_gelus"), 1)
                    if k:
                        act.wait_ge(sem("mlp_gelus"), n + q + 1)
                        act.dma_start(dist[ds(Q * it + q, 1), :, :].rearrange("a p j -> p (a j)"), mh[q][:, :]) \
                            .then_inc(sem(f"mlp_stored{q}"), 16)

            half(0, 0)
            half(0, 1)
            with act.Fori(1, G // Q) as it:
                half(it, 0)
                half(it, 1)

        def mlp_dve(dve):
            def half(it, k):
                n = 2 * Q * it + k * Q
                for q in range(Q):
                    dve.wait_ge(sem("mlp_std"), n + q + 1)
                    dve.reciprocal(mvar[q][:, :], mvar[q][:, :]).then_inc(sem("mlp_rstd"), 1)
                    dve.wait_ge(sem("mlp_rstd"), n + q + 1)
                    if k:
                        dve.scalar_tensor_tensor(mvar[q][:, :], mu[q][:, :], pv4[:, 2:3], mvar[q][:, :],
                                                 ALU.add, ALU.mult).then_inc(sem("mlp_scaled"), 1)
                    else:
                        dve.tensor_tensor(mvar[q][:, :], mu[q][:, :], mvar[q][:, :], ALU.mult) \
                            .then_inc(sem("mlp_scaled"), 1)
            half(0, 0)
            half(0, 1)
            with dve.Fori(1, G // Q) as it:
                half(it, 0)
                half(it, 1)
            for q in range(Q):
                dve.wait_ge(sem(f"mlp_stored{q}"), 16 * (G // Q))

        DI = TT[:, :, :].rearrange("p t c -> p (t c)").bitcast(i32)
        cur, prv = DI[0:G, 0:2 * W], DI[0:G, 2 * W:4 * W]
        heads_i = DI[0:NP, 4 * W:4 * W + TILES]
        heads = SK[:, :, :].rearrange("p t c -> p (t c)")[:, 0:TILES]
        ZC = 3072
        less = R[:, :, :].rearrange("p t c -> p (t c)")
        rows_i = R[:, :, :].bitcast(i32)
        fbuf = O[0][0:G, :, :, :].rearrange("p c j f -> p (c j f)").bitcast(bf16)

        def setup_sp(sp):
            n = [0]

            def load(dst, src, name="setup_loaded"):
                n[0] += 16
                sp.dma_start(dst, src).then_inc(sem(name), 16)

            sp.wait_ge(sem("cleared"), 1)
            load(cst[:, :], a["consts"][:, :])
            d = a["dst_s"]
            for c in range(2):
                load(cur[:, W * c:W * c + W], d[c, 1:S + 1].rearrange("(g w) -> g w", w=W))
                load(prv[:, W * c:W * c + W], d[c, 0:S].rearrange("(g w) -> g w", w=W))
            load(heads_i, a["heads"].unsqueeze(0).to_broadcast([NP, TILES]))
            load(midd[:, :], a["mid"].unsqueeze(0).to_broadcast([64, 2]))
            load(X[:, :, :], a["x"].rearrange("(p t) c -> p t c", t=NT))
            load(wT[:, 0, :], a["w1t"][:, :])
            load(wT[:, 1, :], a["w2t"][:, :])
            col = lambda v: v.rearrange("(f a) -> f a", a=1)
            row = lambda v: v.rearrange("(a f) -> a f", a=1)
            for k, v in enumerate(["L0_gnn_a_src1", "L0_gnn_a_dst1", "L0_gnn_a_src2", "L0_gnn_a_dst2"]):
                load(avec[:, k:k + 1], col(a[v].rearrange("h c -> (h c)")))
            for k in (1, 2):
                w = wc[f"tc{k}"]
                for i, q in enumerate("kvqs"):
                    load(w[0:64, 64 * i:64 * i + 64], a[f"L1_gnn_{q}{k}_w"][:, :])
                    load(w[64:65, 64 * i:64 * i + 64], row(a[f"L1_gnn_{q}{k}_b"]))
                for c in range(2):
                    load(we[k - 1][DE * c:DE * c + DE, 64 * c:64 * c + 64], a[f"L1_gnn_e{k}_w"][:, :])
                load(bias[:, k - 1, :], a[f"L0_gnn_b{k}"].unsqueeze(0).to_broadcast([NP, 64]))
            load(skw[0:64, 0, :], a["L1_gnn_skip_w"][0:64, :])
            load(skw[0:64, 1, :], a["L1_gnn_skip_w"][64:128, :])
            load(skw[64:65, 1, :], row(a["L1_gnn_skip_b"]))
            for i, q in enumerate(["W2", "W3", "W1"]):
                load(wc["pt"][0:64, 64 * i:64 * i + 64], a[f"L2_gnn_{q}"][:, :])
            for c in range(2):
                load(wd1[3 * c:3 * c + 3, 64 * c:64 * c + 64], a["L2_gnn_Wd1"][:, :])
                load(wd1[6:7, 64 * c:64 * c + 64], row(a["L2_gnn_bd1"]))
                load(wd2[64 * c:64 * c + 64, 64 * c:64 * c + 64], a["L2_gnn_Wd2"][:, :])
                for i, q in enumerate(["g1", "b1", None, "g2", "b2"]):
                    if q:
                        load(pv4[64 * c:64 * c + 64, i:i + 1], col(a[f"L2_gnn_{q}"]))
                load(bd2row[:, 64 * c:64 * c + 64], row(a["L2_gnn_bd2"]))
            assert n[0] == 16 * LOADS, n[0] // 16
            sv = spread.rearrange("e f -> (e f)").rearrange("(p k z) -> p k z", p=128, z=2 * W)
            for k in range(EP * 64 // 128 // (2 * W)):
                sp.dma_start(sv[:, k, :], arg[:, :]).then_inc(sem("spread_zero"), 16)
            sp.wait_ge(sem("flags_made"), 1)
            for c in range(2):
                sp.dma_start(flags[:, c, :], fbuf[:, 2 * W * c:2 * W * c + 2 * W]).then_inc(sem("flags_out"), 16)
            sp.wait_ge(sem("starts_made"), 1)
            sp.dma_start(starts_d[0:N].rearrange("(p t) -> p t", t=NT), starts[:, :]).then_inc(sem("starts_out"), 16)
            sp.dma_start(starts_d[N:N + 1].unsqueeze(0), ecol[:, :]).then_inc(sem("starts_out"), 16)
            sp.wait_ge(sem("starts_out"), 32)
            sp.dma_start(endsn[:, :], starts_d[1:N + 1].rearrange("(p t) -> p t", t=NT)).then_inc(sem("ends_in"), 16)
            sp.wait_ge(sem("flags_out"), 32)
            sp.wait_ge(sem("spread_zero"), 16 * (EP * 64 // 128 // (2 * W)))

        LOADS = 5 + 1 + 1 + 2 + 1 + 4 + 2 * (8 + 2 + 1) + 3 + 3 + 2 * (1 + 1 + 1 + 4 + 1)
        bd2row = sb("bd2row", [1, 128])
        ecol = sb("ecol", [1, 1])

        def setup_pool(pool):
            pool.wait_ge(sem("tile_index"), 1)
            for t in range(NT):
                pool.indirect_dma_start(out=rows_i[:, t, :], out_offset=None, in_=a["dst_rows"][:, :],
                                        in_offset=on_axis0(idx_t[:, t:t + 1])).then_inc(sem("rows_in"), 16)

        def setup_pe(pe):
            pe.wait_ge(sem("amat_made"), 1)
            for k in range(2):
                pe.matmul(ps[6][0:64, 192 * k:192 * k + 192], wT[:, k, :], amat[:, k, :], start=True, stop=True) \
                    .then_inc(sem("gat_weights"), 1)
            pe.matmul(ps[7][:, 0:1], bd2row[:, :], cst[0:1, CI:CI + 1], start=True, stop=True) \
                .then_inc(sem("bd2_turned"), 1)

        def setup_dve(dve):
            c = dve_chain(dve)
            for t in (xT, h1T):
                dve.memset(t[64:65, :, :], 1.0)
            for t in mx:
                dve.memset(t[0:32, 0:W], 1.0)
            for t in (we[0], we[1], wd1, wd2):
                dve.memset(t[:, :], 0.0)
            for w in (wc["gat1"], wc["gat2"], wc["pt"]):
                dve.memset(w[64:65, :], 0.0)
            dve.memset(ecol[:, :], float(E))
            for s in (ex[U - 1], num[U - 1], den[U - 1], M[U - 1]):
                dve.memset(s[:, :], 0.0)
            dve.memset(mg[:, :], 0.0)
            dve.memset(epsc[:, :], EPS)
            c(dve.memset(arg[:, :], 0.0))
            dve.sem_inc(sem("cleared"), 1)
            dve.sem_inc(sem("mlp_ones"), 3)
            dve.wait_ge(sem("setup_loaded"), 16 * LOADS)
            for k in range(2):
                c(dve.tensor_copy(amat[:, k, 64:128], ident[0:64, 0:64]))
                for i in range(2):
                    block = amat[:, k, 128 * i:128 * i + 64]
                    mask = bones[0:64, 0:64] if k else hmask
                    c(dve.tensor_scalar(block, mask, avec[:, 2 * k + i:2 * k + i + 1], None, ALU.mult))
            c(dve.tensor_reduce(parity[:, 0:1], even[0:64, :], AX, ALU.add))
            c(dve.tensor_reduce(parity[:, 1:2], odd[0:64, :], AX, ALU.add))
            c(dve.tensor_scalar(bones8[:, :], bones, float(D) ** -0.5, None, ALU.mult))
            for t, p in ((wd1, 7), (wd2, 128), (bd2row, 1)):
                v = t[:, :].rearrange("p (c f) -> p c f", c=2)
                c(dve.tensor_reduce(mcol[0:p, :], v, AX, ALU.add))
                c(dve.tensor_scalar(mcol[0:p, :], mcol[0:p, :], -1.0 / D, None, ALU.mult))
                c(dve.tensor_tensor(v, v, mcol[0:p, :].unsqueeze(2).to_broadcast([p, 2, 64]), ALU.add))
            c(dve.tensor_scalar(wc["pt"][0:64, 0:64], wc["pt"][0:64, 0:64], -1.0, None, ALU.mult))
            dve.sem_inc(sem("amat_made"), 1)
            for k in range(2):
                dve.wait_ge(sem("gat_weights"), 2)
                c(dve.tensor_copy(wc[f"gat{k + 1}"][0:64, :], ps[6][0:64, 192 * k:192 * k + 192]))
            dve.wait_ge(sem("bd2_turned"), 1)
            c(dve.tensor_copy(pv4[:, 2:3], ps[7][:, 0:1]))
            dve.sem_inc(sem("mlp_ready"), 2)
            for k in range(2):
                f = fbuf[:, 2 * W * k:2 * W * k + 2 * W]
                c(dve.tensor_tensor(f[:, 0:W], cur[:, W * k:W * k + W], prv[:, W * k:W * k + W], ALU.is_equal))
                c(dve.tensor_scalar(f[:, W:2 * W], f[:, 0:W], -1.0, BIG, ALU.add, ALU.mult))
            dve.sem_inc(sem("flags_made"), 1)
            c(dve.tensor_tensor(cross[:, :], midd[:, 0:1], midd[:, 1:2], ALU.is_equal))
            c(dve.tensor_scalar(crossb[:, :], cross[:, :], -1.0, BIG, ALU.add, ALU.mult))
            c(dve.tensor_copy(heads, heads_i))
            for t in range(NT):
                c(dve.tensor_scalar(less[:, 0:TILES], heads, nid[:, t:t + 1], None, ALU.is_lt))
                c(dve.tensor_reduce(st1[0][:, t:t + 1], less[:, 0:TILES], AX, ALU.add))
            c(dve.tensor_scalar(st1[0][:, :], st1[0][:, :], -1.0, 0.0, ALU.add, ALU.max))
            c(dve.tensor_copy(idx_t[:, :], st1[0][:, :]))
            dve.sem_inc(sem("tile_index"), 1)
            dve.wait_ge(sem("rows_in"), 16 * NT)
            c(dve.tensor_copy(R[:, :, :], rows_i))
            c(dve.tensor_tensor(R[:, :, :], R[:, :, :], nid.unsqueeze(2).to_broadcast([NP, NT, 128]), ALU.is_lt))
            c(dve.tensor_reduce(starts[:, :], R[:, :, :], AX, ALU.add))
            c(dve.scalar_tensor_tensor(starts[:, :], st1[0][:, :], float(T), starts[:, :], ALU.mult, ALU.add))
            dve.sem_inc(sem("starts_made"), 1)
            dve.wait_ge(sem("ends_in"), 16)
            deg, t1, t2 = st1[1], st1[2], st1[3]
            c(dve.tensor_tensor(deg[:, :], endsn[:, :], starts[:, :], ALU.subtract))
            c(dve.tensor_scalar(has[:, :], deg[:, :], 0.0, None, ALU.is_gt))
            c(dve.tensor_scalar(st1[0][:, :], deg[:, :], 1.0, None, ALU.max))
            dve.sem_inc(sem("degrees"), 1)
            dve.wait_ge(sem("degree_root"), 1)
            c(dve.reciprocal(dinv[:, :], dinv[:, :]))
            c(dve.tensor_tensor(dinv[:, :], dinv[:, :], has[:, :], ALU.mult))
            c(dve.tensor_scalar(t1[:, :], endsn[:, :], -1.0, 0.0, ALU.add, ALU.max))
            c(dve.tensor_scalar(t1[:, :], t1[:, :], float(S - 1), None, ALU.min))
            c(dve.tensor_scalar(t2[:, :], starts[:, :], -1.0, float(3 * S - 1), ALU.mult, ALU.add))
            in_b = deg
            c(dve.tensor_scalar(in_b[:, :], starts[:, :], float(S), None, ALU.is_ge))
            c(dve.tensor_tensor(t2[:, :], t2[:, :], t1[:, :], ALU.subtract))
            c(dve.tensor_tensor(t2[:, :], t2[:, :], in_b[:, :], ALU.mult))
            c(dve.tensor_tensor(t1[:, :], t1[:, :], t2[:, :], ALU.add))
            c(dve.tensor_copy(idx_end[:, :], t1[:, :]))
            def place(out, value, keep):
                c(dve.tensor_tensor(keep, keep, has[:, :], ALU.mult))
                c(dve.tensor_scalar(value, value, -OOB, None, ALU.add))
                c(dve.tensor_tensor(value, value, keep, ALU.mult))
                c(dve.tensor_scalar(value, value, OOB, None, ALU.add))
                c(dve.tensor_copy(out[:, :], value))
            c(dve.tensor_copy(t1[:, :], starts[:, :]))
            c(dve.tensor_scalar(t2[:, :], starts[:, :], float(S), None, ALU.is_lt))
            place(idx_a, t1[:, :], t2[:, :])
            c(dve.tensor_scalar(t1[:, :], endsn[:, :], -1.0, float(3 * S), ALU.mult, ALU.add))
            c(dve.tensor_scalar(t2[:, :], endsn[:, :], float(S), None, ALU.is_gt))
            place(idx_b, t1[:, :], t2[:, :])
            dve.sem_inc(sem("gat1_features"), 2)

        def setup_act(act):
            act.wait_ge(sem("degrees"), 1)
            act.activation(dinv[:, :], st1[0][:, :], ACT.Sqrt).then_inc(sem("degree_root"), 1)

        block = ctx.enter_context(nc.Block())

        @block.sync
        def _(sp):
            setup_sp(sp)
            mlp_sp(sp)
            for kind in KINDS:
                if kind in SOFT:
                    tables_sp(sp, kind)
                else:
                    sp.wait_ge(sem(f"{kind}_features"), 1)
                    sp.dma_start(table3.rearrange("(p t) c -> p t c", t=NT), SK[:, :, :]) \
                        .then_inc(sem("tables_written"), 16)
                if kind == "pt":
                    for q in range(Q):
                        sp.wait_ge(sem(f"mlp_stored{q}"), 16 * (G // Q))
                pass_sp(sp, kind)
                merge_sp(sp, kind)
            sp.wait_ge(sem("out_features"), 1)
            sp.dma_start(a["out"].rearrange("(p t) c -> p t c", t=NT), X[:, :, :]).then_inc(sem("written"), 16)
            sp.wait_ge(sem("written"), 16)

        @block.gpsimd
        def _(pool):
            setup_pool(pool)
            pool.wait_ge(sem("gat1_features"), 2)
            pool.wait_ge(sem("spread_zero"), 16 * (EP * 64 // 128 // (2 * W)))
            for kind in KINDS:
                if kind in SOFT:
                    scatter_pool(pool, kind)
                pass_pool(pool, kind)
                take_pool(pool, kind)

        @block.tensor
        def _(pe):
            setup_pe(pe)
            mlp_pe(pe)
            pe.wait_ge(sem("mlp_scaled"), 2 * G)
            for kind in KINDS:
                if kind in SOFT:
                    tables_pe(pe, kind, *node_in[kind])
                (pass_pe if kind in SOFT else sum_pe)(pe, kind)
                post_pe(pe, kind)

        @block.vector
        def _(dve):
            setup_dve(dve)
            mlp_dve(dve)
            for kind in KINDS:
                if kind in SOFT:
                    tables_dve(dve, kind)
                (pass_dve if kind in SOFT else sum_dve)(dve, kind)
                post_dve(dve, kind)

        @block.scalar
        def _(act):
            setup_act(act)
            mlp_act(act)
            for kind in KINDS:
                if kind in SOFT:
                    turn_nodes_act(act, kind, node_in[kind][1], "x")
                pass_act(act, kind)
                post_act(act, kind)


WEIGHTS = (["L0_gnn_" + w for w in ("a_src1", "a_dst1", "b1", "a_src2", "a_dst2", "b2")]
           + [f"L1_gnn_{w}{k}_{p}" for k in (1, 2) for w in "qkvs" for p in "wb"]
           + ["L1_gnn_e1_w", "L1_gnn_e2_w", "L1_gnn_skip_w", "L1_gnn_skip_b"]
           + ["L2_gnn_" + w for w in ("Wd1", "bd1", "g1", "b1", "Wd2", "bd2", "g2", "b2", "W1", "W2", "W3")])


def lay_out(inputs):
    f = {k: np.asarray(v) for k, v in inputs.items()}

    def streams(v, pad):
        v = np.concatenate([v, np.full((EP - E,) + v.shape[1:], pad, v.dtype)])
        return np.stack([v[:S], v[S:][::-1]])

    src = streams(f["src"], 0).reshape(2, G, J, T)
    dst = np.concatenate([f["dst"], np.full(EP - E, N, f["dst"].dtype)])
    both = streams(f["dst"], N)
    arrays = {
        "x": f["x"],
        "consts": shape_constants(),
        "src_g": np.ascontiguousarray(src.transpose(1, 3, 0, 2).reshape(G, T, 2 * J)),
        "dst_s": np.ascontiguousarray(np.concatenate([np.full((2, 1), -1, both.dtype), both], 1)),
        "dst_rows": dst.reshape(TILES, T),
        "heads": np.ascontiguousarray(dst[::T]),
        "mid": np.ascontiguousarray(dst[S - 1:S + 1]),
        "w1t": np.ascontiguousarray(f["L0_gnn_W1"].T),
        "w2t": np.ascontiguousarray(f["L0_gnn_W2"].T),
    }
    for name, key, k in (("ea32", "edge_attr_32", DE), ("ea3", "edge_attr_3", 3)):
        v = streams(f[key], 0).reshape(2, G, W, k)
        arrays[name] = np.ascontiguousarray(v.transpose(1, 0, 3, 2).reshape(G, 2 * k, W))
    for w in WEIGHTS:
        arrays[w] = f[w]
    return arrays


def kernel(**inputs):
    import concourse.bacc as bacc
    from concourse.bass_utils import run_bass_kernel_spmd

    nc = bacc.Bacc("TRN2", target_bir_lowering=False, num_devices=1)
    arrays = lay_out(inputs)
    a, feeds = {}, {}
    for name, v in arrays.items():
        feeds[f"in_{name}"] = v
        a[name] = nc.dram_tensor(f"in_{name}", v.shape, mybir.dt.from_np(v.dtype), kind="ExternalInput").ap()
    a["out"] = nc.dram_tensor("out_0", (N, D), mybir.dt.float32, kind="ExternalOutput").ap()
    build(nc, a)
    r = run_bass_kernel_spmd(nc, [feeds], core_ids=[0])
    return r.results[0]["out_0"]
```

```python
import numpy as np
import concourse.bass as bass
from concourse import mybir
from contextlib import ExitStack

N, E, D = 3125, 103125, 64
NP, NT = 125, 25
T = 128
J = 4
W = J * T
G = 102
U = 3
B = 6
assert B % U == 0 and G % B == 0
S = G * W
EP = 2 * S
TILES = EP // T
BIG = 1.0e30
OOB = 1.0e6
EPS = 1e-5
DE = 32

MLP_IN = ["gat1", "gat2"]
PARTS = [(0, 9), (9, 8), (17, 8)]
P = len(PARTS)

KINDS = ["gat1", "gat2", "tc1", "tc2", "pt", "gc1", "gc2"]

CI, CB, CM, CN = 0, 128, 256, 320
CE, CO = CN + NT, CN + NT + 128
CW = CO + 128


def shape_constants():
    c = np.zeros((128, CW), np.float32)
    c[:, CI:CI + 128] = np.eye(128)
    c[:64, CB:CB + 64] = 1
    c[64:, CB + 64:CB + 128] = 1
    for k in range(2):
        c[k::2, CE + 128 * k:CE + 128 * k + 128] = np.eye(128)[k::2]
    f = np.arange(64)
    c[:64, CM:CM + 64] = f[:, None] // 16 == f[None, :] // 16
    c[:NP, CN:CN + NT] = np.arange(N).reshape(NP, NT)
    return c


def build(nc, a):
    f32, bf16, i32 = mybir.dt.float32, mybir.dt.bfloat16, mybir.dt.int32
    ALU, ACT, AX = mybir.AluOpType, mybir.ActivationFunctionType, mybir.AxisListType.X
    ds = bass.ds
    on_axis0 = lambda ap: bass.IndirectOffsetOnAxis(ap=ap, axis=0)
    ctx = ExitStack()

    def sb(name, shape, dt=f32):
        return ctx.enter_context(nc.sbuf_tensor(name, shape, dt))

    def dram(name, shape, dt=f32):
        return nc.dram_tensor(name, shape, dt, kind="Internal").ap()

    sems = {}

    def sem(name):
        if name not in sems:
            sems[name] = ctx.enter_context(nc.semaphore(name))
        return sems[name]

    def need(eng, name, value):
        if not isinstance(value, int) or value > 0:
            eng.wait_ge(sem(name), value)

    with ctx:
        table = dram("table", [N, 128])
        table3 = dram("table3", [N, 64])
        spread = dram("spread", [EP, 64])
        flags = dram("flags", [G, 2, 2 * W], bf16)
        ends = dram("ends", [EP, 128])
        ends3 = dram("ends3", [EP, 64])
        dist = dram("dist", [G, 128, W])
        starts_d = dram("starts_d", [N + 1])
        targets = dram("targets", [N, 64])

        cst = sb("cst", [128, CW])
        ident, bones = cst[:, CI:CI + 128], cst[:, CB:CB + 128]
        bones8 = sb("bones8", [128, 128])
        hmask, nid = cst[0:64, CM:CM + 64], cst[0:NP, CN:CN + NT]
        even, odd = cst[:, CE:CE + 128], cst[:, CO:CO + 128]
        X = sb("X", [NP, NT, D])
        H = sb("H", [NP, NT, D])
        scratch = [sb(f"scratch{i}", [128, NT, D]) for i in range(3)]
        tmp, SK = [t[0:NP] for t in scratch[0:2]], scratch[2][0:NP]
        TT = sb("TT", [128, NT, 256])
        R = sb("R", [NP, NT, 128])
        R3 = R[:, :, 0:64]
        xT = sb("xT", [65, NT, NP])
        h1T = sb("h1T", [65, NT, NP])
        starts = sb("starts", [NP, NT])
        endsn = sb("endsn", [NP, NT])
        has = sb("has", [NP, NT])
        dinv = sb("dinv", [NP, NT])
        st1 = [sb(f"st{i}", [NP, NT]) for i in range(4)]
        idx_end = sb("idx_end", [NP, NT], i32)
        idx_first = sb("idx_first", [NP, NT], i32)
        idx_cross = sb("idx_cross", [2, 3], i32)
        cross_end = sb("cross_end", [2, 1])
        cross_row = sb("cross_row", [2, 64])
        idx_t = sb("idx_t", [NP, NT], i32)
        midd = sb("midd", [64, 2], i32)
        cross = sb("cross", [64, 1])
        crossb = sb("crossb", [64, 1])
        wc = {"gat1": sb("wc_gat1", [65, 192]), "gat2": sb("wc_gat2", [65, 192]),
              "tc1": sb("wc_tc1", [65, 256]), "tc2": sb("wc_tc2", [65, 256]), "pt": sb("wc_pt", [65, 192])}
        wT = sb("wT", [64, 2, 64])
        avec = sb("avec", [64, 4])
        amat = sb("amat", [64, 2, 192])
        skw = sb("skw", [65, 2, 64])
        we = [sb(f"we{i}", [64, 128]) for i in range(2)]
        bias = sb("bias", [NP, 2, 64])
        wd1 = sb("wd1", [7, 128])
        wd2 = sb("wd2", [128, 128])
        pv4 = sb("pv4", [128, 6])
        mcol = sb("mcol", [128, 2])
        epsc = sb("epsc", [128, 1])
        Gt = [sb(f"Gt{i}", [128, J, 2, 128]) for i in range(U)]
        ix = [sb(f"ix{i}", [128, 2 * J], i32) for i in range(U)]
        xd = [sb(f"xd{i}", [128, J, 2, 64]) for i in range(U)]
        fl = [sb(f"fl{i}", [128, 2 * W], bf16) for i in range(U)]
        ea = [sb(f"ea{i}", [128, W]) for i in range(U)]
        ex = [sb(f"ex{i}", [128, W]) for i in range(U)]
        sr = sb("sr", [128, W])
        sl = sb("sl", [128, W])
        M = [sb(f"M{i}", [128, W + 1]) for i in range(U)]
        arg = sb("arg", [128, 2 * W])
        ap = sb("ap", [128, 2 * W])
        pv = sb("pv", [128, W])
        num = [sb(f"num{i}", [128, W]) for i in range(U)]
        den = [sb(f"den{i}", [128, W]) for i in range(U)]
        O = [sb(f"O{i}", [128, 2, J, 128]) for i in range(U)]
        mg = sb("mg", [128, 3])
        mgb = sb("mgb", [64, 3])
        mw = sb("mw", [64, 6])
        parity = sb("parity", [64, 2])

        ps = [ctx.enter_context(nc.psum_tensor(f"ps{i}", [128, 512], f32)) for i in range(8)]
        pX, pS, pV, pR, pN, pD = ps[0], ps[1], ps[2:5], ps[5], ps[6], ps[7]

        flat = lambda t: t.rearrange("p t c -> p (t c)")
        bc = lambda t: t.unsqueeze(2).to_broadcast([NP, t.shape[1], 64])

        class Chain:

            def __init__(self, name):
                self.eng, self.sem, self.n = None, sem(name), 0

            def __call__(self, instruction):
                self.n += 1
                instruction.then_inc(self.sem, 1)
                self.eng.wait_ge(self.sem, self.n)

        node_chain = Chain("vector_chain")

        def dve_chain(dve):
            node_chain.eng = dve
            return node_chain

        MG = G // 2
        LAG = 7
        K = 2 * J
        BATCHES = G // U + 1
        LATE = [m for m in range(G, 2 * (MG - 1) + LAG + 1) if m % 2]
        assert MG % U == 0 and len(LATE) == U and LAG >= 2 * U + 1
        mu = mspread = pR
        mv = pV[2][:, 0:U * K]
        rootT = pV[2][0:U * K, 128:256]
        parts = lambda t: [t[:, :, :].rearrange("p t c -> p (t c)")[:, W * j:W * j + W] for j in range(3)]
        ring = parts(scratch[0]) + parts(scratch[1])
        first = parts(scratch[2])
        second = [t[:, :] for t in ea]
        early = h1T[0:64, :, :].rearrange("p t c -> p (t c)")
        mx = [early[0:7, W * j:W * j + W] for j in range(U)]
        picks = early[0:U * K, U * W:U * W + 64 * U * K]
        msq = sb("msq", [128, W])
        root = sb("root", [128, U * K])
        roots = sb("roots", [U * K, 128])

        def mlp_here(it, m):
            return m >= 0 and (not isinstance(it, int) or m in LATE or (m < G and not (m % 2 and m < LAG)))

        def mlp_before(kind, it, m):
            m = m // 2 if m < LAG else G - U + LATE.index(m) if m in LATE else m - U
            return G * order(kind) + B * it + m

        def mlp_done(kind, it, m):
            return mlp_before(kind, it, m) + 1

        def mlp_group(it, m):
            return (m - LAG * (m % 2)) // 2

        def mlp_lap(kind, it, b):
            return MG // U * order(kind) + it + b // U

        def batch_before(kind, it, i):
            return BATCHES * order(kind) + B // U * it + i

        def batch_layers(it, i):
            return LATE if i == BATCHES - 1 else [m for m in range(U * i, U * i + U) if mlp_here(it, m)]

        def batch_columns(m):
            return (BATCHES - 1, K * LATE.index(m)) if m in LATE else (m // U, K * (m % U))

        def mlp_load(sp, kind, it, c):
            b = c // 2
            q = b % U
            if b >= U or order(kind) > 0:
                sp.wait_ge(sem("mlp_products"), mlp_done(kind, it, c - 2 * U))
            g = MG * order(kind) + B // 2 * it + b
            sp.dma_start(mx[q][0:6, :], a["ea3"][ds(g, 1), :, :].rearrange("a p j -> p (a j)")) \
                .then_inc(sem(f"mlp_in{q}"), 16)

        def mlp_product(pe, kind, it, m):
            b = mlp_group(it, m)
            if m % 2:
                pe.wait_ge(sem("mlp_gelus"), mlp_done(kind, it, m - LAG))
                w, x = wd2[:, :], first[b % U]
            else:
                pe.wait_ge(sem(f"mlp_in{b % U}"), 16 * (mlp_lap(kind, it, b) + 1))
                w, x = wd1[:, :], mx[b % U]
            need(pe, "mlp_kept", mlp_before(kind, it, m))
            pe.matmul(mu[:, :], w, x, start=True, stop=True).then_inc(sem("mlp_products"), 1)

        def mlp_keep(act, kind, it, m):
            act.wait_ge(sem("mlp_products"), mlp_done(kind, it, m))
            u = ring[m % (2 * U)]
            if m >= 2 * U:
                act.wait_ge(sem("mlp_gelus"), mlp_done(kind, it, last_layer(it, m - 2 * U)))
            act.activation(u, mu[:, :], ACT.Identity, bias=pv4[:, 2 if m % 2 else 5:3 if m % 2 else 6]) \
                .then_inc(sem("mlp_kept"), 1)
            act.wait_ge(sem("mlp_kept"), mlp_done(kind, it, m))
            need(act, "mlp_variances", mlp_before(kind, it, m))
            act.activation(msq[:, :], u, ACT.Square).then_inc(sem("mlp_squared"), 1)

        def mlp_variance(pe, kind, it, m):
            i, column = batch_columns(m)
            pe.wait_ge(sem("mlp_squared"), mlp_done(kind, it, m))
            need(pe, "mlp_logged", batch_before(kind, it, i))
            need(pe, "mlp_roots_kept", batch_before(kind, it, i) - (m < G and m % U == 0))
            for j in range(J):
                last = pe.matmul(mv[:, column + 2 * j:column + 2 * j + 2], msq[:, T * j:T * j + T],
                                 bones[:, 0:128:64], start=True, stop=True)
            last.then_inc(sem("mlp_variances"), 1)

        def batch_logs(act, kind, it, i):
            n = batch_before(kind, it, i)
            act.wait_ge(sem("mlp_variances"), mlp_done(kind, it, batch_layers(it, i)[-1]))
            need(act, "mlp_roots_turned", n)
            act.activation(root[:, :], mv, ACT.Ln, bias=epsc[:, :], scale=1.0 / D).then_inc(sem("mlp_logged"), 1)

        def batch_roots(act, kind, it, i):
            act.wait_ge(sem("mlp_logged"), batch_before(kind, it, i) + 1)
            act.activation(root[:, :], root[:, :], ACT.Exp, scale=-0.5).then_inc(sem("mlp_rooted"), 1)

        def batch_turn(pe, kind, it, i):
            n = batch_before(kind, it, i)
            pe.wait_ge(sem("mlp_rooted"), n + 1)
            need(pe, "mlp_roots_kept", n)
            pe.transpose(rootT, root[:, :], ident).then_inc(sem("mlp_roots_turned"), 1)

        def batch_keep(dve, kind, it, i):
            dve.wait_ge(sem("mlp_roots_turned"), batch_before(kind, it, i) + 1)
            need(dve, "mlp_spread", mlp_before(kind, it, batch_layers(it, i)[0]))
            dve.tensor_copy(roots[:, :], rootT).then_inc(sem("mlp_roots_kept"), 1)

        def mlp_spread(pe, kind, it, m, product):
            i, row = batch_columns(m)
            pe.wait_ge(sem("mlp_roots_kept"), batch_before(kind, it, i) + 1)
            pe.wait_ge(sem("mlp_kept"), mlp_done(kind, it, product))
            need(pe, "mlp_scaled", mlp_before(kind, it, m))
            for j in range(J):
                r = row + 2 * j
                last = pe.matmul(mspread[:, T * j:T * j + T], picks[:, 64 * r:64 * r + 128], roots[:, :],
                                 start=True, stop=True)
            last.then_inc(sem("mlp_spread"), 1)

        def mlp_scale(dve, kind, it, m):
            u = ring[m % (2 * U)]
            dve.wait_ge(sem("mlp_spread"), mlp_done(kind, it, m))
            dve.tensor_tensor(u, u, mspread[:, :], ALU.mult).then_inc(sem("mlp_scaled"), 1)

        def mlp_gelus(act, kind, it, i):
            layers = batch_layers(it, i)
            for m in layers:
                b, k = mlp_group(it, m), m % 2
                act.wait_ge(sem("mlp_scaled"), mlp_done(kind, it, m))
                if k and (b >= U or order(kind) > 0):
                    act.wait_ge(sem(f"mlp_stored{b % U}"), 16 * mlp_lap(kind, it, b))
                act.activation((second if k else first)[b % U], ring[m % (2 * U)], ACT.Gelu,
                               scale=pv4[:, 3 * k:3 * k + 1], bias=pv4[:, 1 + 3 * k:2 + 3 * k]) \
                    .then_inc(sem("mlp_gelus"), 1)

        def mlp_stores(act, kind, it, i):
            for m in batch_layers(it, i):
                if m % 2:
                    b = mlp_group(it, m)
                    act.wait_ge(sem("mlp_gelus"), mlp_done(kind, it, m))
                    act.dma_start(dist[ds(MG * order(kind) + B // 2 * it + b, 1), :, :]
                                  .rearrange("a p j -> p (a j)"), second[b % U]) \
                        .then_inc(sem(f"mlp_stored{b % U}"), 16)

        def spread_at(it, c, place):
            m = c - 5 if c % U == 2 and place == 0 else c - 4 if c % U == 2 or (c % U == 0 and place == 0) else -1
            return m if mlp_here(it, m) else None

        def last_layer(it, m):
            while not mlp_here(it, m):
                m -= 1
            return m

        def mlp_step_pe(pe, kind, it, c, place):
            if place == 1 and c > 0 and mlp_here(it, c - 1):
                mlp_variance(pe, kind, it, c - 1)
            if spread_at(it, c, place) is not None:
                mlp_spread(pe, kind, it, spread_at(it, c, place), last_layer(it, c - 1))
            if place == 1 and mlp_here(it, c):
                if c > 2 * U - 1:
                    m = last_layer(it, c - 5 if c % U == 1 else c - 4)
                    pe.wait_ge(sem("mlp_scaled"), mlp_done(kind, it, m))
                mlp_product(pe, kind, it, c)

        def mlp_step_act(act, kind, it, c):
            if c % U == 0 and c > U:
                mlp_gelus(act, kind, it, c // U - 2)
            if c % U == 0 and c > 0:
                batch_logs(act, kind, it, c // U - 1)
            if mlp_here(it, c):
                mlp_keep(act, kind, it, c)
            if c % U == 0 and c > 0:
                batch_roots(act, kind, it, c // U - 1)
            if c % U == 1 and c > 2 * U:
                mlp_stores(act, kind, it, c // U - 2)

        def mlp_step_dve(dve, kind, it, c, place):
            if c % U == 2 and c > U and place == 0:
                batch_keep(dve, kind, it, c // U - 1)
            m = c - 5 if (c % U, place) in ((0, 0), (2, 1)) else c - 4 if (c % U, place) == (0, 2) else -1
            if mlp_here(it, m):
                mlp_scale(dve, kind, it, m)

        def mlp_tail_pe(pe, kind):
            full = G // U - 1
            mlp_variance(pe, kind, 0, G - 1)
            mlp_spread(pe, kind, 0, G - U - 1, G - 1)
            batch_turn(pe, kind, 0, full)
            for m in batch_layers(0, full):
                mlp_spread(pe, kind, 0, m, G - 1)
            pe.wait_ge(sem("mlp_scaled"), mlp_done(kind, 0, G - 1))
            for m in LATE:
                mlp_product(pe, kind, 0, m)
                mlp_variance(pe, kind, 0, m)
            batch_turn(pe, kind, 0, full + 1)
            for m in LATE:
                mlp_spread(pe, kind, 0, m, LATE[-1])

        def mlp_tail_act(act, kind):
            full = G // U - 1
            batch_logs(act, kind, 0, full)
            batch_roots(act, kind, 0, full)
            for i in (full - 1, full):
                mlp_gelus(act, kind, 0, i)
                mlp_stores(act, kind, 0, i)
            for m in LATE:
                mlp_keep(act, kind, 0, m)
            batch_logs(act, kind, 0, full + 1)
            batch_roots(act, kind, 0, full + 1)
            mlp_gelus(act, kind, 0, full + 1)
            mlp_stores(act, kind, 0, full + 1)

        def mlp_tail_dve(dve, kind):
            full = G // U - 1
            mlp_scale(dve, kind, 0, G - U - 1)
            for i in (full, full + 1):
                batch_keep(dve, kind, 0, i)
                for m in batch_layers(0, i):
                    mlp_scale(dve, kind, 0, m)
            for q in range(U):
                dve.wait_ge(sem(f"mlp_stored{q}"), 16 * (MG // U) * (order(kind) + 1))


        def order(kind):
            return KINDS.index(kind)

        def base(kind):
            return G * (int(kind[-1]) - 1) if kind.startswith("gc") else G * order(kind)

        def count(kind, it, c):
            return base(kind) + B * it + c + 1

        def lap(it, c):
            return B // U * it + c // U

        def head(kind):
            return 3 * B if kind in MLP_IN else B

        def rows_merged(kind):
            return sum(1 if k.startswith("gc") else 2 for k in KINDS[:order(kind) + 1])

        def nload(kind):
            return 2 if kind.startswith("gc") else 4 if kind.startswith("gat") else 5

        def loads_before(kind):
            return 16 * (G // U) * sum(nload(k) for k in KINDS[:order(kind)])

        def uses(kind, it, c):
            return (G // U) * order(kind) + lap(it, c)

        def walk(eng, step, head=B):
            for c in range(head):
                step(0, c, c == 0, False)
            with eng.Fori(0, (G - B - head) // B) as it:
                for c in range(head, head + B):
                    step(it, c, False, False)
            for c in range(G - B, G):
                step(0, c, False, c == G - 1)

        def pass_sp(sp, kind):
            gc = kind.startswith("gc")

            def load_indices(it, c):
                s = c % U
                need(sp, f"{kind}_gathered{s}", 2 * J * 16 * lap(it, c))
                sp.dma_start(ix[s][:, :], a["src_g"][ds(B * it + c, 1), :, :].rearrange("a p j -> p (a j)")) \
                    .then_inc(sem(f"indices{s}"), 16)

            for c in range(U):
                load_indices(0, c)
            if not gc:
                sp.wait_ge(sem(f"{kind}_spread"), 16 * (NT + 1))

            def step(it, c, first, last):
                s = c % U
                g = B * it + c
                n = count(kind, it, c)
                if kind in MLP_IN and c % 2 == 0:
                    mlp_load(sp, kind, it, c)
                if c >= U:
                    load_indices(it, c)
                loaded = sem(f"loaded{s}")
                if gc:
                    need(sp, "gc_summed", n - U)
                    for h in range(2):
                        sp.dma_start(fl[s][64 * h:64 * h + 64, 0:W],
                                     flags[ds(g, 1), h, 0:W].to_broadcast([64, W])).then_inc(loaded, 16)
                    return
                need(sp, "shifted", n - U)
                need(sp, "values_turned", n - U)
                for h in range(2):
                    sp.dma_start(fl[s][64 * h:64 * h + 64, :], flags[ds(g, 1), h, :].to_broadcast([64, 2 * W])) \
                        .then_inc(loaded, 16)
                sv = spread.rearrange("(c g j p) f -> c g p j f", c=2, g=G, j=J)
                for h in range(2):
                    sp.dma_start(xd[s][:, :, h, :], sv[h, ds(g, 1)].rearrange("a p j f -> p (a j) f")) \
                        .then_inc(loaded, 16)
                if kind in ("tc1", "tc2"):
                    sp.dma_start(ea[s][0:64, :], a["ea32"][ds(g, 1), :, :].rearrange("a p j -> p (a j)")) \
                        .then_inc(loaded, 16)
                if kind == "pt":
                    sp.dma_start(ea[s][:, :], dist[ds(g, 1), :, :].rearrange("a p j -> p (a j)")) \
                        .then_inc(loaded, 16)

            walk(sp, step, head(kind))

        def pass_pool(pool, kind):
            gc = kind.startswith("gc")
            pool.wait_ge(sem("tables_written"), 16 * P * (order(kind) + 1))

            def step(it, c, first, last):
                s = c % U
                pool.wait_ge(sem(f"indices{s}"), 16 * (uses(kind, it, c) + 1))
                need(pool, "gc_turned" if gc else "values_turned", count(kind, it, c) - U)
                if not isinstance(it, int):
                    pool.nop(nofuse=True)
                for h in range(2):
                    for j in range(J):
                        k = h * J + j
                        src = table3 if gc else table
                        to = Gt[s][:, j, 0, 64 * h:64 * h + 64] if gc else Gt[s][:, j, h, :]
                        pool.indirect_dma_start(out=to, out_offset=None, in_=src[:, :],
                                                in_offset=on_axis0(ix[s][:, k:k + 1])) \
                            .then_inc(sem(f"{kind}_gathered{s}"), 16)
                if first and not gc:
                    scatter_crossing(pool, kind)

            walk(pool, step, head(kind))

        def pass_pe(pe, kind):
            gat = kind.startswith("gat")
            edge = None if gat else ident if kind == "pt" else we[int(kind == "tc2")]
            ek = 128 if kind == "pt" else 64

            VS = 2 if gat else U

            def turn(out, s, half, signal):
                if edge is not None:
                    pe.matmul(out[:, :], edge[0:ek, :], ea[s][0:ek, :], start=True, stop=False)
                for j in range(J):
                    rows = Gt[s][:, j, :, :].rearrange("p c f -> p (c f)")[:, half:256:2]
                    cols = out[:, T * j:T * j + T]
                    if edge is None:
                        last = pe.transpose(cols, rows, ident)
                    else:
                        last = pe.matmul(cols, rows, ident, start=False, stop=(j == J - 1))
                last.then_inc(sem(signal), 1)

            def turn_targets(it, c):
                s = c % U
                n = count(kind, it, c)
                pe.wait_ge(sem(f"loaded{s}"), loads_before(kind) + 16 * nload(kind) * (lap(it, c) + 1))
                need(pe, "spread_out", n - 1)
                for j in range(J):
                    last = pe.transpose(pX[:, T * j:T * j + T],
                                        xd[s][:, j, :, :].rearrange("p c f -> p (c f)"), ident)
                last.then_inc(sem("targets_turned"), 1)

            def turn_sources(it, c):
                s = c % U
                n = count(kind, it, c)
                pe.wait_ge(sem(f"{kind}_gathered{s}"), 2 * J * 16 * (lap(it, c) + 1))
                need(pe, "combined", n - 1)
                turn(pS, s, 0, "logits_turned")
                need(pe, "weighed", n - VS)
                turn(pV[c % VS], s, 1, "values_turned")

            def score(it, c):
                s = c % U
                n = count(kind, it, c)
                pe.wait_ge(sem("combined"), n)
                need(pe, "arguments", n - 1)
                pe.matmul(pR[:, :], bones8[:, :], sr[:, :], start=True, stop=True).then_inc(sem("scored"), 1)

            def turn_back(it, c):
                s = c % U
                n = count(kind, it, c)
                pe.wait_ge(sem("denominated"), n)
                need(pe, "evacuated", n - 1)
                for j in range(J):
                    out, part = pD[:, T * j:T * j + T], den[s][:, T * j:T * j + T]
                    if gat:
                        pe.matmul(out, part, even, start=True, stop=False)
                        pe.matmul(out, M[s][:, T * j + 1:T * j + T + 1], odd, start=False, stop=True)
                    else:
                        pe.transpose(out, part, ident)
                pe.wait_ge(sem("numerated"), n)
                for j in range(J):
                    last = pe.transpose(pN[:, T * j:T * j + T], num[s][:, T * j:T * j + T], ident)
                last.then_inc(sem("turned_back"), 1)

            def step(it, c, first, last):
                s = c % U
                if kind in ("tc1", "tc2"):
                    score(it, c)
                if gat and c % U == 2 and c > U:
                    batch_turn(pe, kind, it, c // U - 1)
                if not last:
                    turn_sources(it, c + 1)
                if c + 2 < G:
                    turn_targets(it, c + 2)
                if gat:
                    mlp_step_pe(pe, kind, it, c, 0)
                if not first:
                    turn_back(it, c - 1)
                if gat:
                    mlp_step_pe(pe, kind, it, c, 1)

            turn_targets(0, 0)
            turn_sources(0, 0)
            turn_targets(0, 1)
            walk(pe, step, head(kind))
            turn_back(0, G - 1)
            if gat:
                mlp_tail_pe(pe, kind)

        def sum_pe(pe, kind):
            def turn_back(it, c):
                s = c % U
                n = count(kind, it, c)
                pe.wait_ge(sem("gc_summed"), n)
                need(pe, "gc_evacuated", n - 1)
                for j in range(J):
                    last = pe.transpose(pN[:, T * j:T * j + T], num[s][:, T * j:T * j + T], ident)
                last.then_inc(sem("gc_back"), 1)

            def step(it, c, first, last):
                s = c % U
                n = count(kind, it, c)
                pe.wait_ge(sem(f"{kind}_gathered{s}"), 2 * J * 16 * (lap(it, c) + 1))
                need(pe, "gc_summed", n - U)
                for j in range(J):
                    turned = pe.transpose(pV[s][:, T * j:T * j + T], Gt[s][:, j, 0, :], ident)
                turned.then_inc(sem("gc_turned"), 1)
                if not first:
                    turn_back(it, c - 1)

            walk(pe, step)
            turn_back(0, G - 1)

        def merge_states(dve, kind, gc):
            chain = dve_chain(dve)
            if gc:
                dve.wait_ge(sem("gc_summed"), base(kind) + G)
                chain(dve.tensor_copy(mg[:, 1:2], num[U - 1][:, W - 1:W]))
            else:
                dve.wait_ge(sem("numerated"), base(kind) + G)
                dve.wait_ge(sem("denominated"), base(kind) + G)
                chain(dve.tensor_copy(mg[:, 0:1], M[U - 1][:, W:W + 1]))
                chain(dve.tensor_copy(mg[:, 1:2], num[U - 1][:, W - 1:W]))
                chain(dve.tensor_copy(mg[:, 2:3], den[U - 1][:, W - 1:W]))
            dve.sem_inc(sem("last"), 1)
            dve.wait_ge(sem("moved"), 16 * (order(kind) + 1))
            if gc:
                chain(dve.scalar_tensor_tensor(mw[:, 4:5], mgb[:, 1:2], cross[:, 0:1], mg[0:64, 1:2],
                                               ALU.mult, ALU.add))
            else:
                chain(dve.tensor_tensor(mw[:, 0:1], mgb[:, 0:1], crossb[:, :], ALU.add))
                chain(dve.tensor_tensor(mw[:, 1:2], mw[:, 0:1], mg[0:64, 0:1], ALU.max))
                chain(dve.tensor_tensor(mw[:, 2:3], mg[0:64, 0:1], mw[:, 1:2], ALU.subtract))
                chain(dve.tensor_tensor(mw[:, 3:4], mw[:, 0:1], mw[:, 1:2], ALU.subtract))
                dve.sem_inc(sem("merge_arg"), 1)
                dve.wait_ge(sem("merge_exp"), order(kind) + 1)
                chain(dve.tensor_tensor(mgb[:, 1:2], mgb[:, 1:2], mw[:, 3:4], ALU.mult))
                chain(dve.tensor_tensor(mgb[:, 2:3], mgb[:, 2:3], mw[:, 3:4], ALU.mult))
                chain(dve.scalar_tensor_tensor(mw[:, 4:5], mg[0:64, 1:2], mw[:, 2:3], mgb[:, 1:2],
                                               ALU.mult, ALU.add))
                chain(dve.scalar_tensor_tensor(mw[:, 5:6], mg[0:64, 2:3], mw[:, 2:3], mgb[:, 2:3],
                                               ALU.mult, ALU.add))
                if kind.startswith("gat"):
                    chain(dve.tensor_tensor(mw[:, 5:6], mw[:, 5:6], parity[:, 0:1], ALU.mult))
                    chain(dve.scalar_tensor_tensor(mw[:, 5:6], mw[:, 1:2], parity[:, 1:2], mw[:, 5:6],
                                                   ALU.mult, ALU.add))
            dve.sem_inc(sem("merged"), 1)

        def sum_dve(dve, kind):
            def step(it, c, first, last):
                s = c % U
                n = count(kind, it, c)
                dve.wait_ge(sem(f"loaded{s}"), loads_before(kind) + 16 * nload(kind) * (lap(it, c) + 1))
                dve.wait_ge(sem("gc_turned"), n)
                need(dve, "gc_back", n - U)
                need(dve, "gc_summed", n - 1)
                dve.tensor_tensor_scan(num[s][:, :], fl[s][:, 0:W], pV[s][:, :], num[s - 1][:, W - 1:W],
                                       ALU.mult, ALU.add).then_inc(sem("gc_summed"), 1)

            walk(dve, step)
            merge_states(dve, kind, True)

        def pass_dve(dve, kind):
            tc, gat = kind in ("tc1", "tc2"), kind.startswith("gat")
            logit = pR if tc else sl if gat else sr

            def spread_targets(it, c):
                s = c % U
                n = count(kind, it, c)
                dve.wait_ge(sem("targets_turned"), n)
                dve.wait_ge(sem(f"loaded{s}"), loads_before(kind) + 16 * nload(kind) * (lap(it, c) + 1))
                dve.tensor_tensor_scan(ex[s][:, :], fl[s][:, 0:W], pX[:, :], ex[s - 1][:, W - 1:W],
                                       ALU.mult, ALU.add).then_inc(sem("spread_out"), 1)

            def step(it, c, first, last):
                s = c % U
                n = count(kind, it, c)
                new = fl[s][:, W:2 * W]
                dve.wait_ge(sem("spread_out"), n)
                dve.wait_ge(sem("logits_turned"), n)
                dve.tensor_tensor(sr[:, :], pS[:, :], ex[s][:, :], ALU.mult if tc else ALU.add) \
                    .then_inc(sem("combined"), 1)
                if not last:
                    spread_targets(it, c + 1)
                if gat:
                    dve.wait_ge(sem("combined"), n)
                    dve.scalar_tensor_tensor(sl[:, :], sr[:, :], 0.2, sr[:, :], ALU.mult, ALU.max) \
                        .then_inc(sem("logits"), 1)
                if not first:
                    weigh(it, c - 1)
                if gat:
                    mlp_step_dve(dve, kind, it, c, 0)
                if gat:
                    need(dve, "turned_back", n - U)
                dve.tensor_copy(M[s][:, 0:1], M[s - 1][:, W:W + 1]).then_inc(sem("max_carried"), 1)
                if tc:
                    dve.wait_ge(sem("scored"), n - base("tc1"))
                elif gat:
                    dve.wait_ge(sem("logits"), n)
                else:
                    dve.wait_ge(sem("combined"), n)
                dve.tensor_tensor_scan(M[s][:, 1:W + 1], new, logit[:, :], M[s - 1][:, W:W + 1],
                                       ALU.add, ALU.max).then_inc(sem("maxima"), 1)
                if not first:
                    sum_denominators(it, c - 1)
                dve.wait_ge(sem("max_carried"), n)
                dve.wait_ge(sem("maxima"), n)
                need(dve, "exponentiated", n - 1)
                dve.tensor_tensor(arg[:, W:2 * W], logit[:, :], M[s][:, 1:W + 1], ALU.subtract) \
                    .then_inc(sem("arguments"), 1)
                dve.tensor_tensor(arg[:, 0:W], M[s][:, 0:W], new, ALU.add).then_inc(sem("shifted"), 1)
                if gat:
                    mlp_step_dve(dve, kind, it, c, 1)
                if not first:
                    sum_numerators(it, c - 1)
                dve.wait_ge(sem("shifted"), n)
                dve.tensor_tensor(arg[:, 0:W], arg[:, 0:W], M[s][:, 1:W + 1], ALU.subtract) \
                    .then_inc(sem("decays"), 1)
                if gat:
                    mlp_step_dve(dve, kind, it, c, 2)

            def weigh(it, c):
                s = c % U
                n = count(kind, it, c)
                dve.wait_ge(sem("exponentiated"), n)
                dve.wait_ge(sem("values_turned"), n)
                need(dve, "numerated", n - 1)
                values = pV[c % (2 if gat else U)]
                dve.tensor_tensor(pv[:, :], ap[:, W:2 * W], values[:, :], ALU.mult) \
                    .then_inc(sem("weighed"), 1)

            def sum_denominators(it, c):
                s = c % U
                n = count(kind, it, c)
                need(dve, "turned_back", n - U)
                need(dve, "denominated", n - 1)
                dve.tensor_tensor_scan(den[s][:, :], ap[:, 0:W], ap[:, W:2 * W], den[s - 1][:, W - 1:W],
                                       ALU.mult, ALU.add).then_inc(sem("denominated"), 1)

            def sum_numerators(it, c):
                s = c % U
                dve.wait_ge(sem("weighed"), count(kind, it, c))
                dve.tensor_tensor_scan(num[s][:, :], ap[:, 0:W], pv[:, :], num[s - 1][:, W - 1:W],
                                       ALU.mult, ALU.add).then_inc(sem("numerated"), 1)

            spread_targets(0, 0)
            walk(dve, step, head(kind))
            if gat:
                mlp_scale(dve, kind, 0, G - U - 2)
            for part in (weigh, sum_denominators, sum_numerators):
                part(0, G - 1)
            merge_states(dve, kind, False)
            if gat:
                mlp_tail_dve(dve, kind)

        def pass_act(act, kind):
            gc, gat = kind.startswith("gc"), kind.startswith("gat")
            w = 64 if gc else 128
            to = (ends3 if gc else ends).rearrange("(c g j p) f -> c g p j f", c=2, g=G, j=J)

            def exponentiate(it, c):
                s = c % U
                n = count(kind, it, c)
                act.wait_ge(sem("arguments"), n)
                act.wait_ge(sem("decays"), n)
                need(act, "denominated", n - 1)
                need(act, "numerated", n - 1)
                act.activation(ap[:, :], arg[:, :], ACT.Exp).then_inc(sem("exponentiated"), 1)

            def evacuate(it, c):
                s = c % U
                n = count(kind, it, c)
                act.wait_ge(sem("gc_back" if gc else "turned_back"), n)
                need(act, f"stored{s}", 32 * uses(kind, it, c))
                o = sem("gc_evacuated" if gc else "evacuated")
                for k, bank in enumerate([pN] if gc else [pN, pD]):
                    kept = act.activation(O[s][:, :, :, 64 * k:64 * k + 64],
                                          bank[:, :].rearrange("p (j c f) -> p c j f", j=J, c=2), ACT.Copy)
                kept.then_inc(o, 1)
                act.wait_ge(o, n)
                for h in range(2):
                    act.dma_start(to[h, ds(B * it + c, 1)].rearrange("a p j f -> p (a j) f"), O[s][:, h, :, 0:w]) \
                        .then_inc(sem(f"stored{s}"), 16)

            def step(it, c, first, last):
                s = c % U
                if gc:
                    evacuate(it, c)
                    return
                exponentiate(it, c)
                if not first:
                    evacuate(it, c - 1)
                if gat:
                    mlp_step_act(act, kind, it, c)

            walk(act, step, head(kind))
            if not gc:
                evacuate(0, G - 1)
                act.wait_ge(sem("merge_arg"), order(kind) + 1)
                act.activation(mw[:, 2:4], mw[:, 2:4], ACT.Exp).then_inc(sem("merge_exp"), 1)
            if gat:
                mlp_tail_act(act, kind)

        def merge_sp(sp, kind):
            gc = kind.startswith("gc")
            sp.wait_ge(sem("last"), order(kind) + 1)
            sp.dma_start(mgb[:, :], mg[64:128, :]).then_inc(sem("moved"), 16)
            sp.wait_ge(sem("merged"), order(kind) + 1)
            for s in range(U):
                sp.wait_ge(sem(f"stored{s}"), 32 * (G // U) * (order(kind) + 1))
            if gc:
                sp.dma_start(ends3[S - 1, :].rearrange("(f a) -> f a", a=1), mw[:, 4:5]) \
                    .then_inc(sem("row_merged"), 16)
            else:
                for h in range(2):
                    sp.dma_start(ends[S - 1, 64 * h:64 * h + 64].rearrange("(f a) -> f a", a=1),
                                 mw[:, 4 + h:5 + h]).then_inc(sem("row_merged"), 16)

        SOFT = KINDS[:5]
        NORMS = ["gat2", "tc2", "pt", "gc2"]
        node_in = {"gat1": (X, xT), "gat2": (H, xT), "tc1": (X, xT), "tc2": (H, h1T), "pt": (X, xT)}

        def after(kind):
            return KINDS[order(kind) + 1] if kind != "gc2" else "out"

        def part_count(kind, q):
            return P * order(kind) + q + 1

        def tiles(q):
            return slice(PARTS[q][0], PARTS[q][0] + PARTS[q][1])

        def take_pool(pool, kind):
            gc = kind.startswith("gc")
            pool.wait_ge(sem("row_merged"), 16 * rows_merged(kind))
            for q in range(P):
                for t in range(NT)[tiles(q)]:
                    pool.indirect_dma_start(out=R3[:, t, :] if gc else R[:, t, :], out_offset=None,
                                            in_=(ends3 if gc else ends)[:, :],
                                            in_offset=on_axis0(idx_end[:, t:t + 1])) \
                        .then_inc(sem(f"taken{q}"), 16)

        def scatter_pool(pool, kind):
            for t in range(NT):
                pool.wait_ge(sem("tabled"), NT * order(kind) + t + 1)
                pool.indirect_dma_start(out=spread[:, :], out_offset=on_axis0(idx_first[:, t:t + 1]),
                                        in_=TT[0:NP, t, 128:192], in_offset=None,
                                        bounds_check=EP - 1, oob_is_err=False) \
                    .then_inc(sem(f"{kind}_spread"), 16)
            pool.wait_ge(sem("targets_written"), 16 * P * (order(kind) + 1))
            pool.indirect_dma_start(out=cross_row[:, :], out_offset=None, in_=targets[:, :],
                                    in_offset=on_axis0(idx_cross[:, 0:1])).then_inc(sem("cross_taken"), 16)

        def scatter_crossing(pool, kind):
            pool.wait_ge(sem("cross_taken"), 16 * (order(kind) + 1))
            pool.indirect_dma_start(out=spread[:, :], out_offset=on_axis0(idx_cross[:, 2:3]),
                                    in_=cross_row[:, :], in_offset=None,
                                    bounds_check=EP - 1, oob_is_err=False).then_inc(sem(f"{kind}_spread"), 16)

        def write_table(sp, kind, q):
            if kind in SOFT:
                sp.wait_ge(sem("tabled"), NT * order(kind) + tiles(q).stop)
                sp.dma_start(table.rearrange("(p t) c -> p t c", t=NT)[:, tiles(q), :], TT[0:NP, tiles(q), 0:128]) \
                    .then_inc(sem("tables_written"), 16)
                sp.dma_start(targets.rearrange("(p t) c -> p t c", t=NT)[:, tiles(q), :],
                             TT[0:NP, tiles(q), 128:192]).then_inc(sem("targets_written"), 16)
            else:
                sp.wait_ge(sem(f"{kind}_features"), q + 1)
                sp.dma_start(table3.rearrange("(p t) c -> p t c", t=NT)[:, tiles(q), :], SK[:, tiles(q), :]) \
                    .then_inc(sem("tables_written"), 16)

        def turns(q):
            t0, n = PARTS[q]
            return [(t, min(4, t0 + n - t)) for t in range(t0, t0 + n, 4)]

        def turns_before(kind, q, tag):
            done = 0
            for k in KINDS:
                for r in range(P):
                    if k == "pt":
                        if (kind, q, tag) == ("tc2", r, "h2"):
                            return done
                        done += len(turns(r))
                    if k in SOFT:
                        if (kind, q, tag) == (k, r, "x"):
                            return done
                        done += len(turns(r))

        def turn_nodes_pe(pe, kind, q, x, tag):
            b = turns_before(kind, q, tag)
            for k, (t0, m) in enumerate(turns(q)):
                need(pe, "nodes_kept", b + k - 1)
                for i in range(m):
                    last = pe.transpose(ps[7 * ((b + k) % 2)][0:64, NP * i:NP * i + NP], x[:, t0 + i, :],
                                        ident[0:NP, 0:NP])
                last.then_inc(sem("nodes_turned"), 1)

        def turn_nodes_act(act, kind, q, to, tag):
            b = turns_before(kind, q, tag)
            for k, (t0, m) in enumerate(turns(q)):
                act.wait_ge(sem("nodes_turned"), b + k + 1)
                act.activation(to[0:64, t0:t0 + m, :],
                               ps[7 * ((b + k) % 2)][0:64, 0:NP * m].rearrange("p (t n) -> p t n", n=NP), ACT.Copy) \
                    .then_inc(sem("nodes_kept"), 1)

        def tables_pe(pe, kind, q):
            x, to = node_in[kind]
            pe.wait_ge(sem(f"{kind}_features"), q + 1)
            turn_nodes_pe(pe, kind, q, x, "x")
            pe.wait_ge(sem("nodes_kept"), turns_before(kind, q, "x") + len(turns(q)))
            w = wc[kind]
            for t in range(NT)[tiles(q)]:
                need(pe, "tabled", NT * order(kind) + t - 1)
                pe.matmul(ps[5 + t % 2][0:NP, 0:w.shape[1]], to[:, t, :], w[:, :], start=True, stop=True) \
                    .then_inc(sem("multiplied"), 1)

        def tables_act(act, kind, q):
            turn_nodes_act(act, kind, q, node_in[kind][1], "x")
            w = wc[kind].shape[1]
            for t in range(NT)[tiles(q)]:
                act.wait_ge(sem("multiplied"), NT * order(kind) + t + 1)
                out = ps[5 + t % 2][0:NP, :]
                act.activation(TT[0:NP, t, 0:128].rearrange("p (f h) -> p h f", h=2),
                               out[:, 0:128].rearrange("p (h f) -> p h f", h=2), ACT.Copy)
                act.activation(TT[0:NP, t, 128:w], out[:, 128:w], ACT.Copy).then_inc(sem("tabled"), 1)

        def layer_norm(c, dve, kind, q, x):
            r = tiles(q)
            m, d, sq = st1[0][:, r], st1[1][:, r], tmp[0][:, r, :]
            c(dve.tensor_reduce(m, x, AX, ALU.add))
            c(dve.tensor_scalar(m, m, -1.0 / D, None, ALU.mult))
            c(dve.tensor_tensor(x, x, bc(m), ALU.add))
            c(dve.tensor_tensor(sq, x, x, ALU.mult))
            c(dve.tensor_reduce(m, sq, AX, ALU.add))
            c(dve.tensor_scalar(m, m, 1.0 / D, EPS, ALU.mult, ALU.add))
            dve.sem_inc(sem("variances"), 1)
            dve.wait_ge(sem("deviations"), P * NORMS.index(kind) + q + 1)
            c(dve.reciprocal(d, d))
            c(dve.tensor_tensor(x, x, bc(d), ALU.mult))

        def sqrt_act(act, kind, q, tag):
            if tag == "std":
                act.wait_ge(sem("variances"), P * NORMS.index(kind) + q + 1)
            else:
                act.wait_ge(sem("squared_norms"), q + 1)
            act.activation(st1[1][:, tiles(q)], st1[0][:, tiles(q)], ACT.Sqrt) \
                .then_inc(sem("deviations" if tag == "std" else "norms"), 1)

        def divide(c, dve, q, out):
            r = tiles(q)
            c(dve.reciprocal(out, R[:, r, 64:128]))
            c(dve.tensor_tensor(out, out, R[:, r, 0:64], ALU.mult))
            c(dve.tensor_tensor(out, out, bc(has[:, r]), ALU.mult))

        def add_self_loops(c, dve, kind, q):
            r = tiles(q)
            pairs = lambda t: t.rearrange("p t (i k) -> p t i k", k=2)
            packed = pairs(R[:, r, 64:128])
            own = pairs(TT[0:NP, r, 0:128])
            logit, value = own[:, :, :, 0], own[:, :, :, 1]
            s0, top, sk, h = tmp[0][:, r, :], tmp[1][:, r, :], SK[:, r, :], H[:, r, :]
            c(dve.tensor_tensor(s0, logit, TT[0:NP, r, 128:192], ALU.add))
            c(dve.scalar_tensor_tensor(flat(s0), flat(s0), 0.2, flat(s0), ALU.mult, ALU.max))
            for k in range(2):
                c(dve.tensor_tensor(pairs(sk)[:, :, :, k], packed[:, :, :, 1],
                                    has[:, r].unsqueeze(2).to_broadcast([NP, PARTS[q][1], 32]), ALU.mult))
            c(dve.tensor_scalar(st1[0][:, r], has[:, r], -1.0, BIG, ALU.add, ALU.mult))
            c(dve.tensor_tensor(sk, sk, bc(st1[0][:, r]), ALU.add))
            c(dve.tensor_tensor(top, sk, s0, ALU.max))
            c(dve.tensor_tensor(s0, s0, top, ALU.subtract))
            c(dve.tensor_tensor(sk, sk, top, ALU.subtract))
            dve.sem_inc(sem("loop_args"), 1)
            dve.wait_ge(sem("loop_exps"), 2 * part_count(kind, q))
            for k in range(2):
                c(dve.tensor_tensor(pairs(h)[:, :, :, k], packed[:, :, :, 0], pairs(sk)[:, :, :, k], ALU.mult))
            c(dve.scalar_tensor_tensor(flat(h), flat(h), 1e-16, flat(s0), ALU.add, ALU.add))
            c(dve.reciprocal(h, h))
            c(dve.tensor_tensor(sk, sk, R[:, r, 0:64], ALU.mult))
            c(dve.tensor_tensor(s0, s0, value, ALU.mult))
            c(dve.tensor_tensor(sk, sk, s0, ALU.add))
            c(dve.tensor_tensor(h, h, sk, ALU.mult))

        def post_dve(dve, kind, q):
            c = dve_chain(dve)
            r = tiles(q)
            x, h, sk, t0, t1 = X[:, r, :], H[:, r, :], SK[:, r, :], tmp[0][:, r, :], tmp[1][:, r, :]
            dve.wait_ge(sem(f"taken{q}"), 16 * PARTS[q][1] * (order(kind) + 1))
            if kind == "gat1":
                add_self_loops(c, dve, kind, q)
                c(dve.tensor_tensor(h, h, bias[:, 0:1, :].to_broadcast([NP, PARTS[q][1], 64]), ALU.add))
                c(dve.tensor_scalar(t0, h, 0.0, None, ALU.min))
                dve.sem_inc(sem("elu_arg"), 1)
                dve.wait_ge(sem("elu_exp"), q + 1)
                c(dve.tensor_scalar(t1, t1, -1.0, None, ALU.add))
                c(dve.scalar_tensor_tensor(flat(h), flat(h), 0.0, flat(t1), ALU.max, ALU.add))
            elif kind == "gat2":
                add_self_loops(c, dve, kind, q)
                c(dve.tensor_tensor(h, h, bias[:, 1:2, :].to_broadcast([NP, PARTS[q][1], 64]), ALU.add))
                c(dve.tensor_tensor(t0, h, h, ALU.mult))
                c(dve.tensor_reduce(st1[0][:, r], t0, AX, ALU.add))
                dve.sem_inc(sem("squared_norms"), 1)
                dve.wait_ge(sem("norms"), q + 1)
                c(dve.tensor_scalar(st1[1][:, r], st1[1][:, r], 1e-12, None, ALU.max))
                c(dve.reciprocal(st1[1][:, r], st1[1][:, r]))
                c(dve.tensor_tensor(h, h, bc(st1[1][:, r]), ALU.mult))
                c(dve.tensor_tensor(x, x, h, ALU.add))
                layer_norm(c, dve, kind, q, x)
            elif kind in ("tc1", "tc2"):
                divide(c, dve, q, h)
                c(dve.tensor_tensor(h, h, TT[0:NP, r, 192:256], ALU.add))
                c(dve.tensor_scalar(h, h, 0.0, None, ALU.max))
                if kind == "tc2":
                    dve.sem_inc(sem("h2_ready"), 1)
                    for t in range(NT)[r]:
                        dve.wait_ge(sem("skipped"), t + 1)
                        dve.scalar_tensor_tensor(X[:, t, :], ps[5 + t % 2][0:NP, 0:64], 0.0, X[:, t, :],
                                                 ALU.max, ALU.add).then_inc(sem("skip_added"), 1)
                    dve.wait_ge(sem("skip_added"), r.stop)
                    layer_norm(c, dve, kind, q, x)
            elif kind == "pt":
                divide(c, dve, q, h)
                c(dve.tensor_tensor(x, x, h, ALU.add))
                layer_norm(c, dve, kind, q, x)
                c(dve.tensor_tensor(sk, x, bc(dinv[:, r]), ALU.mult))
            else:
                c(dve.tensor_tensor(h if kind == "gc1" else t1, R3[:, r, :], bc(dinv[:, r]), ALU.mult))
                if kind == "gc1":
                    c(dve.tensor_tensor(sk, h, bc(dinv[:, r]), ALU.mult))
                else:
                    c(dve.tensor_tensor(h, h, x, ALU.add))
                    c(dve.tensor_tensor(h, h, t1, ALU.add))
                    c(dve.scalar_tensor_tensor(flat(x), flat(h), 1.0 / 3.0, flat(x), ALU.mult, ALU.add))
                    layer_norm(c, dve, kind, q, x)
            dve.sem_inc(sem(f"{after(kind)}_features"), 1)

        def post_act(act, kind, q):
            r = tiles(q)
            if kind.startswith("gat"):
                act.wait_ge(sem("loop_args"), part_count(kind, q))
                for t in (tmp[0], SK):
                    act.activation(t[:, r, :], t[:, r, :], ACT.Exp).then_inc(sem("loop_exps"), 1)
            if kind == "gat1":
                act.wait_ge(sem("elu_arg"), q + 1)
                act.activation(tmp[1][:, r, :], tmp[0][:, r, :], ACT.Exp).then_inc(sem("elu_exp"), 1)
            if kind == "gat2":
                sqrt_act(act, kind, q, "norm")
            if kind == "tc2":
                turn_nodes_act(act, kind, q, xT, "h2")
            if kind in ("gat2", "tc2", "pt", "gc2"):
                sqrt_act(act, kind, q, "std")

        def post_pe(pe, kind, q):
            if kind != "tc2":
                return
            pe.wait_ge(sem("h2_ready"), q + 1)
            turn_nodes_pe(pe, kind, q, H, "h2")
            pe.wait_ge(sem("nodes_kept"), turns_before(kind, q, "h2") + len(turns(q)))
            for t in range(NT)[tiles(q)]:
                if t >= 2:
                    pe.wait_ge(sem("skip_added"), t - 1)
                if t == tiles(q).start and q > 0:
                    pe.wait_ge(sem("tabled"), NT * order("pt") + t)
                out = ps[5 + t % 2][0:NP, 0:64]
                pe.matmul(out, h1T[0:64, t, :], skw[0:64, 0, :], start=True, stop=False)
                pe.matmul(out, xT[:, t, :], skw[:, 1, :], start=False, stop=True).then_inc(sem("skipped"), 1)

        DI = TT[:, :, :].rearrange("p t c -> p (t c)").bitcast(i32)
        cur, prv = DI[0:G, 0:2 * W], DI[0:G, 2 * W:4 * W]
        heads_i = DI[0:NP, 4 * W:4 * W + TILES]
        heads = SK[:, :, :].rearrange("p t c -> p (t c)")[:, 0:TILES]
        less = R[:, :, :].rearrange("p t c -> p (t c)")
        rows_i = R[:, :, :].bitcast(i32)
        fbuf = O[0][0:G, :, :, :].rearrange("p c j f -> p (c j f)").bitcast(bf16)

        def load_inputs(act):
            n = [0]

            def load(dst, src, name="setup_loaded"):
                n[0] += 16
                act.dma_start(dst, src).then_inc(sem(name), 16)

            act.wait_ge(sem("cleared"), 1)
            d = a["dst_s"]
            for c in range(2):
                load(cur[:, W * c:W * c + W], d[c, 1:S + 1].rearrange("(g w) -> g w", w=W))
                load(prv[:, W * c:W * c + W], d[c, 0:S].rearrange("(g w) -> g w", w=W))
            load(midd[:, :], a["mid"].unsqueeze(0).to_broadcast([64, 2]))
            load(X[:, :, :], a["x"].rearrange("(p t) c -> p t c", t=NT))
            load(wT[:, 0, :], a["w1t"][:, :])
            load(wT[:, 1, :], a["w2t"][:, :])
            col = lambda v: v.rearrange("(f a) -> f a", a=1)
            row = lambda v: v.rearrange("(a f) -> a f", a=1)
            for k, v in enumerate(["L0_gnn_a_src1", "L0_gnn_a_dst1", "L0_gnn_a_src2", "L0_gnn_a_dst2"]):
                load(avec[:, k:k + 1], col(a[v].rearrange("h c -> (h c)")))
            for k in (1, 2):
                w = wc[f"tc{k}"]
                for i, q in enumerate("kvqs"):
                    load(w[0:64, 64 * i:64 * i + 64], a[f"L1_gnn_{q}{k}_w"][:, :])
                    load(w[64:65, 64 * i:64 * i + 64], row(a[f"L1_gnn_{q}{k}_b"]))
                for c in range(2):
                    load(we[k - 1][DE * c:DE * c + DE, 64 * c:64 * c + 64], a[f"L1_gnn_e{k}_w"][:, :])
                load(bias[:, k - 1, :], a[f"L0_gnn_b{k}"].unsqueeze(0).to_broadcast([NP, 64]))
            load(skw[0:64, 0, :], a["L1_gnn_skip_w"][0:64, :])
            load(skw[0:64, 1, :], a["L1_gnn_skip_w"][64:128, :])
            load(skw[64:65, 1, :], row(a["L1_gnn_skip_b"]))
            for i, q in enumerate(["W2", "W3", "W1"]):
                load(wc["pt"][0:64, 64 * i:64 * i + 64], a[f"L2_gnn_{q}"][:, :])
            for c in range(2):
                load(wd1[3 * c:3 * c + 3, 64 * c:64 * c + 64], a["L2_gnn_Wd1"][:, :])
                load(wd1[6:7, 64 * c:64 * c + 64], row(a["L2_gnn_bd1"]))
                load(wd2[64 * c:64 * c + 64, 64 * c:64 * c + 64], a["L2_gnn_Wd2"][:, :])
                for i, q in enumerate(["g1", "b1", None, "g2", "b2"]):
                    if q:
                        load(pv4[64 * c:64 * c + 64, i:i + 1], col(a[f"L2_gnn_{q}"]))
                load(bd2row[:, 64 * c:64 * c + 64], row(a["L2_gnn_bd2"]))
            assert n[0] == 16 * LOADS, n[0] // 16
        def setup_sp(sp):
            sp.dma_start(heads_i, a["heads"].unsqueeze(0).to_broadcast([NP, TILES])).then_inc(sem("search_loaded"), 16)
            sp.dma_start(cst[:, :], a["consts"][:, :]).then_inc(sem("search_loaded"), 16)
            sp.wait_ge(sem("zeros"), 1)
            sv = spread.rearrange("e f -> (e f)").rearrange("(p k z) -> p k z", p=128, z=2 * W)
            for k in range(EP * 64 // 128 // (2 * W)):
                sp.dma_start(sv[:, k, :], arg[:, :]).then_inc(sem("spread_zero"), 16)
            sp.wait_ge(sem("flags_made"), 1)
            for c in range(2):
                sp.dma_start(flags[:, c, :], fbuf[:, 2 * W * c:2 * W * c + 2 * W]).then_inc(sem("flags_out"), 16)
            sp.wait_ge(sem("starts_made"), 1)
            sp.dma_start(starts_d[0:N].rearrange("(p t) -> p t", t=NT), starts[:, :]).then_inc(sem("starts_out"), 16)
            sp.dma_start(starts_d[N:N + 1].unsqueeze(0), ecol[:, :]).then_inc(sem("starts_out"), 16)
            sp.wait_ge(sem("starts_out"), 32)
            sp.dma_start(endsn[:, :], starts_d[1:N + 1].rearrange("(p t) -> p t", t=NT)).then_inc(sem("ends_in"), 16)
            sp.wait_ge(sem("flags_out"), 32)
            sp.wait_ge(sem("spread_zero"), 16 * (EP * 64 // 128 // (2 * W)))

        LOADS = 4 + 1 + 2 + 1 + 4 + 2 * (8 + 2 + 1) + 3 + 3 + 2 * (1 + 1 + 1 + 4 + 1)
        bd2row = sb("bd2row", [1, 128])
        ecol = sb("ecol", [1, 1])

        def setup_pool(pool):
            pool.wait_ge(sem("tile_index"), 1)
            for t in range(NT):
                pool.indirect_dma_start(out=rows_i[:, t, :], out_offset=None, in_=a["dst_rows"][:, :],
                                        in_offset=on_axis0(idx_t[:, t:t + 1])).then_inc(sem("rows_in"), 16)
            pool.wait_ge(sem("ends_in"), 16)
            pool.indirect_dma_start(out=cross_end[:, :], out_offset=None, in_=starts_d.unsqueeze(1),
                                    in_offset=on_axis0(idx_cross[:, 1:2])).then_inc(sem("cross_end"), 16)

        def setup_pe(pe):
            pe.wait_ge(sem("amat_made"), 1)
            for k in range(2):
                pe.matmul(ps[6][0:64, 192 * k:192 * k + 192], wT[:, k, :], amat[:, k, :], start=True, stop=True) \
                    .then_inc(sem("gat_weights"), 1)
            pe.matmul(ps[7][:, 0:1], bd2row[:, :], cst[0:1, CI:CI + 1], start=True, stop=True) \
                .then_inc(sem("bd2_turned"), 1)

        def setup_dve(dve):
            c = dve_chain(dve)
            c(dve.memset(arg[:, :], 0.0))
            dve.sem_inc(sem("zeros"), 1)
            for t in (xT, h1T):
                dve.memset(t[64:65, :, :], 1.0)
            for x in mx:
                dve.memset(x, 1.0)
            dve.memset(pV[2][:, :], 0.0)
            dve.memset(pv4[:, 5:6], 0.0)
            for t in (we[0], we[1], wd1, wd2):
                dve.memset(t[:, :], 0.0)
            for w in (wc["gat1"], wc["gat2"], wc["pt"]):
                dve.memset(w[64:65, :], 0.0)
            dve.memset(ecol[:, :], float(E))
            for s in (ex[U - 1], num[U - 1], den[U - 1], M[U - 1]):
                dve.memset(s[:, :], 0.0)
            dve.memset(mg[:, :], 0.0)
            c(dve.memset(epsc[:, :], EPS))
            dve.sem_inc(sem("cleared"), 1)
            dve.wait_ge(sem("search_loaded"), 32)
            c(dve.tensor_copy(heads, heads_i))
            for t in range(NT):
                c(dve.tensor_scalar(less[:, 0:TILES], heads, nid[:, t:t + 1], None, ALU.is_lt))
                c(dve.tensor_reduce(st1[0][:, t:t + 1], less[:, 0:TILES], AX, ALU.add))
            c(dve.tensor_scalar(st1[0][:, :], st1[0][:, :], -1.0, 0.0, ALU.add, ALU.max))
            c(dve.tensor_copy(idx_t[:, :], st1[0][:, :]))
            dve.sem_inc(sem("tile_index"), 1)
            dve.wait_ge(sem("setup_loaded"), 16 * LOADS)
            c(dve.tensor_copy(picks.rearrange("p (r f) -> p r f", f=64),
                              ident[0:U * K, 0:U * K].unsqueeze(2).to_broadcast([U * K, U * K, 64])))
            for k in range(2):
                c(dve.tensor_copy(amat[:, k, 64:128], ident[0:64, 0:64]))
                for i in range(2):
                    block = amat[:, k, 128 * i:128 * i + 64]
                    mask = bones[0:64, 0:64] if k else hmask
                    c(dve.tensor_scalar(block, mask, avec[:, 2 * k + i:2 * k + i + 1], None, ALU.mult))
            c(dve.tensor_reduce(parity[:, 0:1], even[0:64, :], AX, ALU.add))
            c(dve.tensor_reduce(parity[:, 1:2], odd[0:64, :], AX, ALU.add))
            c(dve.tensor_scalar(bones8[:, :], bones, float(D) ** -0.5, None, ALU.mult))
            for t, p in ((wd1, 7), (wd2, 128), (bd2row, 1)):
                v = t[:, :].rearrange("p (c f) -> p c f", c=2)
                c(dve.tensor_reduce(mcol[0:p, :], v, AX, ALU.add))
                c(dve.tensor_scalar(mcol[0:p, :], mcol[0:p, :], -1.0 / D, None, ALU.mult))
                c(dve.tensor_tensor(v, v, mcol[0:p, :].unsqueeze(2).to_broadcast([p, 2, 64]), ALU.add))
            c(dve.tensor_scalar(wc["pt"][0:64, 0:64], wc["pt"][0:64, 0:64], -1.0, None, ALU.mult))
            dve.sem_inc(sem("amat_made"), 1)
            for k in range(2):
                dve.wait_ge(sem("gat_weights"), 2)
                c(dve.tensor_copy(wc[f"gat{k + 1}"][0:64, :], ps[6][0:64, 192 * k:192 * k + 192]))
            dve.wait_ge(sem("bd2_turned"), 1)
            c(dve.tensor_copy(pv4[:, 2:3], ps[7][:, 0:1]))
            for k in range(2):
                f = fbuf[:, 2 * W * k:2 * W * k + 2 * W]
                c(dve.tensor_tensor(f[:, 0:W], cur[:, W * k:W * k + W], prv[:, W * k:W * k + W], ALU.is_equal))
                c(dve.tensor_scalar(f[:, W:2 * W], f[:, 0:W], -1.0, BIG, ALU.add, ALU.mult))
            dve.sem_inc(sem("flags_made"), 1)
            dve.sem_inc(sem("gat1_features"), P)
            c(dve.tensor_tensor(cross[:, :], midd[:, 0:1], midd[:, 1:2], ALU.is_equal))
            c(dve.tensor_scalar(crossb[:, :], cross[:, :], -1.0, BIG, ALU.add, ALU.mult))
            c(dve.tensor_copy(idx_cross[:, 0:1], midd[0:2, 1:2]))
            c(dve.tensor_scalar(idx_cross[:, 1:2], midd[0:2, 1:2], 1.0, None, ALU.add))
            dve.wait_ge(sem("rows_in"), 16 * NT)
            c(dve.tensor_copy(R[:, :, :], rows_i))
            c(dve.tensor_tensor(R[:, :, :], R[:, :, :], nid.unsqueeze(2).to_broadcast([NP, NT, 128]), ALU.is_lt))
            c(dve.tensor_reduce(starts[:, :], R[:, :, :], AX, ALU.add))
            c(dve.scalar_tensor_tensor(starts[:, :], st1[0][:, :], float(T), starts[:, :], ALU.mult, ALU.add))
            dve.sem_inc(sem("starts_made"), 1)
            dve.wait_ge(sem("ends_in"), 16)
            deg, t1, t2 = st1[1], st1[2], st1[3]
            c(dve.tensor_tensor(deg[:, :], endsn[:, :], starts[:, :], ALU.subtract))
            c(dve.tensor_scalar(has[:, :], deg[:, :], 0.0, None, ALU.is_gt))
            c(dve.tensor_scalar(st1[0][:, :], deg[:, :], 1.0, None, ALU.max))
            dve.sem_inc(sem("degrees"), 1)
            dve.wait_ge(sem("degree_root"), 1)
            c(dve.reciprocal(dinv[:, :], dinv[:, :]))
            c(dve.tensor_tensor(dinv[:, :], dinv[:, :], has[:, :], ALU.mult))
            c(dve.tensor_scalar(t1[:, :], endsn[:, :], -1.0, 0.0, ALU.add, ALU.max))
            c(dve.tensor_scalar(t1[:, :], t1[:, :], float(S - 1), None, ALU.min))
            c(dve.tensor_scalar(t2[:, :], starts[:, :], -1.0, float(3 * S - 1), ALU.mult, ALU.add))
            in_b = deg
            c(dve.tensor_scalar(in_b[:, :], starts[:, :], float(S), None, ALU.is_ge))
            c(dve.tensor_tensor(t2[:, :], t2[:, :], t1[:, :], ALU.subtract))
            c(dve.tensor_tensor(t2[:, :], t2[:, :], in_b[:, :], ALU.mult))
            c(dve.tensor_tensor(t1[:, :], t1[:, :], t2[:, :], ALU.add))
            c(dve.tensor_copy(idx_end[:, :], t1[:, :]))
            c(dve.tensor_scalar(in_b[:, :], starts[:, :], float(S), None, ALU.is_lt))
            c(dve.tensor_scalar(t1[:, :], endsn[:, :], -1.0, float(3 * S), ALU.mult, ALU.add))
            c(dve.tensor_tensor(t2[:, :], starts[:, :], t1[:, :], ALU.subtract))
            c(dve.tensor_tensor(t2[:, :], t2[:, :], in_b[:, :], ALU.mult))
            c(dve.tensor_tensor(t1[:, :], t1[:, :], t2[:, :], ALU.add))

            def place(out, value, keep):
                c(dve.tensor_scalar(value, value, -OOB, None, ALU.add))
                c(dve.tensor_tensor(value, value, keep, ALU.mult))
                c(dve.tensor_scalar(value, value, OOB, None, ALU.add))
                c(dve.tensor_copy(out, value))

            place(idx_first[:, :], t1[:, :], has[:, :])
            row, keep = t1[0:2, 0:1], t2[0:2, 0:1]
            dve.wait_ge(sem("cross_end"), 16)
            c(dve.tensor_scalar(row, cross_end[:, :], -1.0, float(3 * S), ALU.mult, ALU.add))
            c(dve.tensor_scalar(keep, nid[0:2, 0:1], 0.0, None, ALU.is_equal))
            c(dve.tensor_tensor(keep, keep, cross[0:2, :], ALU.mult))
            place(idx_cross[:, 2:3], row, keep)
            dve.sem_inc(sem("places_ready"), 1)

        def setup_act(act):
            load_inputs(act)
            act.wait_ge(sem("degrees"), 1)
            act.activation(dinv[:, :], st1[0][:, :], ACT.Sqrt).then_inc(sem("degree_root"), 1)

        block = ctx.enter_context(nc.Block())

        @block.sync
        def _(sp):
            setup_sp(sp)
            for q in range(P):
                write_table(sp, KINDS[0], q)
            for kind in KINDS:
                if kind == "pt":
                    for q in range(U):
                        sp.wait_ge(sem(f"mlp_stored{q}"), 16 * (G // U))
                pass_sp(sp, kind)
                merge_sp(sp, kind)
                for q in range(P):
                    if kind != "gc2":
                        write_table(sp, after(kind), q)
                    else:
                        sp.wait_ge(sem("out_features"), q + 1)
                        sp.dma_start(a["out"].rearrange("(p t) c -> p t c", t=NT)[:, tiles(q), :], X[:, tiles(q), :]) \
                            .then_inc(sem("written"), 16)
            sp.wait_ge(sem("written"), 16 * P)

        @block.gpsimd
        def _(pool):
            setup_pool(pool)
            pool.wait_ge(sem("places_ready"), 1)
            pool.wait_ge(sem("spread_zero"), 16 * (EP * 64 // 128 // (2 * W)))
            for kind in KINDS:
                if kind in SOFT:
                    scatter_pool(pool, kind)
                pass_pool(pool, kind)
                take_pool(pool, kind)

        @block.tensor
        def _(pe):
            setup_pe(pe)
            for q in range(P):
                tables_pe(pe, KINDS[0], q)
            for kind in KINDS:
                (pass_pe if kind in SOFT else sum_pe)(pe, kind)
                for q in range(P):
                    post_pe(pe, kind, q)
                    if after(kind) in SOFT:
                        tables_pe(pe, after(kind), q)

        @block.vector
        def _(dve):
            setup_dve(dve)
            for kind in KINDS:
                (pass_dve if kind in SOFT else sum_dve)(dve, kind)
                for q in range(P):
                    post_dve(dve, kind, q)

        @block.scalar
        def _(act):
            setup_act(act)
            for q in range(P):
                tables_act(act, KINDS[0], q)
            for kind in KINDS:
                pass_act(act, kind)
                for q in range(P):
                    post_act(act, kind, q)
                    if after(kind) in SOFT:
                        tables_act(act, after(kind), q)


WEIGHTS = (["L0_gnn_" + w for w in ("a_src1", "a_dst1", "b1", "a_src2", "a_dst2", "b2")]
           + [f"L1_gnn_{w}{k}_{p}" for k in (1, 2) for w in "qkvs" for p in "wb"]
           + ["L1_gnn_e1_w", "L1_gnn_e2_w", "L1_gnn_skip_w", "L1_gnn_skip_b"]
           + ["L2_gnn_" + w for w in ("Wd1", "bd1", "g1", "b1", "Wd2", "bd2", "g2", "b2", "W1", "W2", "W3")])


def lay_out(inputs):
    f = {k: np.asarray(v) for k, v in inputs.items()}

    def streams(v, pad):
        v = np.concatenate([v, np.full((EP - E,) + v.shape[1:], pad, v.dtype)])
        return np.stack([v[:S], v[S:][::-1]])

    src = streams(f["src"], 0).reshape(2, G, J, T)
    dst = np.concatenate([f["dst"], np.full(EP - E, N, f["dst"].dtype)])
    both = streams(f["dst"], N)
    arrays = {
        "x": f["x"],
        "consts": shape_constants(),
        "src_g": np.ascontiguousarray(src.transpose(1, 3, 0, 2).reshape(G, T, 2 * J)),
        "dst_s": np.ascontiguousarray(np.concatenate([np.full((2, 1), -1, both.dtype), both], 1)),
        "dst_rows": dst.reshape(TILES, T),
        "heads": np.ascontiguousarray(dst[::T]),
        "mid": np.ascontiguousarray(dst[S - 1:S + 1]),
        "w1t": np.ascontiguousarray(f["L0_gnn_W1"].T),
        "w2t": np.ascontiguousarray(f["L0_gnn_W2"].T),
    }
    for name, key, k in (("ea32", "edge_attr_32", DE), ("ea3", "edge_attr_3", 3)):
        v = streams(f[key], 0).reshape(2, G, W, k)
        arrays[name] = np.ascontiguousarray(v.transpose(1, 0, 3, 2).reshape(G, 2 * k, W))
    for w in WEIGHTS:
        arrays[w] = f[w]
    return arrays


def kernel(**inputs):
    import concourse.bacc as bacc
    from concourse.bass_utils import run_bass_kernel_spmd

    nc = bacc.Bacc("TRN2", target_bir_lowering=False, num_devices=1)
    arrays = lay_out(inputs)
    a, feeds = {}, {}
    for name, v in arrays.items():
        feeds[f"in_{name}"] = v
        a[name] = nc.dram_tensor(f"in_{name}", v.shape, mybir.dt.from_np(v.dtype), kind="ExternalInput").ap()
    a["out"] = nc.dram_tensor("out_0", (N, D), mybir.dt.float32, kind="ExternalOutput").ap()
    build(nc, a)
    r = run_bass_kernel_spmd(nc, [feeds], core_ids=[0])
    return r.results[0]["out_0"]
```
